# Optimizing a Trainium2 kernel written in Bass

```python
import numpy as np
import jax
import jax.numpy as jnp

def _softmax(x, axis=-1):
    return jax.nn.softmax(x, axis=axis)

def _gelu(x):
    return jax.nn.gelu(x, approximate=True)

def _silu(x):
    return jax.nn.silu(x)

def _sigmoid(x):
    return jax.nn.sigmoid(x)

def _layernorm(x, axis=-1, eps=1e-05):
    m = jnp.mean(x, axis=axis, keepdims=True)
    v = jnp.var(x, axis=axis, keepdims=True)
    return (x - m) / jnp.sqrt(v + eps)

def _scatter_add(tgt, idx, src, axis=0):
    return tgt.at[idx].add(src)

def _segment_sum(src, seg, n):
    return jax.ops.segment_sum(src, seg, n)
kernel_name = 'mk_flamingo_gated_d2_seqx_r8_a93770'

def setup_inputs(seed: int=0):
    np.random.seed(seed)
    _w = jnp.asarray

    def _rec_inputs():
        import jax
        import jax.numpy as jnp
        _rk = jax.random.key(seed)
        x = 0.0001212 + 1 * jax.random.normal(jax.random.fold_in(_rk, 1), (4, 256, 256), jnp.float32)
        _lenS = 256 - jax.random.randint(jax.random.fold_in(_rk, 7), (4,), 0, max(1, 256 // 4) + 1, jnp.int32)
        _lenS2 = 256 - jax.random.randint(jax.random.fold_in(_rk, 8), (4,), 0, max(1, 256 // 4) + 1, jnp.int32)
        _ctx_2048P = jax.random.normal(jax.random.fold_in(_rk, 11), (4, 16, 256), jnp.float32)
        _ctx_2048c = jax.random.dirichlet(jax.random.fold_in(_rk, 511), 0.3 * jnp.ones((16,), jnp.float32), (4, 256))
        _ctx_2048t = jnp.einsum('bsk,bkd->bsd', _ctx_2048c, _ctx_2048P)
        _ctx_2048t = _ctx_2048t * jax.lax.rsqrt(jnp.mean(jnp.square(_ctx_2048t)) + 1e-12) * 0.953939
        ctx_2048 = 0.000173663 + 1.0001 * (_ctx_2048t + 0.3 * jax.random.normal(jax.random.fold_in(_rk, 611), (4, 256, 256), jnp.float32))
        _g = jax.random.normal(jax.random.fold_in(_rk, 9001), (2, 2), jnp.float32)
        _g = jnp.sign(_g) * jnp.maximum(jnp.abs(_g), 1.0) + (_g == 0) * 1.0
        g_xattn = _g[0]
        g_ffn = _g[1]
        return (x, ctx_2048, g_xattn, g_ffn)
    x, ctx_2048, g_xattn, g_ffn = _rec_inputs()

    def _L0_xattn_setup():
        import jax, jax.numpy as jnp
        import numpy as np
        B_DIM, T_DIM, C_DIM = (16, 128, 256)

        def _wkv(w, u, k, v):
            Bn, Tn, Cn = k.shape
            NEG_INF = jnp.float32(-1e+38)

            def step(carry, kv_t):
                p, q, o = carry
                kt, vt = kv_t
                no = jnp.maximum(o, u + kt)
                A = jnp.exp(o - no)
                E = jnp.exp(u + kt - no)
                y = (A * p + E * vt) / (A * q + E)
                no2 = jnp.maximum(w + o, kt)
                A2 = jnp.exp(w + o - no2)
                E2 = jnp.exp(kt - no2)
                return ((A2 * p + E2 * vt, A2 * q + E2, no2), y)
            init = (jnp.zeros((Bn, Cn), k.dtype), jnp.zeros((Bn, Cn), k.dtype), jnp.full((Bn, Cn), NEG_INF, k.dtype))
            kT = jnp.moveaxis(k, 1, 0)
            vT = jnp.moveaxis(v, 1, 0)
            _, yT = jax.lax.scan(step, init, (kT, vT))
            return jnp.moveaxis(yT, 0, 1)
        key = jax.random.key(seed)
        k1, k2, k3, k4 = jax.random.split(key, 4)
        w = -jnp.exp(jax.random.normal(k1, (C_DIM,), jnp.float32))
        u = jax.random.normal(k2, (C_DIM,), jnp.float32)
        k = jax.random.normal(k3, (B_DIM, T_DIM, C_DIM), jnp.float32)
        v = jax.random.normal(k4, (B_DIM, T_DIM, C_DIM), jnp.float32)
        return {'B': B_DIM, 'T': T_DIM, 'C': C_DIM, 'w': w, 'u': u, 'k': k, 'v': v}
    _L0_xattn_all = _L0_xattn_setup()
    _L0_xattn_in = {k: v for k, v in _L0_xattn_all.items() if k in ('w', 'u')}
    del _L0_xattn_all

    def _L0_ffn_setup():
        import jax, jax.numpy as jnp
        import numpy as np
        EPS = 1e-05

        def _quant_weight(w):
            scale = jnp.mean(jnp.abs(w)) + EPS
            wq = jnp.clip(jnp.round(w / scale), -1.0, 1.0)
            return (wq, scale)

        def _quant_act(x):
            s = jnp.max(jnp.abs(x), axis=-1, keepdims=True) / 127.0 + EPS
            xq = jnp.clip(jnp.round(x / s), -128.0, 127.0)
            return (xq, s)

        def _qlinear(x, w):
            wq, ws = _quant_weight(w)
            xq, xs = _quant_act(x)
            y = jnp.einsum('bsi,oi->bso', xq, wq)
            return y * xs * ws
        key = jax.random.key(seed)
        k1, k2, k3, k4 = jax.random.split(key, 4)
        H, I = (256, 1024)
        x = jax.random.normal(k1, (4, 512, H), dtype=jnp.float32)
        w_gate = jax.random.normal(k2, (I, H), dtype=jnp.float32) * (1.0 / np.sqrt(H))
        w_up = jax.random.normal(k3, (I, H), dtype=jnp.float32) * (1.0 / np.sqrt(H))
        w_down = jax.random.normal(k4, (H, I), dtype=jnp.float32) * (1.0 / np.sqrt(I))
        return {'x': x, 'w_gate': w_gate, 'w_up': w_up, 'w_down': w_down}
    _L0_ffn_all = _L0_ffn_setup()
    _L0_ffn_in = {k: v for k, v in _L0_ffn_all.items() if k in ('w_gate', 'w_up', 'w_down')}
    del _L0_ffn_all

    def _L1_xattn_setup():
        import jax, jax.numpy as jnp
        import numpy as np
        DIM = 256
        NHEADS = 32
        HEAD_DIM = DIM // NHEADS
        EPS = 1e-06

        def _rmsnorm(t):
            return t * jax.lax.rsqrt(jnp.mean(t * t, axis=-1, keepdims=True) + EPS)
        key = jax.random.key(seed)
        kx, kc, kq, kk, kv = jax.random.split(key, 5)
        x = jax.random.normal(kx, (2, 512, DIM), dtype=jnp.float32)
        context = jax.random.normal(kc, (2, 64, DIM), dtype=jnp.float32)
        std = 0.02
        Wq = jax.random.normal(kq, (DIM, DIM), dtype=jnp.float32) * std
        Wk = jax.random.normal(kk, (DIM, DIM), dtype=jnp.float32) * std
        Wv = jax.random.normal(kv, (DIM, DIM), dtype=jnp.float32) * std
        return {'x': x, 'context': context, 'Wq': Wq, 'Wk': Wk, 'Wv': Wv}
    _L1_xattn_all = _L1_xattn_setup()
    _L1_xattn_in = {k: v for k, v in _L1_xattn_all.items() if k in ('Wq', 'Wk', 'Wv')}
    del _L1_xattn_all

    def _L1_ffn_setup():
        import jax, jax.numpy as jnp
        import numpy as np
        H = 256
        E = 64
        I = 64
        SI = 64
        TOP_K = 8
        B, T = (2, 64)
        key = jax.random.key(seed)
        ks = jax.random.split(key, 8)
        s = 0.02
        return {'h': jax.random.normal(ks[0], (B, T, H), jnp.float32), 'gate_w': jax.random.normal(ks[1], (E, H), jnp.float32) * s, 'gu_w': jax.random.normal(ks[2], (E, 2 * I, H), jnp.float32) * s, 'dp_w': jax.random.normal(ks[3], (E, H, I), jnp.float32) * s, 'sh_gate_w': jax.random.normal(ks[4], (SI, H), jnp.float32) * s, 'sh_up_w': jax.random.normal(ks[5], (SI, H), jnp.float32) * s, 'sh_down_w': jax.random.normal(ks[6], (H, SI), jnp.float32) * s, 'sh_gate1_w': jax.random.normal(ks[7], (1, H), jnp.float32) * s}
    _L1_ffn_all = _L1_ffn_setup()
    _L1_ffn_in = {k: v for k, v in _L1_ffn_all.items() if k in ('gate_w', 'gu_w', 'dp_w', 'sh_gate_w', 'sh_up_w', 'sh_down_w', 'sh_gate1_w')}
    del _L1_ffn_all
    return {'x': x, 'ctx_2048': ctx_2048, 'g_xattn': g_xattn, 'g_ffn': g_ffn, 'L0_xattn_w': _L0_xattn_in['w'], 'L0_xattn_u': _L0_xattn_in['u'], 'L0_ffn_w_gate': _L0_ffn_in['w_gate'], 'L0_ffn_w_up': _L0_ffn_in['w_up'], 'L0_ffn_w_down': _L0_ffn_in['w_down'], 'L1_xattn_Wq': _L1_xattn_in['Wq'], 'L1_xattn_Wk': _L1_xattn_in['Wk'], 'L1_xattn_Wv': _L1_xattn_in['Wv'], 'L1_ffn_gate_w': _L1_ffn_in['gate_w'], 'L1_ffn_gu_w': _L1_ffn_in['gu_w'], 'L1_ffn_dp_w': _L1_ffn_in['dp_w'], 'L1_ffn_sh_gate_w': _L1_ffn_in['sh_gate_w'], 'L1_ffn_sh_up_w': _L1_ffn_in['sh_up_w'], 'L1_ffn_sh_down_w': _L1_ffn_in['sh_down_w'], 'L1_ffn_sh_gate1_w': _L1_ffn_in['sh_gate1_w']}

def reference(x, ctx_2048, g_xattn, g_ffn, L0_xattn_w, L0_xattn_u, L0_ffn_w_gate, L0_ffn_w_up, L0_ffn_w_down, L1_xattn_Wq, L1_xattn_Wk, L1_xattn_Wv, L1_ffn_gate_w, L1_ffn_gu_w, L1_ffn_dp_w, L1_ffn_sh_gate_w, L1_ffn_sh_up_w, L1_ffn_sh_down_w, L1_ffn_sh_gate1_w):
    import jax
    import jax.numpy as jnp

    def _L0_xattn_ref(B, T, C, w, u, k, v):
        import jax, jax.numpy as jnp
        import numpy as np
        B_DIM, T_DIM, C_DIM = (16, 128, 256)

        def _wkv(w, u, k, v):
            Bn, Tn, Cn = k.shape
            NEG_INF = jnp.float32(-1e+38)

            def step(carry, kv_t):
                p, q, o = carry
                kt, vt = kv_t
                no = jnp.maximum(o, u + kt)
                A = jnp.exp(o - no)
                E = jnp.exp(u + kt - no)
                y = (A * p + E * vt) / (A * q + E)
                no2 = jnp.maximum(w + o, kt)
                A2 = jnp.exp(w + o - no2)
                E2 = jnp.exp(kt - no2)
                return ((A2 * p + E2 * vt, A2 * q + E2, no2), y)
            init = (jnp.zeros((Bn, Cn), k.dtype), jnp.zeros((Bn, Cn), k.dtype), jnp.full((Bn, Cn), NEG_INF, k.dtype))
            kT = jnp.moveaxis(k, 1, 0)
            vT = jnp.moveaxis(v, 1, 0)
            _, yT = jax.lax.scan(step, init, (kT, vT))
            return jnp.moveaxis(yT, 0, 1)
        return _wkv(w, u, k, v)

    def _L0_ffn_ref(x, w_gate, w_up, w_down):
        import jax, jax.numpy as jnp
        import numpy as np
        EPS = 1e-05

        def _quant_weight(w):
            scale = jnp.mean(jnp.abs(w)) + EPS
            wq = jnp.clip(jnp.round(w / scale), -1.0, 1.0)
            return (wq, scale)

        def _quant_act(x):
            s = jnp.max(jnp.abs(x), axis=-1, keepdims=True) / 127.0 + EPS
            xq = jnp.clip(jnp.round(x / s), -128.0, 127.0)
            return (xq, s)

        def _qlinear(x, w):
            wq, ws = _quant_weight(w)
            xq, xs = _quant_act(x)
            y = jnp.einsum('bsi,oi->bso', xq, wq)
            return y * xs * ws
        gate = jax.nn.silu(_qlinear(x, w_gate))
        up = _qlinear(x, w_up)
        return _qlinear(gate * up, w_down)

    def _L1_xattn_ref(x, context, Wq, Wk, Wv):
        import jax, jax.numpy as jnp
        import numpy as np
        DIM = 256
        NHEADS = 32
        HEAD_DIM = DIM // NHEADS
        EPS = 1e-06

        def _rmsnorm(t):
            return t * jax.lax.rsqrt(jnp.mean(t * t, axis=-1, keepdims=True) + EPS)
        b, n, _ = x.shape
        m = context.shape[1]
        q = x @ Wq.T
        k_raw = context @ Wk.T
        v_raw = context @ Wv.T
        q = q.reshape(b, n, NHEADS, HEAD_DIM).transpose(0, 2, 1, 3)
        kv = jnp.concatenate([k_raw, v_raw], axis=-1)
        kv = kv.reshape(b, m, NHEADS, HEAD_DIM, 2)
        k = kv[..., 0].transpose(0, 2, 1, 3)
        v = kv[..., 1].transpose(0, 2, 1, 3)
        q = _rmsnorm(q)
        k = _rmsnorm(k)
        scale = HEAD_DIM ** (-0.5)
        scores = jnp.einsum('bhnd,bhmd->bhnm', q, k) * scale
        attn = jax.nn.softmax(scores, axis=-1)
        out = jnp.einsum('bhnm,bhmd->bhnd', attn, v)
        return out.transpose(0, 2, 1, 3).reshape(b, n, NHEADS * HEAD_DIM)

    def _L1_ffn_ref(h, gate_w, gu_w, dp_w, sh_gate_w, sh_up_w, sh_down_w, sh_gate1_w):
        import jax, jax.numpy as jnp
        import numpy as np
        H = 256
        E = 64
        I = 64
        SI = 64
        TOP_K = 8
        B, T = (2, 64)
        Bb, Tt, Hh = h.shape
        x = h.reshape(Bb * Tt, Hh)
        N = x.shape[0]
        logits = x @ gate_w.T
        topv, topi = jax.lax.top_k(logits, TOP_K)
        rw = jax.nn.softmax(topv.astype(jnp.float32), axis=-1).astype(x.dtype)
        W = jnp.zeros((N, E), x.dtype).at[jnp.arange(N)[:, None], topi].set(rw)
        gu = jnp.einsum('nh,eih->nei', x, gu_w)
        gate, up = (gu[..., :I], gu[..., I:])
        inter = jax.nn.silu(gate) * up
        inter_w = inter * W[:, :, None]
        out = jnp.einsum('nei,ehi->nh', inter_w, dp_w)
        sh_inter = jax.nn.silu(x @ sh_gate_w.T) * (x @ sh_up_w.T)
        sh_out = sh_inter @ sh_down_w.T
        sh_g = jax.nn.sigmoid(x @ sh_gate1_w.T)
        out = out + sh_g * sh_out
        return out.reshape(Bb, Tt, Hh)
    x = x + jnp.tanh(g_xattn[0]) * _L0_xattn_ref(4, 256, 256, L0_xattn_w, L0_xattn_u, _layernorm(x, axis=-1), ctx_2048)
    x = x + jnp.tanh(g_ffn[0]) * _L0_ffn_ref(_layernorm(x, axis=-1), L0_ffn_w_gate, L0_ffn_w_up, L0_ffn_w_down)
    x = x + jnp.tanh(g_xattn[1]) * _L1_xattn_ref(_layernorm(x, axis=-1), ctx_2048, L1_xattn_Wq, L1_xattn_Wk, L1_xattn_Wv)
    x = x + jnp.tanh(g_ffn[1]) * _L1_ffn_ref(_layernorm(x, axis=-1), L1_ffn_gate_w, L1_ffn_gu_w, L1_ffn_dp_w, L1_ffn_sh_gate_w, L1_ffn_sh_up_w, L1_ffn_sh_down_w, L1_ffn_sh_gate1_w)
    return x

_drawn_inputs = setup_inputs


def setup_inputs(seed=0):
    import zlib

    import numpy as np

    out = dict(_drawn_inputs(seed))
    spreads = {'g_ffn': (-1.0, 0.6)}
    factors = {'L1_ffn_gate_w': 8.0,
     'L1_ffn_gu_w': 8.0,
     'L1_ffn_dp_w': 8.0,
     'L1_ffn_sh_gate_w': 8.0,
     'L1_ffn_sh_up_w': 8.0,
     'L1_ffn_sh_down_w': 8.0,
     'L1_ffn_sh_gate1_w': 8.0}
    for name, (base, spread) in spreads.items():
        noise = np.random.default_rng([zlib.crc32(name.encode()), seed]).standard_normal(out[name].shape)
        drawn = base * np.exp(spread * noise) if base else spread * noise
        out[name] = jnp.asarray(drawn.astype(out[name].dtype))
    for name, factor in factors.items():
        out[name] = (out[name] * factor).astype(out[name].dtype)
    return out
```

```python
from contextlib import ExitStack

import numpy as np

import concourse.bass as bass
from concourse import mybir

F32 = mybir.dt.float32
F16 = mybir.dt.float16
BF16 = mybir.dt.bfloat16
ALU = mybir.AluOpType
ACT = mybir.ActivationFunctionType
AX = mybir.AxisListType

P = 128
B, S, D = 4, 256, 256
NT = B * S
TT = NT // P
HT = TT // 2
HALF = NT // 2
DK = D // P
INNER = 1024
KI = INNER // P
HEADS, HD = 32, 8
GROUPS = HEADS // 4
E, EI = 64, 64
PAIRS = E // 2 + 1
TOPK = 8

LN_EPS = 1e-5
Q_EPS = 1e-5
RMS_EPS = 1e-6
MAGIC = 12582912.0
NEG = -1e38
EXP_LN = "natural_log_exp_and_others"
ACT_SCALE = 16.0
W_SCALE = 64.0
UNSCALE = 1.0 / (ACT_SCALE * W_SCALE)
SEL_VALUE = 2.0 ** -6
DOWN_UNSCALE = 1.0 / (ACT_SCALE * W_SCALE * SEL_VALUE * W_SCALE)


def bass_flamingo(nc, x_in, ctxT_in, wkv_in, g_in, ffn_in, proj_in, gate_in, gu_in, dp_in,
                  identf_in, identh_in, sel_in, selS_in, out):
    with ExitStack() as stack:
        def sb(name, shape, dt=F32):
            return stack.enter_context(nc.sbuf_tensor(name, shape, dt))

        def sem(name):
            return stack.enter_context(nc.semaphore(name))

        x = sb("x", [P, TT, D])
        identf = sb("identf", [P, P])
        identh = sb("identh", [P, P], F16)
        wkv = sb("wkv", [P, 2, DK])
        gates = sb("gates", [P, 4])
        tg = sb("tg", [P, 4])
        ntg = sb("ntg", [P, 4])
        magic = sb("magic", [P, 2])
        ones = sb("ones", [P, P])
        xn = sb("xn", [P, 2, HT, D])
        bn = sb("bn", [P, HT, 6])
        mv = sb("mv", [P, HT, 2])
        ve = sb("ve", [P, 2, P])
        lnv = sb("lnv", [P, P])
        root = sb("root", [P, 2, P])
        newt = sb("newt", [P, P])
        rstd = sb("rstd", [P, P])
        hH = sb("hH", [P, DK, NT], F16)
        hL = sb("hL", [P, DK, NT], F16)
        KT = sb("KT", [P, GROUPS, NT], F16)
        vaug = sb("vaug", [P, TT, HEADS, HD + 1])
        ctxT = sb("ctxT", [P, DK, NT])
        ctxH = sb("ctxH", [P, DK, NT], F16)
        ctxL = sb("ctxL", [P, DK, NT], F16)
        proj = sb("proj", [P, DK, 3 * D])
        projH = sb("projH", [P, DK, 3 * D], F16)
        projL = sb("projL", [P, DK, 3 * D], F16)
        gate = sb("gate", [P, DK, E + 1])
        gateH = sb("gateH", [P, DK, E + 1], F16)
        gateL = sb("gateL", [P, DK, E + 1], F16)
        kc = sb("kc", [P, HT, D])
        sq = sb("sq", [P, 2, D])
        ss = sb("ss", [P, HT * HEADS])
        rep = sb("rep", [P, 2, HEADS, 4, HD], F16)
        selS = sb("selS", [2, P], F16)

        regA = sb("regA", [P, 16384])
        regB = sb("regB", [P, 9856])

        def cut(region, start, words):
            return region[:, start:start + words]

        kT = cut(regA, 0, DK * NT).rearrange("p (h t) -> p h t", h=DK)
        fst = cut(regA, 2048, 4096).rearrange("p (b n) -> p b n", b=2)
        CH = 2 * S
        names = ["A2", "E2", "A", "E", "NO", "EV"]
        wk = {n: cut(regA, 6144 + 1024 * i, 1024).rearrange("p (b n) -> p b n", b=2)
              for i, n in enumerate(names)}
        st = {n: cut(regA, 12288 + 1032 * i, 1028).rearrange("p (b s n) -> p b s n", b=2, s=2)
              for i, n in enumerate(["O", "Pn", "Qn"])}
        QT = cut(regA, 0, 4096).bitcast(F16).rearrange("p (g t) -> p g t", g=GROUPS)
        sel = cut(regA, 4096, 2048).bitcast(F16)
        NW = 4
        PW = 2 * DK * P + D
        mst = cut(regA, 6144, NW * PW).rearrange("p (b n) -> p b n", b=NW)
        mwH = cut(regA, 9216, NW * PW // 2).bitcast(F16).rearrange("p (b n) -> p b n", b=NW)
        mwL = cut(regA, 10752, NW * PW // 2).bitcast(F16).rearrange("p (b n) -> p b n", b=NW)
        sgm = cut(regA, 12288, 1024).rearrange("p (b n) -> p b n", b=2)
        inter = cut(regA, 13312, 1024).rearrange("p (b n) -> p b n", b=2)
        inH = cut(regA, 14336, 512).bitcast(F16).rearrange("p (b n) -> p b n", b=2)
        inL = cut(regA, 14848, 512).bitcast(F16).rearrange("p (b n) -> p b n", b=2)
        WT = cut(regA, 15360, 512).bitcast(F16)
        ST = cut(regA, 15872, 512).bitcast(F16)
        accS = cut(regB, 0, 2048).rearrange("p (h t) -> p h t", h=DK)
        YN = cut(regB, 0, 2048).rearrange("p (h t) -> p h t", h=DK)
        fw = cut(regB, 2048, 3072).bitcast(BF16)
        fwg = fw[:, 0:2048].rearrange("p (k n) -> p k n", k=DK)
        fwu = fw[:, 2048:4096].rearrange("p (k n) -> p k n", k=DK)
        fwd = fw[:, 4096:6144].rearrange("p (k n) -> p k n", k=KI)
        xq = cut(regB, 5120, 1024).bitcast(BF16).rearrange("p (k t) -> p k t", k=DK)
        fsg = cut(regB, 6144, 1024)
        fhp = cut(regB, 7168, 1024)
        fz = cut(regB, 8192, 1024)
        hq = cut(regB, 9216, 512).bitcast(BF16).rearrange("p (k t) -> p k t", k=KI)
        NE = 4
        Ex = cut(regB, 0, NE * 1024).rearrange("p (b j n) -> p b j n", b=NE, j=2)
        oT = cut(regB, 4096, 4096).rearrange("p (b g n) -> p b g n", b=2, g=GROUPS)
        oat = cut(regB, 8192, 256)
        LG = cut(regB, 8448, 320).rearrange("p (t e) -> p t e", t=HT)
        zap = cut(regB, 8768, 256).rearrange("p (t e) -> p t e", t=HT)
        ex = cut(regB, 9024, 256).rearrange("p (t e) -> p t e", t=HT)
        Wf = cut(regB, 9280, 256).rearrange("p (t e) -> p t e", t=HT)
        WHL = cut(regB, 9536, 256).bitcast(F16).rearrange("p (t e) -> p t e", t=HT)
        SHL = cut(regB, 9792, 4).bitcast(F16).rearrange("p (t e) -> p t e", t=HT)

        asum = sb("asum", [P, 4])
        ws = sb("ws", [P, 4])
        rws = sb("rws", [P, 4])
        amax = sb("amax", [P, TT])
        qs = sb("qs", [P, TT])
        rqs = sb("rqs", [P, TT])
        sgs = sb("sgs", [P, TT])
        sus = sb("sus", [P, TT])
        tiny = sb("tiny", [P, 8])
        so = sb("so", [P, TT])
        wdt = sb("wdt", [P, 1])
        mx = sb("mx", [P, HT, TOPK])
        nmx = sb("nmx", [P, HT])
        esum = sb("esum", [P, HT])
        ez = sb("ez", [P, HT])
        sgt = sb("sgt", [P, HT])
        rden = sb("rden", [P, HEADS])
        tgd = sb("tgd", [P, 1])

        ps = stack.enter_context(nc.psum_tensor("ps", [P, 8 * 512], F32))

        def bank(i, n=1):
            return ps[:, 512 * i:512 * (i + n)]

        ld_x = [sem(f"ld_x{i}") for i in range(2)]
        ld_const = sem("ld_const")
        ld_ctx = sem("ld_ctx")
        ld_proj = sem("ld_proj")
        ld_ffn = [sem(f"ld_ffn{i}") for i in range(3)]
        ld_sel = sem("ld_sel")
        ld_pair = [sem(f"ld_pair{i}") for i in range(NW)]
        v_ord = sem("v_ord")
        a_ord = sem("a_ord")
        g_ord = sem("g_ord")
        const_set = sem("const_set")
        tanh_done = sem("tanh_done")
        var_ready = sem("var_ready")
        root_ready = sem("root_ready")
        xn_ready = sem("xn_ready")
        xn_turned = sem("xn_turned")
        kT_ready = sem("kT_ready")
        abs_done = sem("abs_done")
        abs_summed = sem("abs_summed")
        ws_ready = sem("ws_ready")
        fz_ready = sem("fz_ready")
        fclamped = sem("fclamped")
        fw_ready = sem("fw_ready")
        scan_done = sem("scan_done")
        diff_done = sem("diff_done")
        exp_done = sem("exp_done")
        den_ready = sem("den_ready")
        recip_ready = sem("recip_ready")
        y_ready = sem("y_ready")
        y_turned = sem("y_turned")
        x1_done = sem("x1_done")
        qs_ready = sem("qs_ready")
        xz_ready = sem("xz_ready")
        xq_ready = sem("xq_ready")
        gu_done = sem("gu_done")
        silu_done = sem("silu_done")
        hp_done = sem("hp_done")
        hz_ready = sem("hz_ready")
        hz_turned = sem("hz_turned")
        hq_ready = sem("hq_ready")
        down_done = sem("down_done")
        x2_done = sem("x2_done")
        splitH = sem("splitH")
        splitL = sem("splitL")
        proj_done = sem("proj_done")
        sq_ready = sem("sq_ready")
        proj_read = sem("proj_read")
        sq_read = sem("sq_read")
        kn_ready = sem("kn_ready")
        repH = sem("repH")
        repL = sem("repL")
        rep_turned = sem("rep_turned")
        qk_ready = sem("qk_ready")
        hH_ready = sem("hH_ready")
        hL_ready = sem("hL_ready")
        score_done = sem("score_done")
        prob_ready = sem("prob_ready")
        pv_done = sem("pv_done")
        oT_ready = sem("oT_ready")
        o_turned = sem("o_turned")
        x3_done = sem("x3_done")
        logit_done = sem("logit_done")
        LG_ready = sem("LG_ready")
        ex_ready = sem("ex_ready")
        W_ready = sem("W_ready")
        W_turned = sem("W_turned")
        WT_ready = sem("WT_ready")
        mwH_ready = sem("mwH_ready")
        mwL_ready = sem("mwL_ready")
        egu_done = sem("egu_done")
        esilu_done = sem("esilu_done")
        et_done = sem("et_done")
        wb_done = sem("wb_done")
        inter_ready = sem("inter_ready")
        inH_ready = sem("inH_ready")
        inL_ready = sem("inL_ready")
        edown_done = sem("edown_done")
        acc_read = sem("acc_read")
        acc_turned = sem("acc_turned")
        out_ready = sem("out_ready")
        out_done = sem("out_done")

        x_rows = x_in.rearrange("(t p) d -> p t d", p=P)
        out_rows = out.rearrange("(t p) d -> p t d", p=P)

        NCH = 2 * PAIRS

        block = stack.enter_context(nc.Block())

        @block.sync
        def _(sp):
            for i in range(2):
                sp.dma_start(x[:, HT * i:HT * (i + 1), :], x_rows[:, HT * i:HT * (i + 1), :]).then_inc(ld_x[i], 16)
                if i == 0:
                    sp.dma_start(identf[:, :], identf_in).then_inc(ld_const, 16)
                    sp.dma_start(wkv[:, :, :], wkv_in).then_inc(ld_const, 16)
                    sp.dma_start(gates[:, :], g_in).then_inc(ld_const, 16)
                    sp.dma_start(identh[:, :], identh_in).then_inc(ld_const, 16)
                    sp.dma_start(selS[:, :], selS_in).then_inc(ld_const, 16)
            sp.dma_start(ctxT[:, :, :], ctxT_in).then_inc(ld_ctx, 16)
            for i in range(2):
                sp.dma_start(fst[:, i, :], ffn_in[:, i, :]).then_inc(ld_ffn[i], 16)
            sp.dma_start(proj[:, :, :], proj_in).then_inc(ld_proj, 16)
            sp.dma_start(gate[:, :, :], gate_in).then_inc(ld_proj, 16)
            sp.wait_ge(fw_ready, 1)
            sp.dma_start(fst[:, 0, :], ffn_in[:, 2, :]).then_inc(ld_ffn[2], 16)
            sp.wait_ge(fw_ready, 3)
            sp.wait_ge(y_ready, 4)
            sp.dma_start(sel[:, :], sel_in).then_inc(ld_sel, 16)
            for p in range(PAIRS):
                if p >= NW:
                    sp.wait_ge(mwH_ready, p - NW + 1)
                    sp.wait_ge(mwL_ready, p - NW + 1)
                sp.dma_start(mst[:, p % NW, 0:2 * DK * P], gu_in[:, p, :]).then_inc(ld_pair[p % NW], 16)
                sp.dma_start(mst[:, p % NW, 2 * DK * P:PW], dp_in[:, p, :]).then_inc(ld_pair[p % NW], 16)
            for h in range(2):
                sp.wait_ge(out_ready, HT * (h + 1))
                sp.dma_start(out_rows[:, HT * h:HT * (h + 1), :], x[:, HT * h:HT * (h + 1), :]).then_inc(out_done, 16)
            sp.wait_ge(out_done, 32)

        @block.gpsimd
        def _(pool):
            def clamp(m):
                pool.wait_ge(fz_ready, m + 1)
                s = m % 2
                nc.gpsimd.tensor_scalar(fst[:, s, :], fst[:, s, :], MAGIC + 1.0, MAGIC - 1.0,
                                        ALU.min, ALU.max).then_inc(fclamped, 1)

            def differences(c):
                h, s = c // 2, c % 2
                O = st["O"][:, s]
                k = kT[:, s, h * CH:(h + 1) * CH].rearrange("p (b n) -> p b n", b=2)
                view = {n: wk[n][:, s, :].rearrange("p (b n) -> p b n", b=2) for n in names}
                pool.wait_ge(scan_done, c + 1)
                nc.gpsimd.tensor_tensor(view["A2"], O[:, :, 0:S], O[:, :, 1:S + 1], ALU.subtract).then_inc(diff_done, 1)
                nc.gpsimd.tensor_tensor(view["E2"], k, O[:, :, 1:S + 1], ALU.subtract).then_inc(diff_done, 1)
                nc.gpsimd.tensor_tensor(view["A"], O[:, :, 0:S], view["NO"], ALU.subtract).then_inc(diff_done, 1)
                nc.gpsimd.tensor_tensor(view["E"], k, view["NO"], ALU.subtract).then_inc(diff_done, 1)

            differences(0)
            differences(1)
            clamp(0)
            clamp(1)
            differences(2)
            differences(3)
            clamp(2)

        @block.scalar
        def _(act):
            done = [0]

            def post(ins):
                done[0] += 1
                ins.then_inc(a_ord, 1)

            def settle():
                act.wait_ge(a_ord, done[0])

            event = [0]

            def first_root(n):
                e = event[0]
                event[0] += 1
                act.wait_ge(var_ready, e + 1)
                post(nc.scalar.activation(lnv[:, 0:n], ve[:, e % 2, 0:n], ACT.Ln))
                settle()
                nc.scalar.activation(root[:, e % 2, 0:n], lnv[:, 0:n], ACT.Exp, scale=-0.5).then_inc(root_ready, 1)
                act.wait_ge(root_ready, e + 1)

            act.wait_ge(ld_const, 80)
            nc.scalar.activation(tg[:, :], gates[:, :], ACT.Tanh).then_inc(tanh_done, 1)
            nc.scalar.preload_act_table_set(EXP_LN)
            first_root(HT)
            first_root(HT)
            for h in range(2):
                act.wait_ge(xn_turned, h + 1)
                for k in range(DK):
                    nc.scalar.copy(kT[:, k, h * HALF:(h + 1) * HALF], bank(2 * h + k)).then_inc(kT_ready, 1)

            def abs_sum(m):
                act.wait_ge(ld_ffn[m], 16)
                nc.scalar.activation(cut(regB, 5120, 2048), fst[:, m % 2, :], ACT.Abs,
                                     accum_out=asum[:, m:m + 1]).then_inc(abs_done, 1)
                act.wait_ge(abs_done, m + 1)

            def to_integers(m):
                act.wait_ge(ws_ready, m + 1)
                nc.scalar.activation(fst[:, m % 2, :], fst[:, m % 2, :], ACT.Identity, bias=magic[:, 0:1],
                                     scale=rws[:, m:m + 1]).then_inc(fz_ready, 1)

            def drop_magic(m):
                act.wait_ge(fclamped, m + 1)
                nc.scalar.activation(fw[:, 2048 * m:2048 * (m + 1)], fst[:, m % 2, :], ACT.Identity,
                                     bias=magic[:, 1:2]).then_inc(fw_ready, 1)

            def exponentials(c):
                s = c % 2
                for i, (n, b) in enumerate((("A2", wkv[:, 0, s:s + 1]), ("E2", 0.0), ("A", 0.0), ("E", wkv[:, 1, s:s + 1]))):
                    act.wait_ge(diff_done, 4 * c + i + 1)
                    nc.scalar.activation(wk[n][:, s, :], wk[n][:, s, :], ACT.Exp, bias=b).then_inc(exp_done, 1)

            def reciprocal_guess(c):
                s = c % 2
                act.wait_ge(den_ready, c + 1)
                post(nc.scalar.activation(wk["A"][:, s, :], wk["EV"][:, s, :], ACT.Ln))
                settle()
                nc.scalar.activation(wk["A"][:, s, :], wk["A"][:, s, :], ACT.Exp, scale=-1.0).then_inc(recip_ready, 1)

            act.wait_ge(const_set, 1)
            abs_sum(0)
            abs_sum(1)
            exponentials(0)
            exponentials(1)
            to_integers(0)
            to_integers(1)
            reciprocal_guess(0)
            reciprocal_guess(1)
            drop_magic(0)
            drop_magic(1)
            exponentials(2)
            exponentials(3)
            abs_sum(2)
            to_integers(2)
            reciprocal_guess(2)
            reciprocal_guess(3)
            drop_magic(2)

            act.wait_ge(ld_ctx, 16)
            nc.scalar.activation(ctxH[:, :, :], ctxT[:, :, :], ACT.Copy, scale=ACT_SCALE).then_inc(splitH, 1)
            act.wait_ge(ld_proj, 32)
            nc.scalar.activation(projH[:, :, :], proj[:, :, :], ACT.Copy, scale=W_SCALE).then_inc(splitH, 1)
            nc.scalar.activation(gateH[:, :, :], gate[:, :, :], ACT.Copy, scale=W_SCALE).then_inc(splitH, 1)

            def projected(n0, keys):
                for n in range(n0, n0 + HT):
                    j = n % HT
                    src = bank(2 + n % 2)
                    act.wait_ge(proj_done, n + 1)
                    if n >= HT:
                        act.wait_ge(repL, n0)
                    post(nc.scalar.activation(kc[:, j, :], src[:, 0:D], ACT.Copy, scale=UNSCALE))
                    if n >= 2:
                        act.wait_ge(sq_read, n - 1)
                    nc.scalar.activation(sq[:, n % 2, :], src[:, 0:D], ACT.Square, scale=UNSCALE).then_inc(sq_ready, 1)
                    if keys:
                        post(nc.scalar.activation(vaug[:, n, :, 0:HD],
                                                  src[:, D:2 * D].rearrange("p (h d) -> p h d", h=HEADS),
                                                  ACT.Copy, scale=UNSCALE))
                    settle()
                    act.wait_ge(sq_ready, n + 1)
                    nc.scalar.nop().then_inc(proj_read, 1)
                first_root(HT * HEADS)
                for n in range(n0, n0 + HT):
                    j = n % HT
                    act.wait_ge(kn_ready, n + 1)
                    if n >= 2:
                        act.wait_ge(rep_turned, n - 1)
                    dst = rep[:, n % 2, :, 0:4:2, :] if keys else rep[:, n % 2, :, 0:2, :]
                    src = kc[:, j, :].rearrange("p (h d) -> p h d", h=HEADS).unsqueeze(2).broadcast_to([P, HEADS, 2, HD])
                    nc.scalar.copy(dst, src).then_inc(repH, 1)

            projected(0, True)
            projected(HT, True)

            def ffn_inputs(h):
                if h == 1:
                    nc.scalar.preload_act_table_set(EXP_LN)
                first_root(HT)
                nc.scalar.preload_act_table(ACT.Silu)
                for j in range(HT):
                    t = h * HT + j
                    act.wait_ge(qs_ready, h + 1)
                    nc.scalar.activation(xn[:, h % 2, j, :], xn[:, h % 2, j, :], ACT.Identity,
                                         bias=magic[:, 0:1], scale=rqs[:, t:t + 1]).then_inc(xz_ready, 1)
                act.wait_ge(xn_turned, 3 + h)
                for k in range(DK):
                    nc.scalar.activation(xq[:, k, h * HALF:(h + 1) * HALF], bank(k), ACT.Identity,
                                         bias=magic[:, 1:2]).then_inc(xq_ready, 1)

            def ffn_silu(t):
                act.wait_ge(gu_done, t + 1)
                if t >= 1:
                    act.wait_ge(hp_done, t)
                nc.scalar.activation(fsg, bank(2, 2), ACT.Silu, scale=sgs[:, t:t + 1]).then_inc(silu_done, 1)

            def ffn_turned(t):
                act.wait_ge(hz_turned, t + 1)
                if t >= 1:
                    act.wait_ge(down_done, t)
                nc.scalar.activation(hq[:, :, :], bank(6, 2).rearrange("p (k t) -> p k t", k=KI), ACT.Identity,
                                     bias=magic[:, 1:2]).then_inc(hq_ready, 1)

            for h in range(2):
                ffn_inputs(h)
                for t in range(h * HT, (h + 1) * HT):
                    ffn_silu(t)
                    if t > h * HT:
                        ffn_turned(t - 1)
                ffn_turned((h + 1) * HT - 1)

            def high_halves(q):
                h = q % 2
                first_root(HT)
                act.wait_ge(xn_turned, q + 1)
                for k in range(DK):
                    nc.scalar.copy(hH[:, k, h * HALF:(h + 1) * HALF], bank(k)).then_inc(hH_ready, 1)

            nc.scalar.preload_act_table_set(EXP_LN)
            for h in range(2):
                high_halves(4 + h)
                projected(2 * HT + HT * h, False)

            def probabilities(u):
                act.wait_ge(score_done, u + 1)
                if u >= NE:
                    act.wait_ge(pv_done, (u - NE) // 2 + 1)
                nc.scalar.activation(Ex[:, u % NE, :, :], bank(2 * (u % 3), 2).rearrange("p (j n) -> p j n", j=2),
                                     ACT.Exp, scale=float(HD) ** -0.5).then_inc(prob_ready, 1)

            def routing(h):
                high_halves(6 + h)
                act.wait_ge(LG_ready, h + 1)
                for j in range(HT):
                    post(nc.scalar.activation(ex[:, j, :], LG[:, j, 0:E], ACT.Exp, bias=nmx[:, j:j + 1]))
                nc.scalar.activation(ez[:, :], LG[:, :, E], ACT.Exp, scale=-1.0).then_inc(ex_ready, 1)
                act.wait_ge(W_turned, h + 1)
                post(nc.scalar.copy(WT[:, h * HALF:(h + 1) * HALF], bank(4).bitcast(F16)[:, 0:HALF]))
                nc.scalar.copy(ST[0:2, h * HALF:(h + 1) * HALF],
                               bank(5)[0:2, :].bitcast(F16)[:, 0:HALF]).then_inc(WT_ready, 1)

            for h in range(2):
                for u in range(32 * h, 32 * (h + 1)):
                    probabilities(u)
                routing(h)

            def weights_high(p):
                act.wait_ge(ld_pair[p % NW], 32 * (p // NW + 1))
                if p >= NW:
                    act.wait_ge(edown_done, 2 * (p - NW + 1))
                nc.scalar.activation(mwH[:, p % NW, :], mst[:, p % NW, :], ACT.Copy, scale=W_SCALE).then_inc(mwH_ready, 1)

            weights_high(0)
            weights_high(1)
            weights_high(2)
            for c in range(NCH + 1):
                if c < NCH:
                    act.wait_ge(egu_done, c + 1)
                    if c >= 2:
                        act.wait_ge(inter_ready, c - 1)
                    nc.scalar.activation(sgm[:, c % 2, :], bank(4 + 2 * (c % 2)), ACT.Silu, scale=UNSCALE).then_inc(esilu_done, 1)
                if c >= 1:
                    if c >= 3:
                        act.wait_ge(edown_done, c - 2)
                    act.wait_ge(inter_ready, c)
                    nc.scalar.copy(inH[:, (c - 1) % 2, :], inter[:, (c - 1) % 2, :]).then_inc(inH_ready, 1)
                if c % 2 == 1 and c // 2 + 3 < PAIRS:
                    weights_high(c // 2 + 3)
            act.wait_ge(edown_done, NCH)
            for k in range(DK):
                nc.scalar.copy(accS[:, k, :], bank(2 * k, 2)).then_inc(acc_read, 1)

        @block.vector
        def _(dve):
            done = [0]

            def post(ins):
                done[0] += 1
                ins.then_inc(v_ord, 1)

            def settle():
                dve.wait_ge(v_ord, done[0])

            def link(ins):
                post(ins)
                settle()

            V = nc.vector
            event = [0]

            def inverse_root(src, n, mul, eps, gain):
                e = event[0]
                event[0] += 1
                v, r = ve[:, e % 2, 0:n], root[:, e % 2, 0:n]
                V.tensor_scalar(v, src, mul, eps, ALU.mult, ALU.add).then_inc(var_ready, 1)
                dve.wait_ge(var_ready, e + 1)
                dve.wait_ge(root_ready, e + 1)
                link(V.tensor_tensor(newt[:, 0:n], v, r, ALU.mult))
                link(V.tensor_tensor(newt[:, 0:n], newt[:, 0:n], r, ALU.mult))
                link(V.tensor_scalar(newt[:, 0:n], newt[:, 0:n], -0.5 * gain, 1.5 * gain, ALU.mult, ALU.add))
                link(V.tensor_tensor(rstd[:, 0:n], newt[:, 0:n], r, ALU.mult))

            def normalise(q, gain, publish=True):
                h = q % 2
                for j in range(HT):
                    post(V.bn_stats(bn[:, j, :], x[:, h * HT + j, :]))
                settle()
                for j in range(HT):
                    post(V.bn_aggr(mv[:, j, :], bn[:, j, :]))
                settle()
                inverse_root(mv[:, :, 1], HT, 1.0, LN_EPS, gain)
                if q >= 2:
                    dve.wait_ge(xn_turned, q - 1)
                for j in range(HT):
                    ins = V.tensor_scalar(xn[:, h, j, :], x[:, h * HT + j, :], mv[:, j, 0:1], rstd[:, j:j + 1],
                                          ALU.subtract, ALU.mult)
                    if publish:
                        ins.then_inc(xn_ready, 1)
                    else:
                        post(ins)

            post(V.memset(magic[:, 0:1], MAGIC))
            post(V.memset(magic[:, 1:2], -MAGIC))
            post(V.memset(ones[:, :], 1.0))
            post(V.memset(vaug[:, :, :, HD:HD + 1], 1.0))
            post(V.memset(st["O"][:, :, :, 0:1], NEG))
            post(V.memset(st["Pn"][:, :, :, 0:1], 0.0))
            post(V.memset(st["Qn"][:, :, :, 0:1], 0.0))
            settle()
            V.memset(tiny[:, :], 0.0).then_inc(const_set, 1)
            dve.wait_ge(tanh_done, 1)
            post(V.tensor_scalar(ntg[:, :], tg[:, :], -1.0, None, ALU.mult))
            post(V.tensor_scalar(tgd[:, :], tg[:, 3:4], DOWN_UNSCALE, None, ALU.mult))

            for h in range(2):
                dve.wait_ge(ld_x[h], 16)
                normalise(h, 1.0)

            def chunk(c):
                h, s = c // 2, c % 2
                two = lambda a: a.rearrange("p (b n) -> p b n", b=2)
                return (h, s, two(kT[:, s, h * CH:(h + 1) * CH]), two(ctxT[:, s, h * CH:(h + 1) * CH]),
                        {n: two(wk[n][:, s, :]) for n in names}, {n: st[n][:, s] for n in st})

            def running_max(c):
                h, s, k, v, W, Z = chunk(c)
                dve.wait_ge(kT_ready, 2 * h + s + 1)
                if c >= 2:
                    dve.wait_ge(exp_done, 4 * (c - 1))
                wb = wkv[:, 0, s:s + 1].broadcast_to([P, S])
                for b in range(2):
                    post(V.tensor_tensor_scan(Z["O"][:, b, 1:S + 1], wb, k[:, b, :], NEG, ALU.add, ALU.max))
                settle()
                V.scalar_tensor_tensor(W["NO"], k, wkv[:, 1, s:s + 1], Z["O"][:, :, 0:S], ALU.add,
                                       ALU.max).then_inc(scan_done, 1)

            def sums(c):
                h, s, k, v, W, Z = chunk(c)
                dve.wait_ge(exp_done, 4 * c + 2)
                link(V.tensor_tensor(W["EV"], W["E2"], v, ALU.mult))
                for b in range(2):
                    post(V.tensor_tensor_scan(Z["Pn"][:, b, 1:S + 1], W["A2"][:, b, :], W["EV"][:, b, :], 0.0, ALU.mult, ALU.add))
                    post(V.tensor_tensor_scan(Z["Qn"][:, b, 1:S + 1], W["A2"][:, b, :], W["E2"][:, b, :], 0.0, ALU.mult, ALU.add))
                settle()
                dve.wait_ge(exp_done, 4 * c + 4)
                post(V.tensor_tensor(W["EV"], W["A"], Z["Qn"][:, :, 0:S], ALU.mult))
                post(V.tensor_tensor(W["NO"], W["A"], Z["Pn"][:, :, 0:S], ALU.mult))
                post(V.tensor_tensor(W["A2"], W["E"], v, ALU.mult))
                settle()
                V.tensor_tensor(W["EV"], W["EV"], W["E"], ALU.add).then_inc(den_ready, 1)
                link(V.tensor_tensor(W["NO"], W["NO"], W["A2"], ALU.add))

            def quotient(c):
                h, s, k, v, W, Z = chunk(c)
                dve.wait_ge(recip_ready, c + 1)
                dve.wait_ge(den_ready, c + 1)
                post(V.tensor_tensor(W["EV"], W["EV"], W["A"], ALU.mult))
                post(V.tensor_tensor(W["NO"], W["NO"], W["A"], ALU.mult))
                settle()
                V.scalar_tensor_tensor(YN[:, s, h * CH:(h + 1) * CH], wk["EV"][:, s, :], -2.0, wk["NO"][:, s, :],
                                       ALU.add, ALU.mult).then_inc(y_ready, 1)

            def weight_scales(m0, m1):
                dve.wait_ge(abs_summed, 1 if m0 == 0 else 2)
                link(V.tensor_scalar(ws[:, m0:m1], bank(7)[:, m0:m1], 1.0 / (INNER * D), Q_EPS, ALU.mult, ALU.add))
                V.reciprocal(rws[:, m0:m1], ws[:, m0:m1]).then_inc(ws_ready, m1 - m0)

            dve.wait_ge(ld_const, 80)
            dve.wait_ge(ld_ctx, 16)
            running_max(0)
            running_max(1)
            weight_scales(0, 2)
            sums(0)
            sums(1)
            quotient(0)
            running_max(2)
            quotient(1)
            running_max(3)
            sums(2)
            sums(3)
            weight_scales(2, 3)
            quotient(2)
            quotient(3)

            for i, (lo, hi, src, scale) in enumerate(((ctxL, ctxH, ctxT, ACT_SCALE), (projL, projH, proj, W_SCALE),
                                                      (gateL, gateH, gate, W_SCALE))):
                dve.wait_ge(splitH, i + 1)
                V.scalar_tensor_tensor(lo[:, :, :], src[:, :, :], scale, hi[:, :, :], ALU.mult,
                                       ALU.subtract).then_inc(splitL, 1)

            def split_rows(n0, keys):
                for n in range(n0, n0 + HT):
                    dve.wait_ge(sq_ready, n + 1)
                    j = n % HT
                    V.tensor_reduce(ss[:, j * HEADS:(j + 1) * HEADS],
                                    sq[:, n % 2, :].rearrange("p (h d) -> p h d", h=HEADS),
                                    AX.X, ALU.add).then_inc(sq_read, 1)
                dve.wait_ge(sq_read, n0 + HT)
                inverse_root(ss[:, :], HT * HEADS, 1.0 / HD, RMS_EPS, 1.0)
                dve.wait_ge(proj_read, n0 + HT)
                for n in range(n0, n0 + HT):
                    j = n % HT
                    rows = kc[:, j, :].rearrange("p (h d) -> p h d", h=HEADS)
                    V.tensor_tensor(rows, rows, rstd[:, j * HEADS:(j + 1) * HEADS].unsqueeze(2).broadcast_to([P, HEADS, HD]),
                                    ALU.mult).then_inc(kn_ready, 1)

                def low(n):
                    dve.wait_ge(repH, n + 1)
                    R = rep[:, n % 2]
                    rows = kc[:, n % HT, :].rearrange("p (h d) -> p h d", h=HEADS).unsqueeze(2).broadcast_to([P, HEADS, 2, HD])
                    hi, lo = (R[:, :, 0:4:2, :], R[:, :, 1:4:2, :]) if keys else (R[:, :, 0:2, :], R[:, :, 2:4, :])
                    V.tensor_tensor(lo, rows, hi, ALU.subtract).then_inc(repL, 1)

                def turned(n):
                    dve.wait_ge(rep_turned, n + 1)
                    dst = KT if keys else QT
                    t = n % TT
                    V.tensor_copy(dst[:, :, t * P:(t + 1) * P],
                                  bank(4 + n % 2).bitcast(F16).rearrange("p (g t) -> p g t", g=GROUPS)).then_inc(qk_ready, 1)

                dve.wait_ge(kn_ready, n0 + HT)
                low(n0)
                for n in range(n0 + 1, n0 + HT):
                    low(n)
                    turned(n - 1)
                turned(n0 + HT - 1)

            split_rows(0, True)
            split_rows(HT, True)

            def ffn_residual(t):
                dve.wait_ge(down_done, t + 1)
                V.scalar_tensor_tensor(x[:, t, :], bank(t % 2)[:, 0:D], so[:, t:t + 1], x[:, t, :],
                                       ALU.mult, ALU.add).then_inc(x2_done, 1)

            for h in range(2):
                for j in range(HT):
                    t = h * HT + j
                    dve.wait_ge(y_turned, (t | 1) + 1)
                    V.scalar_tensor_tensor(x[:, t, :], bank(4 + j // 2)[:, (j % 2) * D:(j % 2 + 1) * D], ntg[:, 0:1],
                                           x[:, t, :], ALU.mult, ALU.add).then_inc(x1_done, 1)
                dve.wait_ge(x1_done, HT * (h + 1))
                normalise(2 + h, 1.0, publish=False)
                settle()
                hs = slice(h * HT, (h + 1) * HT)
                link(V.tensor_reduce(amax[:, hs], xn[:, h, :, :], AX.X, ALU.max, apply_absolute_value=True))
                link(V.tensor_scalar(qs[:, hs], amax[:, hs], 1.0 / 127.0, Q_EPS, ALU.mult, ALU.add))
                post(V.tensor_scalar(sus[:, hs], qs[:, hs], ws[:, 1:2], None, ALU.mult))
                post(V.tensor_scalar(sgs[:, hs], qs[:, hs], ws[:, 0:1], None, ALU.mult))
                post(V.tensor_scalar(wdt[:, :], ws[:, 2:3], tg[:, 1:2], None, ALU.mult))
                V.reciprocal(rqs[:, hs], qs[:, hs]).then_inc(qs_ready, 1)
                settle()
                for t in range(h * HT, (h + 1) * HT):
                    dve.wait_ge(silu_done, t + 1)
                    V.tensor_tensor(fhp, bank(4, 2), fsg, ALU.mult).then_inc(hp_done, 1)
                    dve.wait_ge(hp_done, t + 1)
                    link(V.tensor_reduce(tiny[:, 0:1], fhp, AX.X, ALU.max, apply_absolute_value=True))
                    link(V.tensor_scalar(tiny[:, 1:2], tiny[:, 0:1], sus[:, t:t + 1], 1.0 / 127.0, ALU.mult, ALU.mult))
                    link(V.tensor_scalar(tiny[:, 2:3], tiny[:, 1:2], Q_EPS, None, ALU.add))
                    link(V.reciprocal(tiny[:, 3:4], tiny[:, 2:3]))
                    link(V.tensor_tensor(tiny[:, 4:5], tiny[:, 3:4], sus[:, t:t + 1], ALU.mult))
                    post(V.tensor_tensor(so[:, t:t + 1], tiny[:, 2:3], wdt[:, :], ALU.mult))
                    if t >= 1:
                        dve.wait_ge(hz_turned, t)
                    V.tensor_scalar(fz, fhp, tiny[:, 4:5], MAGIC, ALU.mult, ALU.add).then_inc(hz_ready, 1)
                    settle()
                    dve.wait_ge(hz_ready, t + 1)
                    if t > h * HT:
                        ffn_residual(t - 1)
                ffn_residual((h + 1) * HT - 1)

            def low_halves(q):
                h = q % 2
                normalise(q, ACT_SCALE)
                for k in range(DK):
                    dve.wait_ge(hH_ready, 2 * (q - 4) + k + 1)
                    V.tensor_tensor(hL[:, k, h * HALF:(h + 1) * HALF], bank(k), hH[:, k, h * HALF:(h + 1) * HALF],
                                    ALU.subtract).then_inc(hL_ready, 1)

            for h in range(2):
                dve.wait_ge(x2_done, HT * (h + 1))
                low_halves(4 + h)
                split_rows(2 * HT + HT * h, False)

            for h in range(2):
                for n in range(16 * h, 16 * (h + 1)):
                    b, g = n // GROUPS, n % GROUPS
                    dve.wait_ge(pv_done, n + 1)
                    V.tensor_copy(oT[:, b % 2, g, :], bank(6 + n % 2)[:, 0:S]).then_inc(oT_ready, 1)
                for j in range(HT):
                    t = h * HT + j
                    dve.wait_ge(o_turned, t + 1)
                    o = bank(2 * (j % 2), 2).rearrange("p (h e) -> p h e", e=32)
                    link(V.reciprocal(rden[:, :].unsqueeze(2), o[:, :, HD:HD + 1]))
                    link(V.tensor_tensor(oat.rearrange("p (h d) -> p h d", h=HEADS), o[:, :, 0:HD],
                                         rden[:, :].unsqueeze(2).broadcast_to([P, HEADS, HD]), ALU.mult))
                    V.scalar_tensor_tensor(x[:, t, :], oat, tg[:, 2:3], x[:, t, :], ALU.mult, ALU.add).then_inc(x3_done, 1)
                    dve.wait_ge(x3_done, t + 1)
                low_halves(6 + h)
                dve.wait_ge(logit_done, h + 1)
                link(V.tensor_scalar(LG[:, :, 0:E + 1], bank(6).rearrange("p (t e) -> p t e", t=HT)[:, :, 0:E + 1], UNSCALE,
                                     None, ALU.mult))
                for j in range(HT):
                    post(V.max(mx[:, j, :], LG[:, j, 0:E]))
                settle()
                V.tensor_scalar(nmx[:, :], mx[:, :, 0], -1.0, None, ALU.mult).then_inc(LG_ready, 1)
                for j in range(HT):
                    post(V.match_replace(zap[:, j, :], mx[:, j, :], LG[:, j, 0:E], 2.0 * NEG))
                settle()
                dve.wait_ge(ex_ready, h + 1)
                for j in range(HT):
                    post(V.scalar_tensor_tensor(Wf[:, j, :], zap[:, j, :], NEG, ex[:, j, :], ALU.is_lt, ALU.mult,
                                                accum_out=esum[:, j:j + 1]))
                link(V.tensor_scalar(ez[:, :], ez[:, :], 1.0, None, ALU.add))
                post(V.reciprocal(esum[:, :], esum[:, :]))
                link(V.reciprocal(sgt[:, :], ez[:, :]))
                link(V.tensor_tensor(Wf[:, :, :], Wf[:, :, :], esum[:, :].unsqueeze(2).broadcast_to([P, HT, E]), ALU.mult))
                if h >= 1:
                    dve.wait_ge(W_turned, h)
                post(V.tensor_copy(WHL[:, :, 0:E], Wf[:, :, :]))
                link(V.tensor_copy(SHL[:, :, 0:1], sgt[:, :].unsqueeze(2)))
                post(V.tensor_tensor(WHL[:, :, E:2 * E], Wf[:, :, :], WHL[:, :, 0:E], ALU.subtract))
                V.tensor_tensor(SHL[:, :, 1:2], sgt[:, :].unsqueeze(2), SHL[:, :, 0:1], ALU.subtract).then_inc(W_ready, 1)

            def weights_low(p):
                dve.wait_ge(mwH_ready, p + 1)
                V.scalar_tensor_tensor(mwL[:, p % NW, :], mst[:, p % NW, :], W_SCALE, mwH[:, p % NW, :],
                                       ALU.mult, ALU.subtract).then_inc(mwL_ready, 1)

            weights_low(0)
            weights_low(1)
            weights_low(2)
            for c in range(NCH + 1):
                d = c - 1
                if c >= 1:
                    dve.wait_ge(wb_done, d + 1)
                    dve.wait_ge(et_done, d + 1)
                    if d >= 2:
                        dve.wait_ge(inH_ready, d - 1)
                    V.tensor_tensor(inter[:, d % 2, :], bank(4 + 2 * (d % 2)), sgm[:, d % 2, :], ALU.mult).then_inc(inter_ready, 1)
                if c < NCH:
                    dve.wait_ge(esilu_done, c + 1)
                    V.tensor_tensor(sgm[:, c % 2, :], bank(5 + 2 * (c % 2)), sgm[:, c % 2, :], ALU.mult).then_inc(et_done, 1)
                if c >= 1:
                    dve.wait_ge(inH_ready, d + 1)
                    if d >= 2:
                        dve.wait_ge(edown_done, d - 1)
                    V.tensor_tensor(inL[:, d % 2, :], inter[:, d % 2, :], inH[:, d % 2, :], ALU.subtract).then_inc(inL_ready, 1)
                if c % 2 == 1 and c // 2 + 3 < PAIRS:
                    weights_low(c // 2 + 3)
            for t in range(TT):
                dve.wait_ge(acc_turned, t + 1)
                V.scalar_tensor_tensor(x[:, t, :], bank(4 + t % 4)[:, 0:D], tgd[:, 0:1], x[:, t, :],
                                       ALU.mult, ALU.add).then_inc(out_ready, 1)

        @block.tensor
        def _(pe):
            T = nc.tensor

            def turn_half(q, b0):
                for j in range(HT):
                    if q in (2, 3):
                        pe.wait_ge(xz_ready, HT * (q - 2) + j + 1)
                    else:
                        pe.wait_ge(xn_ready, HT * (q if q < 2 else q - 2) + j + 1)
                    for k in range(DK):
                        mm = T.transpose(bank(b0 + k)[:, j * P:(j + 1) * P], xn[:, q % 2, j, k * P:(k + 1) * P], identf[:, :])
                mm.then_inc(xn_turned, 1)

            pe.wait_ge(ld_const, 80)
            turn_half(0, 0)
            turn_half(1, 2)
            pe.wait_ge(const_set, 1)

            def sum_abs(m0, m1):
                pe.wait_ge(abs_done, m1)
                T.matmul(bank(7)[:, m0:m1], ones[:, :], asum[:, m0:m1], start=True, stop=True).then_inc(abs_summed, 1)

            sum_abs(0, 2)
            sum_abs(2, 3)

            def three_pass(out_ap, wH, wL, aH, aL):
                n = 0
                for k in range(DK):
                    for w, a in ((wH, aH), (wH, aL), (wL, aH)):
                        mm = T.matmul(out_ap, w(k), a(k), start=(n == 0), stop=(n == 3 * DK - 1))
                        n += 1
                return mm

            def project(n0, keys):
                for n in range(n0, n0 + HT):
                    t = n % TT
                    if n >= 2:
                        pe.wait_ge(proj_read, n - 1)
                    H, L = (ctxH, ctxL) if keys else (hH, hL)
                    cols = slice(D, 3 * D) if keys else slice(0, D)
                    width = 2 * D if keys else D
                    three_pass(bank(2 + n % 2)[:, 0:width],
                               lambda k: H[:, k, t * P:(t + 1) * P], lambda k: L[:, k, t * P:(t + 1) * P],
                               lambda k: projH[:, k, cols], lambda k: projL[:, k, cols]).then_inc(proj_done, 1)
                for n in range(n0, n0 + HT):
                    pe.wait_ge(repL, n + 1)
                    if n >= 2:
                        pe.wait_ge(qk_ready, n - 1)
                    for g in range(GROUPS):
                        mm = T.transpose(bank(4 + n % 2).bitcast(F16)[:, g * P:(g + 1) * P],
                                         rep[:, n % 2, 4 * g:4 * g + 4, :, :], identh[:, :])
                    mm.then_inc(rep_turned, 1)

            pe.wait_ge(kT_ready, 4)
            pe.wait_ge(splitL, 3)
            project(0, True)
            project(HT, True)

            def gate_up(t):
                if t % HT == 0:
                    pe.wait_ge(xq_ready, 2 * (t // HT + 1))
                    pe.wait_ge(fw_ready, 3)
                    pe.wait_ge(x1_done, HT * (t // HT + 1))
                if t >= 1:
                    pe.wait_ge(silu_done, t)
                    pe.wait_ge(hp_done, t)
                for half, w in ((0, fwg), (1, fwu)):
                    for n in range(2):
                        for k in range(DK):
                            mm = T.matmul(bank(2 + 2 * half + n), xq[:, k, t * P:(t + 1) * P],
                                          w[:, k, n * 512:(n + 1) * 512], start=(k == 0), stop=(k == DK - 1))
                mm.then_inc(gu_done, 1)

            def ffn_down(t):
                pe.wait_ge(hz_ready, t + 1)
                if t >= 1:
                    pe.wait_ge(hq_ready, t)
                for k in range(KI):
                    mm = T.transpose(bank(6 + k // 4)[:, (k % 4) * P:(k % 4 + 1) * P], fz[:, k * P:(k + 1) * P], identf[:, :])
                mm.then_inc(hz_turned, 1)
                pe.wait_ge(hq_ready, t + 1)
                if t >= 2:
                    pe.wait_ge(x2_done, t - 1)
                for k in range(KI):
                    mm = T.matmul(bank(t % 2)[:, 0:D], hq[:, k, :], fwd[:, k, :], start=(k == 0), stop=(k == KI - 1))
                mm.then_inc(down_done, 1)

            for h in range(2):
                pe.wait_ge(y_ready, 2 * (h + 1))
                if h == 0:
                    pe.wait_ge(qk_ready, TT)
                else:
                    pe.wait_ge(hp_done, HT)
                for j in range(HT):
                    for k in range(DK):
                        t = h * HT + j
                        mm = T.transpose(bank(4 + j // 2)[:, (j % 2) * D + k * P:(j % 2) * D + (k + 1) * P],
                                         YN[:, k, t * P:(t + 1) * P], identf[:, :])
                    mm.then_inc(y_turned, 1)
                if h == 1:
                    pe.wait_ge(x2_done, HT)
                turn_half(2 + h, 0)
                gate_up(h * HT)
                for t in range(h * HT, (h + 1) * HT):
                    if t + 1 < (h + 1) * HT:
                        gate_up(t + 1)
                    ffn_down(t)

            for h in range(2):
                if h == 0:
                    pe.wait_ge(x2_done, TT)
                else:
                    pe.wait_ge(hL_ready, 2)
                turn_half(4 + h, 0)
                pe.wait_ge(hL_ready, 2 * (h + 1))
                project(2 * HT + HT * h, False)

            def scores(u):
                b, g, jp = u // 16, (u // 2) % GROUPS, u % 2
                if u >= 3:
                    pe.wait_ge(prob_ready, u - 2)
                for mt in range(2):
                    for jj in range(2):
                        r = 32 * (2 * jp + jj)
                        mm = T.matmul(bank(2 * (u % 3) + jj)[:, mt * S:(mt + 1) * S],
                                      KT[r:r + 32, g, b * S + mt * P:b * S + (mt + 1) * P],
                                      QT[r:r + 32, g, b * S:(b + 1) * S], start=True, stop=True)
                mm.then_inc(score_done, 1)

            def weighted_values(n):
                b, g = n // GROUPS, n % GROUPS
                pe.wait_ge(prob_ready, 2 * n + 2)
                if n >= 2:
                    pe.wait_ge(oT_ready, n - 1)
                for mt in range(2):
                    for j in range(4):
                        u = 2 * n + j // 2
                        mm = T.matmul(bank(6 + n % 2)[32 * j:32 * j + HD + 1, 0:S], vaug[:, 2 * b + mt, 4 * g + j, :],
                                      Ex[:, u % NE, j % 2, mt * S:(mt + 1) * S], start=(mt == 0), stop=(mt == 1),
                                      skip_group_check=True)
                mm.then_inc(pv_done, 1)

            def logits(h):
                turn_half(6 + h, 0)
                pe.wait_ge(hL_ready, 4 + 2 * (h + 1))
                for j in range(HT):
                    t = h * HT + j
                    n = 0
                    for k in range(DK):
                        for a in (hH, hL):
                            for w in (gateH, gateL):
                                mm = T.matmul(bank(6)[:, j * P:j * P + E + 1], a[:, k, t * P:(t + 1) * P], w[:, k, :],
                                              start=(n == 0), stop=(n == 4 * DK - 1))
                                n += 1
                mm.then_inc(logit_done, 1)
                pe.wait_ge(W_ready, h + 1)
                for j in range(HT):
                    T.transpose(bank(4).bitcast(F16)[:, j * P:(j + 1) * P], WHL[:, j, :], identh[:, :])
                for j in range(HT):
                    mm = T.transpose(bank(5)[0:2, :].bitcast(F16)[:, j * P:(j + 1) * P], SHL[:, j, :], identh[:, :])
                mm.then_inc(W_turned, 1)

            for h in range(2):
                if h == 0:
                    pe.wait_ge(qk_ready, 2 * TT)
                else:
                    pe.wait_ge(WT_ready, 1)
                LAG = 2
                for u in range(32 * h, 32 * (h + 1) + LAG):
                    if u < 32 * (h + 1):
                        scores(u)
                    v = u - LAG
                    if v >= 32 * h and v % 2 == 1:
                        weighted_values(v // 2)
                pe.wait_ge(oT_ready, 16 * (h + 1))
                for j in range(HT):
                    if j >= 2:
                        pe.wait_ge(x3_done, h * HT + j - 1)
                    for g in range(GROUPS):
                        mm = T.transpose(bank(2 * (j % 2) + g // 4)[:, (g % 4) * P:(g % 4 + 1) * P],
                                         oT[:, j // 2, g, (j % 2) * P:(j % 2 + 1) * P], identf[:, :])
                    mm.then_inc(o_turned, 1)
                pe.wait_ge(x3_done, HT * (h + 1))
                logits(h)

            pe.wait_ge(ld_sel, 16)
            pe.wait_ge(WT_ready, 2)

            def experts_in(c):
                p, h = c // 2, c % 2
                s = p % NW
                if h == 0:
                    pe.wait_ge(mwH_ready, p + 1)
                    pe.wait_ge(mwL_ready, p + 1)
                if c >= 2:
                    pe.wait_ge(inter_ready, c - 1)
                for i in range(2):
                    at = lambda k: slice((i * DK + k) * P, (i * DK + k + 1) * P)
                    mm = three_pass(bank(4 + 2 * h + i), lambda k: mwH[:, s, at(k)], lambda k: mwL[:, s, at(k)],
                                    lambda k: hH[:, k, h * HALF:(h + 1) * HALF],
                                    lambda k: hL[:, k, h * HALF:(h + 1) * HALF])
                mm.then_inc(egu_done, 1)

            def routing_weights(c):
                p, h = c // 2, c % 2
                pe.wait_ge(esilu_done, c + 1)
                if p < PAIRS - 1:
                    mm = T.matmul(bank(4 + 2 * h), sel[:, p * P:(p + 1) * P], WT[:, h * HALF:(h + 1) * HALF], start=True, stop=True)
                else:
                    mm = T.matmul(bank(4 + 2 * h), selS[:, :], ST[0:2, h * HALF:(h + 1) * HALF], start=True, stop=True)
                mm.then_inc(wb_done, 1)

            def experts_out(c):
                p, h = c // 2, c % 2
                s = p % NW
                pe.wait_ge(inL_ready, c + 1)
                for k in range(DK):
                    at = slice(2 * DK * P + k * P, 2 * DK * P + (k + 1) * P)
                    for n, (w, a) in enumerate(((mwH, inH), (mwH, inL), (mwL, inH))):
                        mm = T.matmul(bank(2 * k + h), w[:, s, at], a[:, c % 2, :], start=(p == 0 and n == 0),
                                      stop=(p == PAIRS - 1 and n == 2), skip_group_check=True)
                mm.then_inc(edown_done, 1)

            for c in range(NCH + 2):
                if c < NCH:
                    experts_in(c)
                if 1 <= c <= NCH:
                    routing_weights(c - 1)
                if c >= 2:
                    experts_out(c - 2)
            for k in range(DK):
                pe.wait_ge(acc_read, k + 1)
            for t in range(TT):
                if t >= 4:
                    pe.wait_ge(out_ready, t - 3)
                for k in range(DK):
                    mm = T.transpose(bank(4 + t % 4)[:, k * P:(k + 1) * P], accS[:, k, t * P:(t + 1) * P], identf[:, :])
                mm.then_inc(acc_turned, 1)


def kernel(x, ctx_2048, g_xattn, g_ffn, L0_xattn_w, L0_xattn_u, L0_ffn_w_gate, L0_ffn_w_up, L0_ffn_w_down,
           L1_xattn_Wq, L1_xattn_Wk, L1_xattn_Wv, L1_ffn_gate_w, L1_ffn_gu_w, L1_ffn_dp_w,
           L1_ffn_sh_gate_w, L1_ffn_sh_up_w, L1_ffn_sh_down_w, L1_ffn_sh_gate1_w):
    import concourse.bacc as _bacc
    from concourse.bass_utils import run_bass_kernel_spmd as _run

    A = np.asarray

    def rows(a):
        a = A(a)
        return a.reshape(-1, P, a.shape[-1]).transpose(1, 0, 2)

    x = A(x)
    g_x, g_f = A(g_xattn), A(g_ffn)
    gains = np.broadcast_to(np.stack([g_x[0], g_f[0], g_x[1], g_f[1]]), (P, 4))
    ffn = np.stack([rows(A(w).T).reshape(P, -1) for w in (L0_ffn_w_gate, L0_ffn_w_up, L0_ffn_w_down)], 1)
    kv = np.concatenate([A(L1_xattn_Wk), A(L1_xattn_Wv)], 0)
    proj = np.concatenate([rows(A(L1_xattn_Wq).T), rows(kv[0::2].T), rows(kv[1::2].T)], 2)
    gate = rows(np.concatenate([A(L1_ffn_gate_w), A(L1_ffn_sh_gate1_w)], 0).T)
    shared_gu = np.concatenate([A(L1_ffn_sh_gate_w), A(L1_ffn_sh_up_w)], 0)[None]
    gu = np.concatenate([A(L1_ffn_gu_w), shared_gu, np.zeros_like(shared_gu)], 0)
    gu = gu.reshape(PAIRS, 2, 2, EI, DK, P)
    gu = gu.transpose(5, 0, 2, 4, 1, 3).reshape(P, PAIRS, 2 * DK * P)
    shared_dp = A(L1_ffn_sh_down_w)[None]
    dp = np.concatenate([A(L1_ffn_dp_w), shared_dp, np.zeros_like(shared_dp)], 0)
    dp = dp.reshape(PAIRS, 2, D, EI).transpose(1, 3, 0, 2).reshape(P, PAIRS, D)
    sel = np.zeros((P, (PAIRS - 1) * P), np.float16)
    for r in range(P):
        e = r % E
        sel[r, e * EI:(e + 1) * EI] = SEL_VALUE
    arrays = {
        "x": x.reshape(NT, D),
        "ctxT": rows(A(ctx_2048).reshape(NT, D).T),
        "wkv": np.stack([A(L0_xattn_w).reshape(DK, P).T, A(L0_xattn_u).reshape(DK, P).T], 1),
        "g": gains,
        "ffn": ffn,
        "proj": proj,
        "gate": gate,
        "gu": gu,
        "dp": dp,
        "identf": np.eye(P, dtype=np.float32),
        "identh": np.eye(P, dtype=np.float16),
        "sel": sel,
        "selS": np.full((2, P), SEL_VALUE, np.float16),
    }
    arrays = {f"in_{n}_dram": np.ascontiguousarray(a) for n, a in arrays.items()}
    nc = _bacc.Bacc("TRN2", target_bir_lowering=False, num_devices=1)
    args = [nc.dram_tensor(n, a.shape, mybir.dt.from_np(a.dtype), kind="ExternalInput").ap() for n, a in arrays.items()]
    args.append(nc.dram_tensor("out_0_dram", (NT, D), F32, kind="ExternalOutput").ap())
    bass_flamingo(nc, *args)
    r = _run(nc, [arrays], core_ids=[0])
    return r.results[0]["out_0_dram"].reshape(B, S, D)
```

```python
from contextlib import ExitStack

import numpy as np

import concourse.bass as bass
from concourse import mybir

F32 = mybir.dt.float32
F16 = mybir.dt.float16
BF16 = mybir.dt.bfloat16
ALU = mybir.AluOpType
ACT = mybir.ActivationFunctionType
AX = mybir.AxisListType

P = 128
B, S, D = 4, 256, 256
NT = B * S
TT = NT // P
HT = TT // 2
HALF = NT // 2
DK = D // P
INNER = 1024
KI = INNER // P
HEADS, HD = 32, 8
GROUPS = HEADS // 4
E, EI = 64, 64
PAIRS = E // 2 + 1
TOPK = 8

LN_EPS = 1e-5
Q_EPS = 1e-5
RMS_EPS = 1e-6
MAGIC = 12582912.0
NEG = -1e38
EXP_LN = "natural_log_exp_and_others"
ACT_SCALE = 16.0
W_SCALE = 64.0
UNSCALE = 1.0 / (ACT_SCALE * W_SCALE)
SEL_VALUE = 2.0 ** -6
DOWN_UNSCALE = 1.0 / (ACT_SCALE * W_SCALE * SEL_VALUE * W_SCALE)


def bass_flamingo(nc, x_in, ctxT_in, wkv_in, g_in, ffn_in, proj_in, gate_in, gu_in, dp_in,
                  identf_in, identh_in, sel_in, selS_in, out):
    with ExitStack() as stack:
        def sb(name, shape, dt=F32):
            return stack.enter_context(nc.sbuf_tensor(name, shape, dt))

        def sem(name):
            return stack.enter_context(nc.semaphore(name))

        x = sb("x", [P, TT, D])
        identf = sb("identf", [P, P])
        identh = sb("identh", [P, P], F16)
        wkv = sb("wkv", [P, 2, DK])
        gates = sb("gates", [P, 4])
        tg = sb("tg", [P, 4])
        ntg = sb("ntg", [P, 4])
        magic = sb("magic", [P, 2])
        ones = sb("ones", [P, P])
        xn = sb("xn", [P, 2, HT, D])
        bn = sb("bn", [P, 2, HT, 6])
        mv = sb("mv", [P, 2, HT, 2])
        ve = sb("ve", [P, 2, P])
        lnv = sb("lnv", [P, P])
        root = sb("root", [P, 2, P])
        newt = sb("newt", [P, P])
        rstd = sb("rstd", [P, P])
        hH = sb("hH", [P, DK, NT], F16)
        hL = sb("hL", [P, DK, NT], F16)
        KT = sb("KT", [P, GROUPS, NT], F16)
        vaug = sb("vaug", [P, TT, HEADS, HD + 1])
        ctxT = sb("ctxT", [P, DK, NT])
        ctxH = sb("ctxH", [P, DK, NT], F16)
        ctxL = sb("ctxL", [P, DK, NT], F16)
        proj = sb("proj", [P, DK, 3 * D])
        projH = sb("projH", [P, DK, 3 * D], F16)
        projL = sb("projL", [P, DK, 3 * D], F16)
        gate = sb("gate", [P, DK, E + 1])
        gateH = sb("gateH", [P, DK, E + 1], F16)
        gateL = sb("gateL", [P, DK, E + 1], F16)
        kc = sb("kc", [P, HT, D])
        sq = sb("sq", [P, 2, D])
        ss = sb("ss", [P, HT * HEADS])
        rep = sb("rep", [P, 2, HEADS, 4, HD], F16)
        selS = sb("selS", [2, P], F16)

        regA = sb("regA", [P, 16384])
        regB = sb("regB", [P, 9856])

        def cut(region, start, words):
            return region[:, start:start + words]

        kT = cut(regA, 0, DK * NT).rearrange("p (h t) -> p h t", h=DK)
        fst = [cut(regA, 2048, 2048), cut(regA, 4096, 2048), cut(regB, 6144, 2048)]
        CH = 2 * S
        names = ["A2", "E2", "A", "E", "NO", "EV"]
        wk = {n: cut(regA, 6144 + 1024 * i, 1024).rearrange("p (b n) -> p b n", b=2)
              for i, n in enumerate(names)}
        st = {n: cut(regA, 12288 + 1032 * i, 1028).rearrange("p (b s n) -> p b s n", b=2, s=2)
              for i, n in enumerate(["O", "Pn", "Qn"])}
        QT = cut(regA, 0, 4096).bitcast(F16).rearrange("p (g t) -> p g t", g=GROUPS)
        sel = cut(regA, 4096, 2048).bitcast(F16)
        NW = 4
        PW = 2 * DK * P + D
        mst = cut(regA, 6144, NW * PW).rearrange("p (b n) -> p b n", b=NW)
        mwH = cut(regA, 9216, NW * PW // 2).bitcast(F16).rearrange("p (b n) -> p b n", b=NW)
        mwL = cut(regA, 10752, NW * PW // 2).bitcast(F16).rearrange("p (b n) -> p b n", b=NW)
        sgm = cut(regA, 12288, 1024).rearrange("p (b n) -> p b n", b=2)
        inter = cut(regA, 13312, 1024).rearrange("p (b n) -> p b n", b=2)
        inH = cut(regA, 14336, 512).bitcast(F16).rearrange("p (b n) -> p b n", b=2)
        inL = cut(regA, 14848, 512).bitcast(F16).rearrange("p (b n) -> p b n", b=2)
        WT = cut(regA, 15360, 512).bitcast(F16)
        ST = cut(regA, 15872, 512).bitcast(F16)
        accS = cut(regB, 0, 2048).rearrange("p (h t) -> p h t", h=DK)
        YN = cut(regB, 0, 2048).rearrange("p (h t) -> p h t", h=DK)
        fw = cut(regB, 2048, 3072).bitcast(BF16)
        fwg = fw[:, 0:2048].rearrange("p (k n) -> p k n", k=DK)
        fwu = fw[:, 2048:4096].rearrange("p (k n) -> p k n", k=DK)
        fwd = fw[:, 4096:6144].rearrange("p (k n) -> p k n", k=KI)
        xq = cut(regB, 5120, 1024).bitcast(BF16).rearrange("p (k t) -> p k t", k=DK)
        fsg = cut(regB, 6144, 1024)
        fhp = cut(regB, 7168, 1024)
        fz = cut(regB, 8192, 1024)
        hq = cut(regB, 9216, 512).bitcast(BF16).rearrange("p (k t) -> p k t", k=KI)
        NE = 4
        Ex = cut(regB, 0, NE * 1024).rearrange("p (b j n) -> p b j n", b=NE, j=2)
        oT = cut(regB, 4096, 4096).rearrange("p (b g n) -> p b g n", b=2, g=GROUPS)
        oat = cut(regB, 8192, 256)
        LG = cut(regB, 8448, 320).rearrange("p (t e) -> p t e", t=HT)
        zap = cut(regB, 8768, 256).rearrange("p (t e) -> p t e", t=HT)
        ex = cut(regB, 9024, 256).rearrange("p (t e) -> p t e", t=HT)
        Wf = cut(regB, 9280, 256).rearrange("p (t e) -> p t e", t=HT)
        WHL = cut(regB, 9536, 256).bitcast(F16).rearrange("p (t e) -> p t e", t=HT)
        SHL = cut(regB, 9792, 4).bitcast(F16).rearrange("p (t e) -> p t e", t=HT)

        asum = sb("asum", [P, 4])
        ws = sb("ws", [P, 4])
        rws = sb("rws", [P, 4])
        amax = sb("amax", [P, TT])
        qs = sb("qs", [P, TT])
        rqs = sb("rqs", [P, TT])
        sgs = sb("sgs", [P, TT])
        sus = sb("sus", [P, TT])
        tiny = sb("tiny", [P, 8])
        so = sb("so", [P, TT])
        wdt = sb("wdt", [P, 1])
        mx = sb("mx", [P, HT, TOPK])
        nmx = sb("nmx", [P, HT])
        esum = sb("esum", [P, HT])
        ez = sb("ez", [P, HT])
        sgt = sb("sgt", [P, HT])
        rden = sb("rden", [P, HEADS])
        tgd = sb("tgd", [P, 1])

        ps = stack.enter_context(nc.psum_tensor("ps", [P, 8 * 512], F32))

        def bank(i, n=1):
            return ps[:, 512 * i:512 * (i + n)]

        ld_x = [sem(f"ld_x{i}") for i in range(2)]
        ld_const = sem("ld_const")
        ld_ctx = sem("ld_ctx")
        ld_proj = sem("ld_proj")
        ld_ffn = [sem(f"ld_ffn{i}") for i in range(3)]
        ld_sel = sem("ld_sel")
        ld_pair = [sem(f"ld_pair{i}") for i in range(NW)]
        v_ord = sem("v_ord")
        a_ord = sem("a_ord")
        g_ord = sem("g_ord")
        const_set = sem("const_set")
        tanh_done = sem("tanh_done")
        var_ready = sem("var_ready")
        root_ready = sem("root_ready")
        xn_ready = sem("xn_ready")
        xn_turned = sem("xn_turned")
        kT_ready = sem("kT_ready")
        abs_done = sem("abs_done")
        abs_summed = sem("abs_summed")
        ws_ready = sem("ws_ready")
        fz_ready = sem("fz_ready")
        fclamped = sem("fclamped")
        fw_ready = sem("fw_ready")
        scan_done = sem("scan_done")
        diff_done = sem("diff_done")
        exp_done = sem("exp_done")
        den_ready = sem("den_ready")
        recip_ready = sem("recip_ready")
        y_ready = sem("y_ready")
        y_turned = sem("y_turned")
        x1_done = sem("x1_done")
        qs_ready = sem("qs_ready")
        xz_ready = sem("xz_ready")
        xq_ready = sem("xq_ready")
        gu_done = sem("gu_done")
        silu_done = sem("silu_done")
        hp_done = sem("hp_done")
        hz_ready = sem("hz_ready")
        hz_turned = sem("hz_turned")
        hq_ready = sem("hq_ready")
        down_done = sem("down_done")
        x2_done = sem("x2_done")
        splitH = sem("splitH")
        splitL = sem("splitL")
        proj_done = sem("proj_done")
        sq_ready = sem("sq_ready")
        proj_read = sem("proj_read")
        sq_read = sem("sq_read")
        kn_ready = sem("kn_ready")
        repH = sem("repH")
        repL = sem("repL")
        rep_turned = sem("rep_turned")
        qk_ready = sem("qk_ready")
        hH_ready = sem("hH_ready")
        hL_ready = sem("hL_ready")
        score_done = sem("score_done")
        prob_ready = sem("prob_ready")
        pv_done = sem("pv_done")
        oT_ready = sem("oT_ready")
        o_turned = sem("o_turned")
        x3_done = sem("x3_done")
        logit_done = sem("logit_done")
        LG_ready = sem("LG_ready")
        ex_ready = sem("ex_ready")
        W_ready = sem("W_ready")
        W_turned = sem("W_turned")
        WT_ready = sem("WT_ready")
        mwH_ready = sem("mwH_ready")
        mwL_ready = sem("mwL_ready")
        egu_done = sem("egu_done")
        esilu_done = sem("esilu_done")
        et_done = sem("et_done")
        wb_done = sem("wb_done")
        inter_ready = sem("inter_ready")
        inH_ready = sem("inH_ready")
        inL_ready = sem("inL_ready")
        edown_done = sem("edown_done")
        acc_read = sem("acc_read")
        acc_turned = sem("acc_turned")
        out_ready = sem("out_ready")
        out_done = sem("out_done")

        x_rows = x_in.rearrange("(t p) d -> p t d", p=P)
        out_rows = out.rearrange("(t p) d -> p t d", p=P)

        CHUNKS = [(p, 0) for p in range(NW)] + [(p, 1) for p in range(NW)]
        CHUNKS += [(p, h) for p in range(NW, PAIRS - NW) for h in range(2)]
        CHUNKS += [(p, 0) for p in range(PAIRS - NW, PAIRS)] + [(p, 1) for p in range(PAIRS - NW, PAIRS)]
        NCH = len(CHUNKS)
        LAST_USE = [max(c for c in range(NCH) if CHUNKS[c][0] == p) for p in range(PAIRS)]
        FIRST_DONE = max(c for c in range(NCH) if CHUNKS[c][1] == 0)

        BESIDE = {
            0: [("project", 8), ("stats", 5)], 1: [("norm", 5), ("project", 9)], 2: [("project", 10)],
            3: [("project", 11)], 4: [("rows", 2), ("turn", 5)], 5: [("split", 8), ("split", 9)],
            6: [("turn_rows", 8), ("split", 10)], 7: [("turn_rows", 9), ("split", 11)],
            8: [("turn_rows", 10), ("project", 12)], 9: [("turn_rows", 11), ("project", 13)],
            10: [("project", 14)], 11: [("project", 15)], 12: [("rows", 3)], 13: [("split", 12), ("split", 13)],
            14: [("turn_rows", 12), ("split", 14), ("turn_rows", 13), ("split", 15)],
            15: [("turn_rows", 14), ("turn_rows", 15), ("heads_out", 0)],
            16: [("heads_out", 1)], 17: [("heads_out", 2)], 18: [("heads_out", 3)], 19: [("stats", 6)],
            20: [("norm", 6)], 21: [("turn", 6)], 22: [("logits", 0)], 23: [("weigh", 0)],
            24: [("turn_weights", 0)], 25: [("heads_out", 4)], 26: [("heads_out", 5)],
        }
        BESIDE_EXPERTS = {
            0: [("heads_out", 7), ("stats", 7)], 1: [("norm", 7)], 2: [("turn", 7)], 3: [("logits", 1)],
            4: [("weigh", 1), ("turn_weights", 1)],
        }
        NG = B * GROUPS

        block = stack.enter_context(nc.Block())

        @block.sync
        def _(sp):
            for i in range(2):
                sp.dma_start(x[:, HT * i:HT * (i + 1), :], x_rows[:, HT * i:HT * (i + 1), :]).then_inc(ld_x[i], 16)
                if i == 0:
                    sp.dma_start(identf[:, :], identf_in).then_inc(ld_const, 16)
                    sp.dma_start(wkv[:, :, :], wkv_in).then_inc(ld_const, 16)
                    sp.dma_start(gates[:, :], g_in).then_inc(ld_const, 16)
                    sp.dma_start(identh[:, :], identh_in).then_inc(ld_const, 16)
                    sp.dma_start(selS[:, :], selS_in).then_inc(ld_const, 16)
            for i in range(3):
                sp.dma_start(fst[i], ffn_in[:, i, :]).then_inc(ld_ffn[i], 16)
                if i == 1:
                    sp.dma_start(ctxT[:, :, :], ctxT_in).then_inc(ld_ctx, 16)
            sp.dma_start(proj[:, :, :], proj_in).then_inc(ld_proj, 16)
            sp.dma_start(gate[:, :, :], gate_in).then_inc(ld_proj, 16)
            sp.wait_ge(fw_ready, 3)
            sp.wait_ge(y_ready, 4)
            sp.dma_start(sel[:, :], sel_in).then_inc(ld_sel, 16)
            for p in range(PAIRS):
                if p >= NW:
                    sp.wait_ge(mwH_ready, p - NW + 1)
                    sp.wait_ge(mwL_ready, p - NW + 1)
                sp.dma_start(mst[:, p % NW, 0:2 * DK * P], gu_in[:, p, :]).then_inc(ld_pair[p % NW], 16)
                sp.dma_start(mst[:, p % NW, 2 * DK * P:PW], dp_in[:, p, :]).then_inc(ld_pair[p % NW], 16)
            for h in range(2):
                sp.wait_ge(out_ready, HT * (h + 1))
                sp.dma_start(out_rows[:, HT * h:HT * (h + 1), :], x[:, HT * h:HT * (h + 1), :]).then_inc(out_done, 16)
            sp.wait_ge(out_done, 32)

        @block.gpsimd
        def _(pool):
            def clamp(m):
                pool.wait_ge(fz_ready, m + 1)
                nc.gpsimd.tensor_scalar(fst[m], fst[m], MAGIC + 1.0, MAGIC - 1.0,
                                        ALU.min, ALU.max).then_inc(fclamped, 1)

            def differences(c):
                h, s = c // 2, c % 2
                O = st["O"][:, s]
                k = kT[:, s, h * CH:(h + 1) * CH].rearrange("p (b n) -> p b n", b=2)
                view = {n: wk[n][:, s, :].rearrange("p (b n) -> p b n", b=2) for n in names}
                pool.wait_ge(scan_done, c + 1)
                nc.gpsimd.tensor_tensor(view["A2"], O[:, :, 0:S], O[:, :, 1:S + 1], ALU.subtract).then_inc(diff_done, 1)
                nc.gpsimd.tensor_tensor(view["E2"], k, O[:, :, 1:S + 1], ALU.subtract).then_inc(diff_done, 1)
                nc.gpsimd.tensor_tensor(view["A"], O[:, :, 0:S], view["NO"], ALU.subtract).then_inc(diff_done, 1)
                nc.gpsimd.tensor_tensor(view["E"], k, view["NO"], ALU.subtract).then_inc(diff_done, 1)

            differences(0)
            differences(1)
            clamp(0)
            clamp(1)
            clamp(2)
            differences(2)
            differences(3)

        @block.scalar
        def _(act):
            done = [0]

            def post(ins):
                done[0] += 1
                ins.then_inc(a_ord, 1)

            def settle():
                act.wait_ge(a_ord, done[0])

            event = [0]

            def first_root(n):
                e = event[0]
                event[0] += 1
                act.wait_ge(var_ready, e + 1)
                post(nc.scalar.activation(lnv[:, 0:n], ve[:, e % 2, 0:n], ACT.Ln))
                settle()
                nc.scalar.activation(root[:, e % 2, 0:n], lnv[:, 0:n], ACT.Exp, scale=-0.5).then_inc(root_ready, 1)
                act.wait_ge(root_ready, e + 1)

            def abs_sum(m):
                act.wait_ge(ld_ffn[m], 16)
                nc.scalar.activation(cut(regB, 0, 2048), fst[m], ACT.Abs,
                                     accum_out=asum[:, m:m + 1]).then_inc(abs_done, 1)
                act.wait_ge(abs_done, m + 1)

            def to_integers(m):
                act.wait_ge(ws_ready, 1)
                nc.scalar.activation(fst[m], fst[m], ACT.Identity, bias=magic[:, 0:1],
                                     scale=rws[:, m:m + 1]).then_inc(fz_ready, 1)

            def drop_magic(m):
                act.wait_ge(fclamped, m + 1)
                nc.scalar.activation(fw[:, 2048 * m:2048 * (m + 1)], fst[m], ACT.Identity,
                                     bias=magic[:, 1:2]).then_inc(fw_ready, 1)

            def exponentials(c):
                s = c % 2
                for i, (n, b) in enumerate((("A2", wkv[:, 0, s:s + 1]), ("E2", 0.0), ("A", 0.0), ("E", wkv[:, 1, s:s + 1]))):
                    act.wait_ge(diff_done, 4 * c + i + 1)
                    nc.scalar.activation(wk[n][:, s, :], wk[n][:, s, :], ACT.Exp, bias=b).then_inc(exp_done, 1)

            def reciprocal_guess(c):
                s = c % 2
                act.wait_ge(den_ready, c + 1)
                post(nc.scalar.activation(wk["A"][:, s, :], wk["EV"][:, s, :], ACT.Ln))
                settle()
                nc.scalar.activation(wk["A"][:, s, :], wk["A"][:, s, :], ACT.Exp, scale=-1.0).then_inc(recip_ready, 1)

            def project(n, src):
                stage, j = n // HT, n % HT
                act.wait_ge(proj_done, n + 1)
                if n >= HT:
                    act.wait_ge(repL, HT * stage)
                post(nc.scalar.activation(kc[:, j, :], src[:, 0:D], ACT.Copy, scale=UNSCALE))
                if n >= 2:
                    act.wait_ge(sq_read, n - 1)
                nc.scalar.activation(sq[:, n % 2, :], src[:, 0:D], ACT.Square, scale=UNSCALE).then_inc(sq_ready, 1)
                if stage % 2 == 0:
                    post(nc.scalar.activation(vaug[:, HT * (stage // 2) + j, :, 0:HD],
                                              src[:, D:2 * D].rearrange("p (h d) -> p h d", h=HEADS),
                                              ACT.Copy, scale=UNSCALE))
                settle()
                act.wait_ge(sq_ready, n + 1)
                nc.scalar.nop().then_inc(proj_read, 1)

            def split(n):
                act.wait_ge(kn_ready, n + 1)
                if n >= 2:
                    act.wait_ge(rep_turned, n - 1)
                keys = (n // HT) % 2 == 0
                dst = rep[:, n % 2, :, 0:4:2, :] if keys else rep[:, n % 2, :, 0:2, :]
                src = kc[:, n % HT, :].rearrange("p (h d) -> p h d", h=HEADS).unsqueeze(2).broadcast_to([P, HEADS, 2, HD])
                nc.scalar.copy(dst, src).then_inc(repH, 1)

            def high_halves(q, b0):
                h = q % 2
                act.wait_ge(xn_turned, q + 1)
                for k in range(DK):
                    nc.scalar.copy(hH[:, k, h * HALF:(h + 1) * HALF], bank(b0 + k)).then_inc(hH_ready, 1)

            def ffn_integers(h):
                for j in range(HT):
                    t = h * HT + j
                    act.wait_ge(qs_ready, h + 1)
                    nc.scalar.activation(xn[:, h % 2, j, :], xn[:, h % 2, j, :], ACT.Identity,
                                         bias=magic[:, 0:1], scale=rqs[:, t:t + 1]).then_inc(xz_ready, 1)
                act.wait_ge(xn_turned, 3 + h)
                for k in range(DK):
                    nc.scalar.activation(xq[:, k, h * HALF:(h + 1) * HALF], bank(2 + k), ACT.Identity,
                                         bias=magic[:, 1:2]).then_inc(xq_ready, 1)

            def ffn_silu(t):
                act.wait_ge(gu_done, t + 1)
                if t >= 1:
                    act.wait_ge(hp_done, t)
                nc.scalar.activation(fsg, bank(2, 2), ACT.Silu, scale=sgs[:, t:t + 1]).then_inc(silu_done, 1)

            def ffn_turned(t):
                act.wait_ge(hz_turned, t + 1)
                if t >= 1:
                    act.wait_ge(down_done, t)
                nc.scalar.activation(hq[:, :, :], bank(6, 2).rearrange("p (k t) -> p k t", k=KI), ACT.Identity,
                                     bias=magic[:, 1:2]).then_inc(hq_ready, 1)

            act.wait_ge(ld_const, 80)
            nc.scalar.activation(tg[:, :], gates[:, :], ACT.Tanh).then_inc(tanh_done, 1)
            nc.scalar.preload_act_table_set(EXP_LN)
            first_root(HT)
            first_root(HT)
            act.wait_ge(const_set, 1)
            for h in range(2):
                act.wait_ge(xn_turned, h + 1)
                for k in range(DK):
                    nc.scalar.copy(kT[:, k, h * HALF:(h + 1) * HALF], bank(2 * h + k)).then_inc(kT_ready, 1)
                abs_sum(h)
            abs_sum(2)
            act.wait_ge(ld_ctx, 16)
            nc.scalar.activation(ctxH[:, :, :], ctxT[:, :, :], ACT.Copy, scale=ACT_SCALE).then_inc(splitH, 1)
            act.wait_ge(ld_proj, 32)
            nc.scalar.activation(projH[:, :, :], proj[:, :, :], ACT.Copy, scale=W_SCALE).then_inc(splitH, 1)
            nc.scalar.activation(gateH[:, :, :], gate[:, :, :], ACT.Copy, scale=W_SCALE).then_inc(splitH, 1)
            exponentials(0)
            exponentials(1)
            to_integers(0)
            to_integers(1)
            to_integers(2)
            for n in range(HT):
                project(n, bank(4 + n % 2))
            reciprocal_guess(0)
            reciprocal_guess(1)
            first_root(HT * HEADS)
            drop_magic(0)
            drop_magic(1)
            drop_magic(2)
            first_root(HT)
            for n in range(HT):
                split(n)
            ffn_integers(0)
            exponentials(2)
            exponentials(3)
            nc.scalar.preload_act_table(ACT.Silu)
            ffn_silu(0)
            ffn_silu(1)
            ffn_turned(0)
            ffn_silu(2)
            ffn_turned(1)
            nc.scalar.preload_act_table_set(EXP_LN)
            reciprocal_guess(2)
            reciprocal_guess(3)
            nc.scalar.preload_act_table(ACT.Silu)
            ffn_silu(3)
            ffn_turned(2)
            ffn_turned(3)
            nc.scalar.preload_act_table_set(EXP_LN)
            first_root(HT)
            first_root(HT)
            ffn_integers(1)
            high_halves(4, 4)
            for n in range(HT, 2 * HT):
                project(n, bank(6 + n % 2))
            first_root(HT * HEADS)
            nc.scalar.preload_act_table(ACT.Silu)
            ffn_silu(HT)
            for t in range(HT, 2 * HT):
                split(t)
                if t + 1 < 2 * HT:
                    ffn_silu(t + 1)
                ffn_turned(t)
            nc.scalar.preload_act_table_set(EXP_LN)

            def probabilities(u):
                act.wait_ge(score_done, u + 1)
                if u >= NE:
                    act.wait_ge(pv_done, (u - NE) // 2 + 1)
                nc.scalar.activation(Ex[:, u % NE, :, :], bank(2 * (u % 2), 2).rearrange("p (j n) -> p j n", j=2),
                                     ACT.Exp, scale=float(HD) ** -0.5).then_inc(prob_ready, 1)

            def beside(name, i, b0):
                if name == "project":
                    project(i, bank(6))
                elif name == "rows":
                    first_root(HT * HEADS)
                elif name == "split":
                    split(i)
                elif name == "norm":
                    first_root(HT)
                elif name == "turn":
                    high_halves(i, b0)
                elif name == "weigh":
                    act.wait_ge(LG_ready, i + 1)
                    for j in range(HT):
                        post(nc.scalar.activation(ex[:, j, :], LG[:, j, 0:E], ACT.Exp, bias=nmx[:, j:j + 1]))
                    nc.scalar.activation(ez[:, :], LG[:, :, E], ACT.Exp, scale=-1.0).then_inc(ex_ready, 1)
                elif name == "turn_weights":
                    act.wait_ge(W_turned, i + 1)
                    post(nc.scalar.copy(WT[:, i * HALF:(i + 1) * HALF], bank(b0).bitcast(F16)[:, 0:HALF]))
                    nc.scalar.copy(ST[0:2, i * HALF:(i + 1) * HALF],
                                   bank(b0 + 1)[0:2, :].bitcast(F16)[:, 0:HALF]).then_inc(WT_ready, 1)

            for n in range(NG):
                probabilities(2 * n)
                probabilities(2 * n + 1)
                for name, i in BESIDE.get(n, ()):
                    beside(name, i, 6)

            def weights_high(p):
                act.wait_ge(ld_pair[p % NW], 32 * (p // NW + 1))
                if p >= NW:
                    act.wait_ge(edown_done, LAST_USE[p - NW] + 1)
                nc.scalar.activation(mwH[:, p % NW, :], mst[:, p % NW, :], ACT.Copy, scale=W_SCALE).then_inc(mwH_ready, 1)

            def experts_high(d):
                if d >= 2:
                    act.wait_ge(edown_done, d - 1)
                act.wait_ge(inter_ready, d + 1)
                nc.scalar.copy(inH[:, d % 2, :], inter[:, d % 2, :]).then_inc(inH_ready, 1)

            for p in range(NW):
                weights_high(p)
            nc.scalar.preload_act_table(ACT.Silu)
            fetched = NW
            for c in range(NCH + 1):
                if c < NCH:
                    act.wait_ge(egu_done, c + 1)
                    if c >= 2:
                        act.wait_ge(inter_ready, c - 1)
                    nc.scalar.activation(sgm[:, c % 2, :], bank(4 + 2 * (c % 2)), ACT.Silu, scale=UNSCALE).then_inc(esilu_done, 1)
                if c >= 1:
                    experts_high(c - 1)
                for name, i in BESIDE_EXPERTS.get(c, ()):
                    if name in ("norm", "weigh"):
                        nc.scalar.preload_act_table_set(EXP_LN)
                    beside(name, i, 2)
                    if name in ("norm", "weigh"):
                        nc.scalar.preload_act_table(ACT.Silu)
                if c >= 2 and fetched < PAIRS and LAST_USE[fetched - NW] <= c - 2:
                    weights_high(fetched)
                    fetched += 1
                if c == FIRST_DONE + 2:
                    act.wait_ge(edown_done, FIRST_DONE + 1)
                    for k in range(DK):
                        nc.scalar.copy(accS[:, k, 0:HALF], bank(k)).then_inc(acc_read, 1)
            act.wait_ge(edown_done, NCH)
            for k in range(DK):
                nc.scalar.copy(accS[:, k, HALF:NT], bank(2 + k)).then_inc(acc_read, 1)

        @block.vector
        def _(dve):
            done = [0]

            def post(ins):
                done[0] += 1
                ins.then_inc(v_ord, 1)

            def settle():
                dve.wait_ge(v_ord, done[0])

            def link(ins):
                post(ins)
                settle()

            V = nc.vector
            begun, ended = [0], [0]

            def root_begin(src, n, mul, eps):
                e = begun[0]
                begun[0] += 1
                V.tensor_scalar(ve[:, e % 2, 0:n], src, mul, eps, ALU.mult, ALU.add).then_inc(var_ready, 1)

            def root_end(n, gain):
                e = ended[0]
                ended[0] += 1
                v, r = ve[:, e % 2, 0:n], root[:, e % 2, 0:n]
                dve.wait_ge(var_ready, e + 1)
                dve.wait_ge(root_ready, e + 1)
                link(V.tensor_tensor(newt[:, 0:n], v, r, ALU.mult))
                link(V.tensor_tensor(newt[:, 0:n], newt[:, 0:n], r, ALU.mult))
                link(V.tensor_scalar(newt[:, 0:n], newt[:, 0:n], -0.5 * gain, 1.5 * gain, ALU.mult, ALU.add))
                link(V.tensor_tensor(rstd[:, 0:n], newt[:, 0:n], r, ALU.mult))

            def stats(q):
                h = q % 2
                for j in range(HT):
                    post(V.bn_stats(bn[:, h, j, :], x[:, h * HT + j, :]))
                settle()
                for j in range(HT):
                    post(V.bn_aggr(mv[:, h, j, :], bn[:, h, j, :]))
                settle()
                root_begin(mv[:, h, :, 1], HT, 1.0, LN_EPS)

            def norm(q, gain, publish=True):
                h = q % 2
                root_end(HT, gain)
                if q >= 2:
                    dve.wait_ge(xn_turned, q - 1)
                for j in range(HT):
                    ins = V.tensor_scalar(xn[:, h, j, :], x[:, h * HT + j, :], mv[:, h, j, 0:1], rstd[:, j:j + 1],
                                          ALU.subtract, ALU.mult)
                    if publish:
                        ins.then_inc(xn_ready, 1)
                    else:
                        post(ins)

            def chunk(c):
                h, s = c // 2, c % 2
                two = lambda a: a.rearrange("p (b n) -> p b n", b=2)
                return (h, s, two(kT[:, s, h * CH:(h + 1) * CH]), two(ctxT[:, s, h * CH:(h + 1) * CH]),
                        {n: two(wk[n][:, s, :]) for n in names}, {n: st[n][:, s] for n in st})

            def running_max(c):
                h, s, k, v, W, Z = chunk(c)
                dve.wait_ge(kT_ready, 2 * h + s + 1)
                if c >= 2:
                    dve.wait_ge(exp_done, 4 * (c - 1))
                wb = wkv[:, 0, s:s + 1].broadcast_to([P, S])
                for b in range(2):
                    post(V.tensor_tensor_scan(Z["O"][:, b, 1:S + 1], wb, k[:, b, :], NEG, ALU.add, ALU.max))
                settle()
                V.scalar_tensor_tensor(W["NO"], k, wkv[:, 1, s:s + 1], Z["O"][:, :, 0:S], ALU.add,
                                       ALU.max).then_inc(scan_done, 1)

            def sums(c):
                h, s, k, v, W, Z = chunk(c)
                dve.wait_ge(exp_done, 4 * c + 2)
                post(V.tensor_tensor(W["EV"], W["E2"], v, ALU.mult))
                for b in range(2):
                    post(V.tensor_tensor_scan(Z["Qn"][:, b, 1:S + 1], W["A2"][:, b, :], W["E2"][:, b, :], 0.0, ALU.mult, ALU.add))
                settle()
                for b in range(2):
                    post(V.tensor_tensor_scan(Z["Pn"][:, b, 1:S + 1], W["A2"][:, b, :], W["EV"][:, b, :], 0.0, ALU.mult, ALU.add))
                settle()
                dve.wait_ge(exp_done, 4 * c + 4)
                post(V.tensor_tensor(W["EV"], W["A"], Z["Qn"][:, :, 0:S], ALU.mult))
                post(V.tensor_tensor(W["NO"], W["A"], Z["Pn"][:, :, 0:S], ALU.mult))
                post(V.tensor_tensor(W["A2"], W["E"], v, ALU.mult))
                settle()
                V.tensor_tensor(W["EV"], W["EV"], W["E"], ALU.add).then_inc(den_ready, 1)
                link(V.tensor_tensor(W["NO"], W["NO"], W["A2"], ALU.add))

            def quotient(c):
                h, s, k, v, W, Z = chunk(c)
                dve.wait_ge(recip_ready, c + 1)
                dve.wait_ge(den_ready, c + 1)
                post(V.tensor_tensor(W["EV"], W["EV"], W["A"], ALU.mult))
                post(V.tensor_tensor(W["NO"], W["NO"], W["A"], ALU.mult))
                settle()
                V.scalar_tensor_tensor(YN[:, s, h * CH:(h + 1) * CH], wk["EV"][:, s, :], -2.0, wk["NO"][:, s, :],
                                       ALU.add, ALU.mult).then_inc(y_ready, 1)

            def weight_scales():
                dve.wait_ge(abs_summed, 1)
                link(V.tensor_scalar(ws[:, 0:3], bank(7)[:, 0:3], 1.0 / (INNER * D), Q_EPS, ALU.mult, ALU.add))
                post(V.tensor_scalar(wdt[:, :], ws[:, 2:3], tg[:, 1:2], None, ALU.mult))
                V.reciprocal(rws[:, 0:3], ws[:, 0:3]).then_inc(ws_ready, 1)

            def project(n):
                j = n % HT
                dve.wait_ge(sq_ready, n + 1)
                V.tensor_reduce(ss[:, j * HEADS:(j + 1) * HEADS], sq[:, n % 2, :].rearrange("p (h d) -> p h d", h=HEADS),
                                AX.X, ALU.add).then_inc(sq_read, 1)

            def rows_begin(stage):
                dve.wait_ge(sq_read, HT * (stage + 1))
                root_begin(ss[:, :], HT * HEADS, 1.0 / HD, RMS_EPS)

            def rows_end(stage):
                root_end(HT * HEADS, 1.0)
                dve.wait_ge(proj_read, HT * (stage + 1))
                for j in range(HT):
                    rows = kc[:, j, :].rearrange("p (h d) -> p h d", h=HEADS)
                    V.tensor_tensor(rows, rows, rstd[:, j * HEADS:(j + 1) * HEADS].unsqueeze(2).broadcast_to([P, HEADS, HD]),
                                    ALU.mult).then_inc(kn_ready, 1)
                dve.wait_ge(kn_ready, HT * (stage + 1))

            def split(n):
                keys = (n // HT) % 2 == 0
                dve.wait_ge(repH, n + 1)
                R = rep[:, n % 2]
                rows = kc[:, n % HT, :].rearrange("p (h d) -> p h d", h=HEADS).unsqueeze(2).broadcast_to([P, HEADS, 2, HD])
                hi, lo = (R[:, :, 0:4:2, :], R[:, :, 1:4:2, :]) if keys else (R[:, :, 0:2, :], R[:, :, 2:4, :])
                V.tensor_tensor(lo, rows, hi, ALU.subtract).then_inc(repL, 1)

            def turn_rows(n, src):
                stage = n // HT
                dve.wait_ge(rep_turned, n + 1)
                dst = KT if stage % 2 == 0 else QT
                t = HT * (stage // 2) + n % HT
                V.tensor_copy(dst[:, :, t * P:(t + 1) * P],
                              src.bitcast(F16).rearrange("p (g t) -> p g t", g=GROUPS)).then_inc(qk_ready, 1)

            def low_halves(q, b0):
                h = q % 2
                for k in range(DK):
                    dve.wait_ge(hH_ready, 2 * (q - 4) + k + 1)
                    V.tensor_tensor(hL[:, k, h * HALF:(h + 1) * HALF], bank(b0 + k), hH[:, k, h * HALF:(h + 1) * HALF],
                                    ALU.subtract).then_inc(hL_ready, 1)

            def add_y(h):
                for j in range(HT):
                    t = h * HT + j
                    dve.wait_ge(y_turned, (t | 1) + 1)
                    V.scalar_tensor_tensor(x[:, t, :], bank(j // 2)[:, (j % 2) * D:(j % 2 + 1) * D], ntg[:, 0:1],
                                           x[:, t, :], ALU.mult, ALU.add).then_inc(x1_done, 1)
                dve.wait_ge(x1_done, HT * (h + 1))

            def token_scales(h):
                settle()
                hs = slice(h * HT, (h + 1) * HT)
                link(V.tensor_reduce(amax[:, hs], xn[:, h, :, :], AX.X, ALU.max, apply_absolute_value=True))
                link(V.tensor_scalar(qs[:, hs], amax[:, hs], 1.0 / 127.0, Q_EPS, ALU.mult, ALU.add))
                post(V.tensor_scalar(sus[:, hs], qs[:, hs], ws[:, 1:2], None, ALU.mult))
                post(V.tensor_scalar(sgs[:, hs], qs[:, hs], ws[:, 0:1], None, ALU.mult))
                V.reciprocal(rqs[:, hs], qs[:, hs]).then_inc(qs_ready, 1)
                settle()

            def ffn_inner(t):
                dve.wait_ge(silu_done, t + 1)
                V.tensor_tensor(fhp, bank(4, 2), fsg, ALU.mult).then_inc(hp_done, 1)
                dve.wait_ge(hp_done, t + 1)
                link(V.tensor_reduce(tiny[:, 0:1], fhp, AX.X, ALU.max, apply_absolute_value=True))
                link(V.tensor_scalar(tiny[:, 1:2], tiny[:, 0:1], sus[:, t:t + 1], 1.0 / 127.0, ALU.mult, ALU.mult))
                link(V.tensor_scalar(tiny[:, 2:3], tiny[:, 1:2], Q_EPS, None, ALU.add))
                link(V.reciprocal(tiny[:, 3:4], tiny[:, 2:3]))
                link(V.tensor_tensor(tiny[:, 4:5], tiny[:, 3:4], sus[:, t:t + 1], ALU.mult))
                post(V.tensor_tensor(so[:, t:t + 1], tiny[:, 2:3], wdt[:, :], ALU.mult))
                if t >= 1:
                    dve.wait_ge(hz_turned, t)
                V.tensor_scalar(fz, fhp, tiny[:, 4:5], MAGIC, ALU.mult, ALU.add).then_inc(hz_ready, 1)
                settle()
                dve.wait_ge(hz_ready, t + 1)

            def ffn_residual(t):
                dve.wait_ge(down_done, t + 1)
                V.scalar_tensor_tensor(x[:, t, :], bank(t % 2)[:, 0:D], so[:, t:t + 1], x[:, t, :],
                                       ALU.mult, ALU.add).then_inc(x2_done, 1)

            post(V.memset(magic[:, 0:1], MAGIC))
            post(V.memset(magic[:, 1:2], -MAGIC))
            post(V.memset(ones[:, :], 1.0))
            post(V.memset(vaug[:, :, :, HD:HD + 1], 1.0))
            post(V.memset(st["O"][:, :, :, 0:1], NEG))
            post(V.memset(st["Pn"][:, :, :, 0:1], 0.0))
            post(V.memset(st["Qn"][:, :, :, 0:1], 0.0))
            settle()
            V.memset(tiny[:, :], 0.0).then_inc(const_set, 1)
            dve.wait_ge(ld_x[0], 16)
            stats(0)
            dve.wait_ge(ld_x[1], 16)
            stats(1)
            norm(0, 1.0)
            norm(1, 1.0)
            dve.wait_ge(tanh_done, 1)
            post(V.tensor_scalar(ntg[:, :], tg[:, :], -1.0, None, ALU.mult))
            post(V.tensor_scalar(tgd[:, :], tg[:, 3:4], DOWN_UNSCALE, None, ALU.mult))
            dve.wait_ge(ld_const, 80)
            running_max(0)
            running_max(1)
            weight_scales()
            dve.wait_ge(ld_ctx, 16)
            for i, (lo, hi, src, scale) in enumerate(((ctxL, ctxH, ctxT, ACT_SCALE), (projL, projH, proj, W_SCALE),
                                                      (gateL, gateH, gate, W_SCALE))):
                dve.wait_ge(splitH, i + 1)
                V.scalar_tensor_tensor(lo[:, :, :], src[:, :, :], scale, hi[:, :, :], ALU.mult,
                                       ALU.subtract).then_inc(splitL, 1)
            sums(0)
            sums(1)
            for n in range(HT):
                project(n)
            rows_begin(0)
            quotient(0)
            quotient(1)
            rows_end(0)
            add_y(0)
            stats(2)
            for n in range(HT):
                split(n)
                if n >= 1:
                    turn_rows(n - 1, bank(6 + (n - 1) % 2))
            turn_rows(HT - 1, bank(6 + (HT - 1) % 2))
            norm(2, 1.0, publish=False)
            token_scales(0)
            running_max(2)
            running_max(3)
            ffn_inner(0)
            sums(2)
            ffn_residual(0)
            ffn_inner(1)
            sums(3)
            ffn_residual(1)
            ffn_inner(2)
            quotient(2)
            quotient(3)
            ffn_residual(2)
            ffn_inner(3)
            add_y(1)
            stats(3)
            norm(3, 1.0, publish=False)
            ffn_residual(3)
            dve.wait_ge(x2_done, HT)
            token_scales(1)
            stats(4)
            norm(4, ACT_SCALE)
            low_halves(4, 4)
            for n in range(HT, 2 * HT):
                project(n)
            rows_begin(1)
            ffn_inner(HT)
            rows_end(1)
            for t in range(HT, 2 * HT):
                split(t)
                turn_rows(t, bank(t % 2))
                if t + 1 < 2 * HT:
                    ffn_inner(t + 1)
                ffn_residual(t)
            dve.wait_ge(x2_done, TT)

            def heads_out(t, b0):
                dve.wait_ge(o_turned, t + 1)
                o = bank(b0, 2).rearrange("p (h e) -> p h e", e=32)
                link(V.reciprocal(rden[:, :].unsqueeze(2), o[:, :, HD:HD + 1]))
                link(V.tensor_tensor(oat.rearrange("p (h d) -> p h d", h=HEADS), o[:, :, 0:HD],
                                     rden[:, :].unsqueeze(2).broadcast_to([P, HEADS, HD]), ALU.mult))
                V.scalar_tensor_tensor(x[:, t, :], oat, tg[:, 2:3], x[:, t, :], ALU.mult, ALU.add).then_inc(x3_done, 1)
                dve.wait_ge(x3_done, t + 1)

            def logits(h, src):
                dve.wait_ge(logit_done, h + 1)
                link(V.tensor_scalar(LG[:, :, 0:E + 1], src.rearrange("p (t e) -> p t e", t=HT)[:, :, 0:E + 1], UNSCALE,
                                     None, ALU.mult))
                for j in range(HT):
                    post(V.max(mx[:, j, :], LG[:, j, 0:E]))
                settle()
                V.tensor_scalar(nmx[:, :], mx[:, :, 0], -1.0, None, ALU.mult).then_inc(LG_ready, 1)
                for j in range(HT):
                    post(V.match_replace(zap[:, j, :], mx[:, j, :], LG[:, j, 0:E], 2.0 * NEG))
                settle()

            def weigh(h):
                dve.wait_ge(ex_ready, h + 1)
                for j in range(HT):
                    post(V.scalar_tensor_tensor(Wf[:, j, :], zap[:, j, :], NEG, ex[:, j, :], ALU.is_lt, ALU.mult,
                                                accum_out=esum[:, j:j + 1]))
                link(V.tensor_scalar(ez[:, :], ez[:, :], 1.0, None, ALU.add))
                post(V.reciprocal(esum[:, :], esum[:, :]))
                link(V.reciprocal(sgt[:, :], ez[:, :]))
                link(V.tensor_tensor(Wf[:, :, :], Wf[:, :, :], esum[:, :].unsqueeze(2).broadcast_to([P, HT, E]), ALU.mult))
                if h >= 1:
                    dve.wait_ge(W_turned, h)
                post(V.tensor_copy(WHL[:, :, 0:E], Wf[:, :, :]))
                link(V.tensor_copy(SHL[:, :, 0:1], sgt[:, :].unsqueeze(2)))
                post(V.tensor_tensor(WHL[:, :, E:2 * E], Wf[:, :, :], WHL[:, :, 0:E], ALU.subtract))
                V.tensor_tensor(SHL[:, :, 1:2], sgt[:, :].unsqueeze(2), SHL[:, :, 0:1], ALU.subtract).then_inc(W_ready, 1)

            def beside(name, i, b0):
                if name == "project":
                    project(i)
                elif name == "rows":
                    rows_begin(i)
                    rows_end(i)
                elif name == "split":
                    split(i)
                elif name == "turn_rows":
                    turn_rows(i, bank(7))
                elif name == "stats":
                    stats(i)
                elif name == "norm":
                    norm(i, ACT_SCALE)
                elif name == "turn":
                    low_halves(i, b0)
                elif name == "heads_out":
                    heads_out(i, b0)
                elif name == "logits":
                    logits(i, bank(b0))
                elif name == "weigh":
                    weigh(i)

            def heads_sum(n):
                b, g = n // GROUPS, n % GROUPS
                dve.wait_ge(pv_done, n + 1)
                if b >= 2:
                    dve.wait_ge(o_turned, 2 * (b - 1))
                V.tensor_copy(oT[:, b % 2, g, :], bank(4 + n % 2)[:, 0:S]).then_inc(oT_ready, 1)

            for n in range(NG + 1):
                if n >= 1:
                    heads_sum(n - 1)
                for name, i in BESIDE.get(n, ()):
                    beside(name, i, 6)

            def weights_low(p):
                dve.wait_ge(mwH_ready, p + 1)
                V.scalar_tensor_tensor(mwL[:, p % NW, :], mst[:, p % NW, :], W_SCALE, mwH[:, p % NW, :],
                                       ALU.mult, ALU.subtract).then_inc(mwL_ready, 1)

            for p in range(NW):
                weights_low(p)
                if p == 0:
                    heads_out(6, 2)
            fetched = NW
            for c in range(NCH + 1):
                d = c - 1
                if c >= 1:
                    dve.wait_ge(wb_done, d + 1)
                    dve.wait_ge(et_done, d + 1)
                    if d >= 2:
                        dve.wait_ge(inH_ready, d - 1)
                    V.tensor_tensor(inter[:, d % 2, :], bank(4 + 2 * (d % 2)), sgm[:, d % 2, :], ALU.mult).then_inc(inter_ready, 1)
                if c < NCH:
                    dve.wait_ge(esilu_done, c + 1)
                    V.tensor_tensor(sgm[:, c % 2, :], bank(5 + 2 * (c % 2)), sgm[:, c % 2, :], ALU.mult).then_inc(et_done, 1)
                if c >= 1:
                    dve.wait_ge(inH_ready, d + 1)
                    if d >= 2:
                        dve.wait_ge(edown_done, d - 1)
                    V.tensor_tensor(inL[:, d % 2, :], inter[:, d % 2, :], inH[:, d % 2, :], ALU.subtract).then_inc(inL_ready, 1)
                for name, i in BESIDE_EXPERTS.get(c, ()):
                    beside(name, i, 2)
                if c >= 2 and fetched < PAIRS and LAST_USE[fetched - NW] <= c - 2:
                    weights_low(fetched)
                    fetched += 1
            for t in range(TT):
                dve.wait_ge(acc_turned, t + 1)
                V.scalar_tensor_tensor(x[:, t, :], bank(4 + t % 4)[:, 0:D], tgd[:, 0:1], x[:, t, :],
                                       ALU.mult, ALU.add).then_inc(out_ready, 1)

        @block.tensor
        def _(pe):
            T = nc.tensor

            def turn_half(q, b0):
                for j in range(HT):
                    if q in (2, 3):
                        pe.wait_ge(xz_ready, HT * (q - 2) + j + 1)
                    else:
                        pe.wait_ge(xn_ready, HT * (q if q < 2 else q - 2) + j + 1)
                    for k in range(DK):
                        mm = T.transpose(bank(b0 + k)[:, j * P:(j + 1) * P], xn[:, q % 2, j, k * P:(k + 1) * P], identf[:, :])
                mm.then_inc(xn_turned, 1)

            def three_pass(out_ap, wH, wL, aH, aL):
                n = 0
                for k in range(DK):
                    for w, a in ((wH, aH), (wH, aL), (wL, aH)):
                        mm = T.matmul(out_ap, w(k), a(k), start=(n == 0), stop=(n == 3 * DK - 1))
                        n += 1
                return mm

            def project(n, dst):
                stage = n // HT
                keys = stage % 2 == 0
                t = HT * (stage // 2) + n % HT
                H, L = (ctxH, ctxL) if keys else (hH, hL)
                if keys:
                    pe.wait_ge(splitL, 3)
                else:
                    pe.wait_ge(hL_ready, 2 * (stage // 2 + 1))
                cols = slice(D, 3 * D) if keys else slice(0, D)
                width = 2 * D if keys else D
                three_pass(dst[:, 0:width],
                           lambda k: H[:, k, t * P:(t + 1) * P], lambda k: L[:, k, t * P:(t + 1) * P],
                           lambda k: projH[:, k, cols], lambda k: projL[:, k, cols]).then_inc(proj_done, 1)

            def turn_rows(n, dst):
                pe.wait_ge(repL, n + 1)
                for g in range(GROUPS):
                    mm = T.transpose(dst.bitcast(F16)[:, g * P:(g + 1) * P],
                                     rep[:, n % 2, 4 * g:4 * g + 4, :, :], identh[:, :])
                mm.then_inc(rep_turned, 1)

            def turn_y(h):
                pe.wait_ge(y_ready, 2 * (h + 1))
                for j in range(HT):
                    for k in range(DK):
                        t = h * HT + j
                        mm = T.transpose(bank(j // 2)[:, (j % 2) * D + k * P:(j % 2) * D + (k + 1) * P],
                                         YN[:, k, t * P:(t + 1) * P], identf[:, :])
                    mm.then_inc(y_turned, 1)

            def gate_up(t):
                if t >= 1:
                    pe.wait_ge(silu_done, t)
                    pe.wait_ge(hp_done, t)
                for half, w in ((0, fwg), (1, fwu)):
                    for n in range(2):
                        for k in range(DK):
                            mm = T.matmul(bank(2 + 2 * half + n), xq[:, k, t * P:(t + 1) * P],
                                          w[:, k, n * 512:(n + 1) * 512], start=(k == 0), stop=(k == DK - 1))
                mm.then_inc(gu_done, 1)

            def ffn_down(t):
                pe.wait_ge(hz_ready, t + 1)
                if t >= 1:
                    pe.wait_ge(hq_ready, t)
                for k in range(KI):
                    mm = T.transpose(bank(6 + k // 4)[:, (k % 4) * P:(k % 4 + 1) * P], fz[:, k * P:(k + 1) * P], identf[:, :])
                mm.then_inc(hz_turned, 1)
                pe.wait_ge(hq_ready, t + 1)
                if t >= 2:
                    pe.wait_ge(x2_done, t - 1)
                for k in range(KI):
                    mm = T.matmul(bank(t % 2)[:, 0:D], hq[:, k, :], fwd[:, k, :], start=(k == 0), stop=(k == KI - 1))
                mm.then_inc(down_done, 1)

            pe.wait_ge(ld_const, 80)
            turn_half(0, 0)
            turn_half(1, 2)
            pe.wait_ge(const_set, 1)
            pe.wait_ge(abs_done, 3)
            T.matmul(bank(7)[:, 0:3], ones[:, :], asum[:, 0:3], start=True, stop=True).then_inc(abs_summed, 1)
            for n in range(HT):
                if n >= 2:
                    pe.wait_ge(proj_read, n - 1)
                project(n, bank(4 + n % 2))
            pe.wait_ge(kT_ready, 4)
            turn_y(0)
            pe.wait_ge(ws_ready, 1)
            for n in range(HT):
                if n >= 2:
                    pe.wait_ge(qk_ready, n - 1)
                turn_rows(n, bank(6 + n % 2))
            turn_half(2, 2)
            pe.wait_ge(xq_ready, 2)
            pe.wait_ge(fw_ready, 3)
            pe.wait_ge(proj_read, HT)
            pe.wait_ge(qk_ready, HT)
            pe.wait_ge(x1_done, HT)
            gate_up(0)
            for t in range(HT):
                if t + 1 < HT:
                    gate_up(t + 1)
                ffn_down(t)
                if t == HT - 1 - 1:
                    pe.wait_ge(x2_done, HT - 1)
                    turn_y(1)
                    pe.wait_ge(x1_done, 2 * HT)
            pe.wait_ge(silu_done, HT)
            turn_half(3, 2)
            pe.wait_ge(hp_done, HT)
            turn_half(4, 4)
            pe.wait_ge(hq_ready, HT)
            for n in range(HT, 2 * HT):
                if n >= HT + 2:
                    pe.wait_ge(proj_read, n - 1)
                project(n, bank(6 + n % 2))
            pe.wait_ge(xq_ready, 4)
            pe.wait_ge(x2_done, HT)
            gate_up(HT)
            for t in range(HT, 2 * HT):
                if t >= HT + 2:
                    pe.wait_ge(x2_done, t - 1)
                turn_rows(t, bank(t % 2))
                if t + 1 < 2 * HT:
                    gate_up(t + 1)
                pe.wait_ge(qk_ready, t + 1)
                pe.wait_ge(proj_read, 2 * HT)
                ffn_down(t)

            reader = {6: (hq_ready, TT), 7: (hq_ready, TT), 2: (prob_ready, 2 * NG), 3: (prob_ready, 2 * NG)}

            def take(b, sem_value):
                pe.wait_ge(*reader[b])
                reader[b] = sem_value

            def beside(name, i, b0):
                if name == "project":
                    take(6, (proj_read, i + 1))
                    project(i, bank(6))
                elif name == "turn_rows":
                    take(7, (qk_ready, i + 1))
                    turn_rows(i, bank(7))
                elif name == "turn":
                    for b in (b0, b0 + 1):
                        take(b, (hL_ready, 2 * (i - 3)))
                    turn_half(i, b0)
                elif name == "heads_out":
                    for b in (b0, b0 + 1):
                        take(b, (x3_done, i + 1))
                    pe.wait_ge(oT_ready, GROUPS * (i // 2 + 1))
                    for g in range(GROUPS):
                        mm = T.transpose(bank(b0 + g // 4)[:, (g % 4) * P:(g % 4 + 1) * P],
                                         oT[:, (i // 2) % 2, g, (i % 2) * P:(i % 2 + 1) * P], identf[:, :])
                    mm.then_inc(o_turned, 1)
                elif name == "logits":
                    take(b0, (LG_ready, i + 1))
                    pe.wait_ge(hL_ready, 4 + 2 * (i + 1))
                    for j in range(HT):
                        t = i * HT + j
                        n = 0
                        for k in range(DK):
                            for a in (hH, hL):
                                for w in (gateH, gateL):
                                    mm = T.matmul(bank(b0)[:, j * P:j * P + E + 1], a[:, k, t * P:(t + 1) * P], w[:, k, :],
                                                  start=(n == 0), stop=(n == 4 * DK - 1))
                                    n += 1
                    mm.then_inc(logit_done, 1)
                elif name == "turn_weights":
                    take(b0, (WT_ready, i + 1))
                    take(b0 + 1, (WT_ready, i + 1))
                    pe.wait_ge(W_ready, i + 1)
                    for j in range(HT):
                        T.transpose(bank(b0).bitcast(F16)[:, j * P:(j + 1) * P], WHL[:, j, :], identh[:, :])
                    for j in range(HT):
                        mm = T.transpose(bank(b0 + 1)[0:2, :].bitcast(F16)[:, j * P:(j + 1) * P], SHL[:, j, :], identh[:, :])
                    mm.then_inc(W_turned, 1)

            def scores(u):
                b, g, jp = u // 16, (u // 2) % GROUPS, u % 2
                if u >= 2:
                    pe.wait_ge(prob_ready, u - 1)
                for mt in range(2):
                    for jj in range(2):
                        r = 32 * (2 * jp + jj)
                        mm = T.matmul(bank(2 * (u % 2) + jj)[:, mt * S:(mt + 1) * S],
                                      KT[r:r + 32, g, b * S + mt * P:b * S + (mt + 1) * P],
                                      QT[r:r + 32, g, b * S:(b + 1) * S], start=True, stop=True)
                mm.then_inc(score_done, 1)

            def weighted_values(n):
                b, g = n // GROUPS, n % GROUPS
                pe.wait_ge(prob_ready, 2 * n + 2)
                if n >= 2:
                    pe.wait_ge(oT_ready, n - 1)
                for mt in range(2):
                    for j in range(4):
                        u = 2 * n + j // 2
                        mm = T.matmul(bank(4 + n % 2)[32 * j:32 * j + HD + 1, 0:S], vaug[:, 2 * b + mt, 4 * g + j, :],
                                      Ex[:, u % NE, j % 2, mt * S:(mt + 1) * S], start=(mt == 0), stop=(mt == 1),
                                      skip_group_check=True)
                mm.then_inc(pv_done, 1)

            pe.wait_ge(x2_done, TT)
            for n in range(NG + 1):
                if n == NG // 2:
                    pe.wait_ge(qk_ready, 2 * TT)
                if n < NG:
                    scores(2 * n)
                    scores(2 * n + 1)
                if n >= 1:
                    weighted_values(n - 1)
                for name, i in BESIDE.get(n, ()):
                    beside(name, i, 6)

            def experts_in(c):
                p, h = CHUNKS[c]
                s = p % NW
                pe.wait_ge(mwH_ready, p + 1)
                pe.wait_ge(mwL_ready, p + 1)
                if h == 1:
                    pe.wait_ge(hL_ready, 8)
                if c >= 2:
                    pe.wait_ge(inter_ready, c - 1)
                for i in range(2):
                    at = lambda k: slice((i * DK + k) * P, (i * DK + k + 1) * P)
                    mm = three_pass(bank(4 + 2 * (c % 2) + i), lambda k: mwH[:, s, at(k)], lambda k: mwL[:, s, at(k)],
                                    lambda k: hH[:, k, h * HALF:(h + 1) * HALF],
                                    lambda k: hL[:, k, h * HALF:(h + 1) * HALF])
                mm.then_inc(egu_done, 1)

            def routing_weights(c):
                p, h = CHUNKS[c]
                pe.wait_ge(esilu_done, c + 1)
                if h == 1:
                    pe.wait_ge(WT_ready, 2)
                if p < PAIRS - 1:
                    mm = T.matmul(bank(4 + 2 * (c % 2)), sel[:, p * P:(p + 1) * P], WT[:, h * HALF:(h + 1) * HALF], start=True, stop=True)
                else:
                    mm = T.matmul(bank(4 + 2 * (c % 2)), selS[:, :], ST[0:2, h * HALF:(h + 1) * HALF], start=True, stop=True)
                mm.then_inc(wb_done, 1)

            def experts_out(c):
                p, h = CHUNKS[c]
                s = p % NW
                pe.wait_ge(inL_ready, c + 1)
                for k in range(DK):
                    at = slice(2 * DK * P + k * P, 2 * DK * P + (k + 1) * P)
                    for n, (w, a) in enumerate(((mwH, inH), (mwH, inL), (mwL, inH))):
                        mm = T.matmul(bank(2 * h + k), w[:, s, at], a[:, c % 2, :], start=(p == 0 and n == 0),
                                      stop=(p == PAIRS - 1 and n == 2), skip_group_check=True)
                mm.then_inc(edown_done, 1)

            pe.wait_ge(ld_sel, 16)
            pe.wait_ge(WT_ready, 1)
            pe.wait_ge(oT_ready, NG)
            beside("heads_out", 6, 2)
            for c in range(NCH + 2):
                if c < NCH:
                    experts_in(c)
                if 1 <= c <= NCH:
                    routing_weights(c - 1)
                if c >= 2:
                    experts_out(c - 2)
                for name, i in BESIDE_EXPERTS.get(c, ()):
                    beside(name, i, 2)
            for t in range(TT):
                pe.wait_ge(acc_read, DK * (t // HT + 1))
                pe.wait_ge(inter_ready, NCH)
                if t >= 4:
                    pe.wait_ge(out_ready, t - 3)
                for k in range(DK):
                    mm = T.transpose(bank(4 + t % 4)[:, k * P:(k + 1) * P], accS[:, k, t * P:(t + 1) * P], identf[:, :])
                mm.then_inc(acc_turned, 1)


def kernel(x, ctx_2048, g_xattn, g_ffn, L0_xattn_w, L0_xattn_u, L0_ffn_w_gate, L0_ffn_w_up, L0_ffn_w_down,
           L1_xattn_Wq, L1_xattn_Wk, L1_xattn_Wv, L1_ffn_gate_w, L1_ffn_gu_w, L1_ffn_dp_w,
           L1_ffn_sh_gate_w, L1_ffn_sh_up_w, L1_ffn_sh_down_w, L1_ffn_sh_gate1_w):
    import concourse.bacc as _bacc
    from concourse.bass_utils import run_bass_kernel_spmd as _run

    A = np.asarray

    def rows(a):
        a = A(a)
        return a.reshape(-1, P, a.shape[-1]).transpose(1, 0, 2)

    x = A(x)
    g_x, g_f = A(g_xattn), A(g_ffn)
    gains = np.broadcast_to(np.stack([g_x[0], g_f[0], g_x[1], g_f[1]]), (P, 4))
    ffn = np.stack([rows(A(w).T).reshape(P, -1) for w in (L0_ffn_w_gate, L0_ffn_w_up, L0_ffn_w_down)], 1)
    kv = np.concatenate([A(L1_xattn_Wk), A(L1_xattn_Wv)], 0)
    proj = np.concatenate([rows(A(L1_xattn_Wq).T), rows(kv[0::2].T), rows(kv[1::2].T)], 2)
    gate = rows(np.concatenate([A(L1_ffn_gate_w), A(L1_ffn_sh_gate1_w)], 0).T)
    shared_gu = np.concatenate([A(L1_ffn_sh_gate_w), A(L1_ffn_sh_up_w)], 0)[None]
    gu = np.concatenate([A(L1_ffn_gu_w), shared_gu, np.zeros_like(shared_gu)], 0)
    gu = gu.reshape(PAIRS, 2, 2, EI, DK, P)
    gu = gu.transpose(5, 0, 2, 4, 1, 3).reshape(P, PAIRS, 2 * DK * P)
    shared_dp = A(L1_ffn_sh_down_w)[None]
    dp = np.concatenate([A(L1_ffn_dp_w), shared_dp, np.zeros_like(shared_dp)], 0)
    dp = dp.reshape(PAIRS, 2, D, EI).transpose(1, 3, 0, 2).reshape(P, PAIRS, D)
    sel = np.zeros((P, (PAIRS - 1) * P), np.float16)
    for r in range(P):
        e = r % E
        sel[r, e * EI:(e + 1) * EI] = SEL_VALUE
    arrays = {
        "x": x.reshape(NT, D),
        "ctxT": rows(A(ctx_2048).reshape(NT, D).T),
        "wkv": np.stack([A(L0_xattn_w).reshape(DK, P).T, A(L0_xattn_u).reshape(DK, P).T], 1),
        "g": gains,
        "ffn": ffn,
        "proj": proj,
        "gate": gate,
        "gu": gu,
        "dp": dp,
        "identf": np.eye(P, dtype=np.float32),
        "identh": np.eye(P, dtype=np.float16),
        "sel": sel,
        "selS": np.full((2, P), SEL_VALUE, np.float16),
    }
    arrays = {f"in_{n}_dram": np.ascontiguousarray(a) for n, a in arrays.items()}
    nc = _bacc.Bacc("TRN2", target_bir_lowering=False, num_devices=1)
    args = [nc.dram_tensor(n, a.shape, mybir.dt.from_np(a.dtype), kind="ExternalInput").ap() for n, a in arrays.items()]
    args.append(nc.dram_tensor("out_0_dram", (NT, D), F32, kind="ExternalOutput").ap())
    bass_flamingo(nc, *args)
    r = _run(nc, [arrays], core_ids=[0])
    return r.results[0]["out_0_dram"].reshape(B, S, D)
```

```python
from contextlib import ExitStack

import numpy as np

import concourse.bass as bass
from concourse import mybir

F32 = mybir.dt.float32
F16 = mybir.dt.float16
BF16 = mybir.dt.bfloat16
ALU = mybir.AluOpType
ACT = mybir.ActivationFunctionType
AX = mybir.AxisListType

P = 128
B, S, D = 4, 256, 256
NT = B * S
TT = NT // P
HT = TT // 2
HALF = NT // 2
DK = D // P
INNER = 1024
KI = INNER // P
HEADS, HD = 32, 8
GROUPS = HEADS // 4
E, EI = 64, 64
PAIRS = E // 2 + 1
TOPK = 8

LN_EPS = 1e-5
Q_EPS = 1e-5
RMS_EPS = 1e-6
MAGIC = 12582912.0
NEG = -1e38
EXP_LN = "natural_log_exp_and_others"
ACT_SCALE = 16.0
W_SCALE = 64.0
UNSCALE = 1.0 / (ACT_SCALE * W_SCALE)
ROUTING_SCALE = 2.0 ** -6
DOWN_UNSCALE = 1.0 / (ACT_SCALE * W_SCALE * ROUTING_SCALE * W_SCALE)


def bass_flamingo(nc, x_in, ctxT_in, wkv_in, g_in, ffn_in, proj_in, gate_in, gu_in, dp_in,
                  identf_in, identh_in, routing, out):
    with ExitStack() as stack:
        def sb(name, shape, dt=F32):
            return stack.enter_context(nc.sbuf_tensor(name, shape, dt))

        def sem(name):
            return stack.enter_context(nc.semaphore(name))

        x = sb("x", [P, TT, D])
        identf = sb("identf", [P, P])
        identh = sb("identh", [P, P], F16)
        wkv = sb("wkv", [P, 2, DK])
        gates = sb("gates", [P, 4])
        tg = sb("tg", [P, 4])
        ntg = sb("ntg", [P, 4])
        magic = sb("magic", [P, 2])
        ones = sb("ones", [P, P])
        xn = sb("xn", [P, TT, D])
        bn = sb("bn", [P, TT, 6])
        mv = sb("mv", [P, TT, 2])
        ve = sb("ve", [P, 2, P])
        lnv = sb("lnv", [P, P])
        root = sb("root", [P, 2, P])
        newt = sb("newt", [P, P])
        rstd = sb("rstd", [P, P])
        hH = sb("hH", [P, DK, NT], F16)
        hL = sb("hL", [P, DK, NT], F16)
        KT = sb("KT", [P, GROUPS, NT], F16)
        vaug = sb("vaug", [P, TT, HEADS, HD + 1])
        ctxT = sb("ctxT", [P, DK, NT])
        ctxH = sb("ctxH", [P, DK, NT], F16)
        ctxL = sb("ctxL", [P, DK, NT], F16)
        proj = sb("proj", [P, DK, 3 * D])
        projH = sb("projH", [P, DK, 3 * D], F16)
        projL = sb("projL", [P, DK, 3 * D], F16)
        gate = sb("gate", [P, DK, E + 1])
        gateH = sb("gateH", [P, DK, E + 1], F16)
        gateL = sb("gateL", [P, DK, E + 1], F16)
        kc = sb("kc", [P, HT, D])
        sq = sb("sq", [P, 2, D])
        ss = sb("ss", [P, HT * HEADS])
        rep = sb("rep", [P, 2, HEADS, 4, HD], F16)

        regA = sb("regA", [P, 16384])
        regB = sb("regB", [P, 9856])

        def cut(region, start, words):
            return region[:, start:start + words]

        kT = cut(regA, 0, DK * NT).rearrange("p (h t) -> p h t", h=DK)
        fst = [cut(regA, 2048, 2048), cut(regA, 4096, 2048), cut(regB, 6144, 2048)]
        CH = 2 * S
        names = ["A2", "E2", "A", "E", "NO", "EV"]
        wk = {n: cut(regA, 6144 + 1024 * i, 1024).rearrange("p (b n) -> p b n", b=2)
              for i, n in enumerate(names)}
        st = {n: cut(regA, 12288 + 1032 * i, 1028).rearrange("p (b s n) -> p b s n", b=2, s=2)
              for i, n in enumerate(["O", "Pn", "Qn"])}
        QT = cut(regA, 0, 4096).bitcast(F16).rearrange("p (g t) -> p g t", g=GROUPS)
        NE = 4
        Ex = cut(regA, 6144, NE * 1024).rearrange("p (b j n) -> p b j n", b=NE, j=2)
        NO = 3
        oT = cut(regA, 10240, NO * 2048).rearrange("p (b g n) -> p b g n", b=NO, g=GROUPS)
        sgm = cut(regA, 6144, 1024).rearrange("p (b n) -> p b n", b=2)
        inter = cut(regA, 7168, 1024).rearrange("p (b n) -> p b n", b=2)
        inH = cut(regA, 8192, 512).bitcast(F16).rearrange("p (b n) -> p b n", b=2)
        inL = cut(regA, 8704, 512).bitcast(F16).rearrange("p (b n) -> p b n", b=2)
        NR = 4
        route = cut(regA, 14336, NR * HALF).rearrange("p (b n) -> p b n", b=NR)
        accS = cut(regA, 12288, 2048).rearrange("p (h t) -> p h t", h=DK)
        LG = cut(regB, 0, 320).rearrange("p (t e) -> p t e", t=HT)
        zap = cut(regB, 320, 256).rearrange("p (t e) -> p t e", t=HT)
        ex = cut(regB, 576, 256).rearrange("p (t e) -> p t e", t=HT)
        Wf = cut(regB, 832, HT * (E + 1)).rearrange("p (t e) -> p t e", t=HT)
        oat = cut(regB, 1536, 256)
        NW = 8
        NS = 2
        PW = 2 * DK * P + D
        mwH = cut(regB, 2048, NW * PW // 2).bitcast(F16).rearrange("p (b n) -> p b n", b=NW)
        mwL = cut(regB, 2048 + NW * PW // 2, NW * PW // 2).bitcast(F16).rearrange("p (b n) -> p b n", b=NW)
        WT = cut(regA, 4096, HALF)
        mst = cut(regA, 4096 + HALF, NS * PW).rearrange("p (b n) -> p b n", b=NS)
        YN = cut(regB, 0, 2048).rearrange("p (h t) -> p h t", h=DK)
        fw = cut(regB, 2048, 3072).bitcast(BF16)
        fwg = fw[:, 0:2048].rearrange("p (k n) -> p k n", k=DK)
        fwu = fw[:, 2048:4096].rearrange("p (k n) -> p k n", k=DK)
        fwd = fw[:, 4096:6144].rearrange("p (k n) -> p k n", k=KI)
        xq = cut(regB, 5120, 1024).bitcast(BF16).rearrange("p (k t) -> p k t", k=DK)
        fsg = cut(regB, 6144, 1024)
        fhp = cut(regA, 6144, 2048).rearrange("p (b n) -> p b n", b=2)
        fz = cut(regB, 8192, 1024)
        hq = cut(regB, 7168, 1024).bitcast(BF16).rearrange("p (b k t) -> p b k t", b=2, k=KI)

        asum = sb("asum", [P, 4])
        ws = sb("ws", [P, 4])
        rws = sb("rws", [P, 4])
        amax = sb("amax", [P, TT])
        qs = sb("qs", [P, TT])
        rqs = sb("rqs", [P, TT])
        sgs = sb("sgs", [P, TT])
        sus = sb("sus", [P, TT])
        rhs = sb("rhs", [P, TT])
        tiny = sb("tiny", [P, 8])
        so = sb("so", [P, TT])
        wdt = sb("wdt", [P, 1])
        mx = sb("mx", [P, HT, TOPK])
        nmx = sb("nmx", [P, HT])
        esum = sb("esum", [P, HT])
        ez = sb("ez", [P, HT])
        rden = sb("rden", [P, HEADS])
        tgd = sb("tgd", [P, 1])

        ps = stack.enter_context(nc.psum_tensor("ps", [P, 8 * 512], F32))

        def bank(i, n=1):
            return ps[:, 512 * i:512 * (i + n)]

        ld_x = [sem(f"ld_x{i}") for i in range(2)]
        ld_const = sem("ld_const")
        ld_ctx = sem("ld_ctx")
        ld_proj = sem("ld_proj")
        ld_ffn = [sem(f"ld_ffn{i}") for i in range(3)]
        ld_pair = [sem(f"ld_pair{i}") for i in range(NS)]
        WT_stored = sem("WT_stored")
        ld_route = [sem(f"ld_route{i}") for i in range(NR)]
        v_ord = sem("v_ord")
        a_ord = sem("a_ord")
        g_ord = sem("g_ord")
        const_set = sem("const_set")
        tanh_done = sem("tanh_done")
        var_ready = sem("var_ready")
        root_ready = sem("root_ready")
        xn_ready = sem("xn_ready")
        xn_turned = sem("xn_turned")
        kT_ready = sem("kT_ready")
        abs_done = sem("abs_done")
        abs_summed = sem("abs_summed")
        ws_ready = sem("ws_ready")
        fz_ready = sem("fz_ready")
        fclamped = sem("fclamped")
        fw_ready = sem("fw_ready")
        scan_done = sem("scan_done")
        diff_done = sem("diff_done")
        exp_done = sem("exp_done")
        den_ready = sem("den_ready")
        recip_ready = sem("recip_ready")
        y_ready = sem("y_ready")
        y_turned = sem("y_turned")
        x1_done = sem("x1_done")
        qs_ready = sem("qs_ready")
        xz_ready = sem("xz_ready")
        xq_ready = sem("xq_ready")
        gate_done = sem("gate_done")
        up_done = sem("up_done")
        silu_done = sem("silu_done")
        hp_done = sem("hp_done")
        hscale_ready = sem("hscale_ready")
        hz_ready = sem("hz_ready")
        hz_turned = sem("hz_turned")
        hq_ready = sem("hq_ready")
        down_done = sem("down_done")
        x2_done = sem("x2_done")
        splitH = sem("splitH")
        splitL = sem("splitL")
        proj_done = sem("proj_done")
        sq_ready = sem("sq_ready")
        proj_read = sem("proj_read")
        sq_read = sem("sq_read")
        kn_ready = sem("kn_ready")
        repH = sem("repH")
        repL = sem("repL")
        rep_turned = sem("rep_turned")
        qk_ready = sem("qk_ready")
        hH_ready = sem("hH_ready")
        hL_ready = sem("hL_ready")
        score_done = sem("score_done")
        prob_ready = sem("prob_ready")
        pv_done = sem("pv_done")
        oT_ready = sem("oT_ready")
        o_turned = sem("o_turned")
        x3_done = sem("x3_done")
        logit_done = sem("logit_done")
        LG_ready = sem("LG_ready")
        ex_ready = sem("ex_ready")
        W_ready = sem("W_ready")
        W_turned = sem("W_turned")
        WT_ready = sem("WT_ready")
        mwH_ready = sem("mwH_ready")
        mwL_ready = sem("mwL_ready")
        egu_done = sem("egu_done")
        esilu_done = sem("esilu_done")
        et_done = sem("et_done")
        inter_ready = sem("inter_ready")
        inH_ready = sem("inH_ready")
        inL_ready = sem("inL_ready")
        edown_done = sem("edown_done")
        acc_read = sem("acc_read")
        acc_read_v = sem("acc_read_v")
        acc_turned = sem("acc_turned")
        out_ready = sem("out_ready")
        out_done = sem("out_done")

        x_rows = x_in.rearrange("(t p) d -> p t d", p=P)
        out_rows = out.rearrange("(t p) d -> p t d", p=P)

        CHUNKS = [(p, 0) for p in range(NW)] + [(p, 1) for p in range(NW)]
        CHUNKS += [(p, h) for p in range(NW, PAIRS - NW) for h in range(2)]
        CHUNKS += [(p, 0) for p in range(PAIRS - NW, PAIRS)] + [(p, 1) for p in range(PAIRS - NW, PAIRS)]
        NCH = len(CHUNKS)
        LAST_USE = [max(c for c in range(NCH) if CHUNKS[c][0] == p) for p in range(PAIRS)]
        FETCH_AT = {}
        for c in range(2, NCH + 1):
            p = NW + len(FETCH_AT)
            if p < PAIRS and LAST_USE[p - NW] <= c - 2:
                FETCH_AT[p] = c
        FETCHED = {c: p for p, c in FETCH_AT.items()}
        FIRST_DONE = max(c for c in range(NCH) if CHUNKS[c][1] == 0)

        NORM_TILES = [(0, 4), (4, 8), (0, 4), (4, 8), (0, 4), (4, 6), (6, 8), (0, 4), (4, 8)]
        FORMER = {2: 0, 3: 1, 4: 2, 5: 3, 6: 3, 7: 4, 8: 6}
        FFN_NORMS = (2, 3)
        SPLIT_NORMS = (4, 5, 6, 7, 8)

        def normed_rows(q):
            return sum(b - a for i, (a, b) in enumerate(NORM_TILES[:q]) if i not in FFN_NORMS)

        def halves_before(q):
            return DK * SPLIT_NORMS.index(q)

        VECTOR_ROWS = (8, 9)
        ROW_RUNS = [(0, 4), (4, 8), (8, 10), (10, 12), (12, 14), (14, 16)]

        BESIDE = {
            0: [("project", 10), ("stats", 5)], 1: [("project", 11), ("norm", 5)], 2: [("rows", 3), ("turn", 5)],
            3: [("split", 10), ("split", 11), ("project", 12)], 4: [("turn_rows", 10), ("project", 13)],
            5: [("turn_rows", 11), ("rows", 4)], 6: [("stats", 6), ("split", 12), ("split", 13)],
            7: [("norm", 6), ("turn_rows", 12)], 8: [("turn_rows", 13)], 9: [("turn", 6)], 10: [("project", 14)],
            11: [("project", 15)], 12: [("rows", 5)], 13: [("split", 14), ("split", 15)], 14: [("turn_rows", 14)],
            15: [("turn_rows", 15)], 16: [("heads_out", 0)], 17: [("heads_out", 1)],
            18: [("heads_out", 2)], 19: [("heads_out", 3)], 20: [("stats", 7)], 21: [("norm", 7)],
            22: [("turn", 7)], 23: [("logits", 0)], 24: [("weigh", 0)], 25: [("turn_weights", 0)],
            26: [("weights", 0)], 27: [("weights", 1), ("weights", 2)], 28: [("weights", 3), ("heads_out", 4)],
            29: [("weights", 4), ("heads_out", 5)], 30: [("weights", 5), ("weights", 6)], 31: [("weights", 7)],
        }
        BESIDE_EXPERTS = {
            0: [("heads_out", 6)], 1: [("heads_out", 7), ("stats", 8)], 2: [("norm", 8)], 3: [("turn", 8)],
            4: [("logits", 1)], 5: [("weigh", 1)], 6: [("turn_weights", 1)],
        }
        GATE_BANK = (6, 4)
        OUT_BANK = (0, 1, 4, 5)
        NG = B * GROUPS

        block = stack.enter_context(nc.Block())

        @block.sync
        def _(sp):
            for i in range(2):
                sp.dma_start(x[:, HT * i:HT * (i + 1), :], x_rows[:, HT * i:HT * (i + 1), :]).then_inc(ld_x[i], 16)
                if i == 0:
                    sp.dma_start(identf[:, :], identf_in).then_inc(ld_const, 16)
                    sp.dma_start(wkv[:, :, :], wkv_in).then_inc(ld_const, 16)
                    sp.dma_start(gates[:, :], g_in).then_inc(ld_const, 16)
                    sp.dma_start(identh[:, :], identh_in).then_inc(ld_const, 16)
            for i in range(3):
                sp.dma_start(fst[i], ffn_in[:, i, :]).then_inc(ld_ffn[i], 16)
                if i == 0:
                    sp.dma_start(ctxT[:, :, :], ctxT_in).then_inc(ld_ctx, 16)
            sp.dma_start(proj[:, :, :], proj_in).then_inc(ld_proj, 16)
            sp.dma_start(gate[:, :, :], gate_in).then_inc(ld_proj, 16)
            def load_pair(p):
                if p >= NS:
                    sp.wait_ge(mwH_ready, p - NS + 1)
                    sp.wait_ge(mwL_ready, p - NS + 1)
                sp.dma_start(mst[:, p % NS, 0:2 * DK * P], gu_in[:, p, :]).then_inc(ld_pair[p % NS], 16)
                sp.dma_start(mst[:, p % NS, 2 * DK * P:PW], dp_in[:, p, :]).then_inc(ld_pair[p % NS], 16)

            def store_routing(h):
                sp.wait_ge(WT_ready, h + 1)
                sp.dma_start(routing[:, h * HALF:(h + 1) * HALF], WT[0:E + 1, :]).then_inc(WT_stored, 16)
                sp.wait_ge(WT_stored, 16 * (h + 1))

            sp.wait_ge(x2_done, TT)
            for p in range(NS):
                load_pair(p)
            store_routing(0)
            for p in range(NS, NW + NS):
                load_pair(p)
            for c in range(NCH):
                p, h = CHUNKS[c]
                for q in range(NW + NS, PAIRS):
                    if c == FETCH_AT[q - NS] + 3:
                        load_pair(q)
                if c == NW:
                    store_routing(1)
                if c >= NR:
                    sp.wait_ge(inter_ready, c - NR + 1)
                for i in range(2):
                    row = min(2 * p + i, E)
                    sp.dma_start(route[i * EI:(i + 1) * EI, c % NR, :],
                                 routing[row:row + 1, h * HALF:(h + 1) * HALF].broadcast_to([EI, HALF])
                                 ).then_inc(ld_route[c % NR], 16)
            for h in range(2):
                sp.wait_ge(out_ready, HT * (h + 1))
                sp.dma_start(out_rows[:, HT * h:HT * (h + 1), :], x[:, HT * h:HT * (h + 1), :]).then_inc(out_done, 16)
            sp.wait_ge(out_done, 32)

        @block.gpsimd
        def _(pool):
            def clamp(m):
                pool.wait_ge(fz_ready, m + 1)
                nc.gpsimd.tensor_scalar(fst[m], fst[m], MAGIC + 1.0, MAGIC - 1.0,
                                        ALU.min, ALU.max).then_inc(fclamped, 1)

            def differences(c):
                h, s = c // 2, c % 2
                O = st["O"][:, s]
                k = kT[:, s, h * CH:(h + 1) * CH].rearrange("p (b n) -> p b n", b=2)
                view = {n: wk[n][:, s, :].rearrange("p (b n) -> p b n", b=2) for n in names}
                pool.wait_ge(scan_done, c + 1)
                nc.gpsimd.tensor_tensor(view["A2"], O[:, :, 0:S], O[:, :, 1:S + 1], ALU.subtract).then_inc(diff_done, 1)
                nc.gpsimd.tensor_tensor(view["E2"], k, O[:, :, 1:S + 1], ALU.subtract).then_inc(diff_done, 1)
                nc.gpsimd.tensor_tensor(view["A"], O[:, :, 0:S], view["NO"], ALU.subtract).then_inc(diff_done, 1)
                nc.gpsimd.tensor_tensor(view["E"], k, view["NO"], ALU.subtract).then_inc(diff_done, 1)

            def split(n):
                keys = n < TT
                pool.wait_ge(repH, n + 1)
                R = rep[:, n % 2]
                rows = kc[:, n % HT, :].rearrange("p (h d) -> p h d", h=HEADS).unsqueeze(2).broadcast_to([P, HEADS, 2, HD])
                hi, lo = (R[:, :, 0:4:2, :], R[:, :, 1:4:2, :]) if keys else (R[:, :, 0:2, :], R[:, :, 2:4, :])
                nc.gpsimd.tensor_tensor(lo, rows, hi, ALU.subtract).then_inc(repL, 1)

            for c in range(4):
                differences(c)
            clamp(0)
            clamp(1)
            for n in range(2 * TT):
                if n == HT:
                    clamp(2)
                if n not in VECTOR_ROWS:
                    split(n)

        @block.scalar
        def _(act):
            done = [0]

            def post(ins):
                done[0] += 1
                ins.then_inc(a_ord, 1)

            def settle():
                act.wait_ge(a_ord, done[0])

            event = [0]

            def first_root(n):
                e = event[0]
                event[0] += 1
                act.wait_ge(var_ready, e + 1)
                post(nc.scalar.activation(lnv[:, 0:n], ve[:, e % 2, 0:n], ACT.Ln))
                settle()
                nc.scalar.activation(root[:, e % 2, 0:n], lnv[:, 0:n], ACT.Exp, scale=-0.5).then_inc(root_ready, 1)
                act.wait_ge(root_ready, e + 1)

            def abs_sum(m):
                act.wait_ge(ld_ffn[m], 16)
                nc.scalar.activation(cut(regB, 0, 2048), fst[m], ACT.Abs,
                                     accum_out=asum[:, m:m + 1]).then_inc(abs_done, 1)
                act.wait_ge(abs_done, m + 1)

            def to_integers(m):
                act.wait_ge(ws_ready, 1)
                nc.scalar.activation(fst[m], fst[m], ACT.Identity, bias=magic[:, 0:1],
                                     scale=rws[:, m:m + 1]).then_inc(fz_ready, 1)

            def drop_magic(m):
                act.wait_ge(fclamped, m + 1)
                nc.scalar.activation(fw[:, 2048 * m:2048 * (m + 1)], fst[m], ACT.Identity,
                                     bias=magic[:, 1:2]).then_inc(fw_ready, 1)

            def exponentials(c, which=range(4)):
                s = c % 2
                for i, (n, b) in enumerate((("A2", wkv[:, 0, s:s + 1]), ("E2", 0.0), ("A", 0.0), ("E", wkv[:, 1, s:s + 1]))):
                    if i not in which:
                        continue
                    act.wait_ge(diff_done, 4 * c + i + 1)
                    nc.scalar.activation(wk[n][:, s, :], wk[n][:, s, :], ACT.Exp, bias=b).then_inc(exp_done, 1)

            def reciprocal_guess(c):
                s = c % 2
                act.wait_ge(den_ready, c + 1)
                post(nc.scalar.activation(wk["A"][:, s, :], wk["EV"][:, s, :], ACT.Ln))
                settle()
                nc.scalar.activation(wk["A"][:, s, :], wk["A"][:, s, :], ACT.Exp, scale=-1.0).then_inc(recip_ready, 1)

            def project(n, src):
                j = n % HT
                act.wait_ge(proj_done, n + 1)
                if n >= HT:
                    act.wait_ge(repL, n - HT + 1)
                post(nc.scalar.activation(kc[:, j, :], src[:, 0:D], ACT.Copy, scale=UNSCALE))
                if n >= 2:
                    act.wait_ge(sq_read, n - 1)
                nc.scalar.activation(sq[:, n % 2, :], src[:, 0:D], ACT.Square, scale=UNSCALE).then_inc(sq_ready, 1)
                if n < TT:
                    post(nc.scalar.activation(vaug[:, n, :, 0:HD],
                                              src[:, D:2 * D].rearrange("p (h d) -> p h d", h=HEADS),
                                              ACT.Copy, scale=UNSCALE))
                settle()
                act.wait_ge(sq_ready, n + 1)
                nc.scalar.nop().then_inc(proj_read, 1)

            def split(n):
                act.wait_ge(kn_ready, n + 1)
                if n >= 2:
                    act.wait_ge(rep_turned, n - 1)
                keys = n < TT
                dst = rep[:, n % 2, :, 0:4:2, :] if keys else rep[:, n % 2, :, 0:2, :]
                src = kc[:, n % HT, :].rearrange("p (h d) -> p h d", h=HEADS).unsqueeze(2).broadcast_to([P, HEADS, 2, HD])
                nc.scalar.copy(dst, src).then_inc(repH, 1)

            def high_halves(q, b0):
                a, b = NORM_TILES[q]
                act.wait_ge(xn_turned, q + 1)
                for k in range(DK):
                    nc.scalar.copy(hH[:, k, a * P:b * P], bank(b0 + k)[:, 0:(b - a) * P]).then_inc(hH_ready, 1)

            def tokens_to_integers(h):
                for j in range(HT):
                    t = h * HT + j
                    act.wait_ge(qs_ready, h + 1)
                    nc.scalar.activation(xn[:, t, :], xn[:, t, :], ACT.Identity,
                                         bias=magic[:, 0:1], scale=rqs[:, t:t + 1]).then_inc(xz_ready, 1)

            def turned_integers(h, b0):
                act.wait_ge(xn_turned, FFN_NORMS[h] + 1)
                for k in range(DK):
                    nc.scalar.activation(xq[:, k, h * HALF:(h + 1) * HALF], bank(b0 + k), ACT.Identity,
                                         bias=magic[:, 1:2]).then_inc(xq_ready, 1)

            def ffn_silu(t):
                act.wait_ge(gate_done, t + 1)
                if t >= 1:
                    act.wait_ge(hp_done, t)
                nc.scalar.activation(fsg, bank(2, 2), ACT.Silu, scale=sgs[:, t:t + 1]).then_inc(silu_done, 1)

            def ffn_scale(t):
                act.wait_ge(hscale_ready, t + 1)
                if t >= 1:
                    act.wait_ge(hz_turned, t)
                nc.scalar.activation(fz, fhp[:, t % 2, :], ACT.Identity, bias=magic[:, 0:1],
                                     scale=rhs[:, t:t + 1]).then_inc(hz_ready, 1)

            def ffn_turned(t):
                act.wait_ge(hz_turned, t + 1)
                if t >= 2:
                    act.wait_ge(down_done, t - 1)
                nc.scalar.activation(hq[:, t % 2, :, :], bank(6, 2).rearrange("p (k t) -> p k t", k=KI), ACT.Identity,
                                     bias=magic[:, 1:2]).then_inc(hq_ready, 1)

            act.wait_ge(ld_const, 64)
            nc.scalar.activation(tg[:, :], gates[:, :], ACT.Tanh).then_inc(tanh_done, 1)
            nc.scalar.preload_act_table_set(EXP_LN)
            first_root(HT)
            first_root(HT)
            act.wait_ge(const_set, 1)
            def keys_before_steps(h):
                act.wait_ge(xn_turned, h + 1)
                for k in range(DK):
                    nc.scalar.copy(kT[:, k, h * HALF:(h + 1) * HALF], bank(2 * h + k)).then_inc(kT_ready, 1)

            keys_before_steps(0)
            abs_sum(0)
            keys_before_steps(1)
            exponentials(0, (0, 1))
            act.wait_ge(ld_ctx, 16)
            nc.scalar.activation(ctxH[:, :, :], ctxT[:, :, :], ACT.Copy, scale=ACT_SCALE).then_inc(splitH, 1)
            exponentials(0, (2, 3))
            abs_sum(1)
            exponentials(1)
            abs_sum(2)
            act.wait_ge(ld_proj, 32)
            nc.scalar.activation(projH[:, :, :], proj[:, :, :], ACT.Copy, scale=W_SCALE).then_inc(splitH, 1)
            nc.scalar.activation(gateH[:, :, :], gate[:, :, :], ACT.Copy, scale=W_SCALE).then_inc(splitH, 1)
            reciprocal_guess(0)
            reciprocal_guess(1)
            to_integers(0)
            to_integers(1)
            to_integers(2)
            for n in range(HT):
                project(n, bank(4 + n % 2))
            exponentials(2)
            first_root(HT)
            first_root(HT * HEADS)
            exponentials(3)
            tokens_to_integers(0)
            split(0)
            split(1)
            turned_integers(0, 2)
            drop_magic(0)
            split(2)
            split(3)
            drop_magic(1)
            reciprocal_guess(2)
            project(4, bank(0))
            project(5, bank(1))
            drop_magic(2)
            reciprocal_guess(3)
            project(6, bank(0))
            project(7, bank(1))
            nc.scalar.preload_act_table(ACT.Silu)
            ffn_silu(0)
            ffn_silu(1)
            for t in range(TT):
                ffn_scale(t)
                if t == 1:
                    tokens_to_integers(1)
                    turned_integers(1, 0)
                elif t == TT - 2:
                    nc.scalar.preload_act_table_set(EXP_LN)
                elif t == TT - 1:
                    first_root(2 * HEADS)
                ffn_turned(t)
                if t == 0:
                    nc.scalar.preload_act_table_set(EXP_LN)
                    first_root(HT * HEADS)
                    first_root(HT)
                    nc.scalar.preload_act_table(ACT.Silu)
                elif t == 4:
                    nc.scalar.preload_act_table_set(EXP_LN)
                    first_root(HT)
                    nc.scalar.preload_act_table(ACT.Silu)
                if t + 2 < TT:
                    ffn_silu(t + 2)
                if t == 1:
                    split(4)
                    split(5)
                elif t in (2, 3):
                    split(t + 4)
                elif t == 5:
                    high_halves(4, 0)
                elif t == 6:
                    project(8, bank(0))
                    project(9, bank(1))
            split(8)
            split(9)

            def probabilities(u):
                act.wait_ge(score_done, u + 1)
                if u >= NE:
                    act.wait_ge(pv_done, (u - NE) // 2 + 1)
                nc.scalar.activation(Ex[:, u % NE, :, :], bank(2 * (u % 2), 2).rearrange("p (j n) -> p j n", j=2),
                                     ACT.Exp, scale=float(HD) ** -0.5).then_inc(prob_ready, 1)

            def weights_high(p):
                act.wait_ge(ld_pair[p % NS], 32 * (p // NS + 1))
                if p >= NW:
                    act.wait_ge(edown_done, LAST_USE[p - NW] + 1)
                nc.scalar.activation(mwH[:, p % NW, :], mst[:, p % NS, :], ACT.Copy, scale=W_SCALE).then_inc(mwH_ready, 1)

            def beside(name, i, b0):
                if name == "project":
                    project(i, bank(6))
                elif name == "rows":
                    first_root((ROW_RUNS[i][1] - ROW_RUNS[i][0]) * HEADS)
                elif name == "split":
                    split(i)
                elif name == "norm":
                    first_root(NORM_TILES[i][1] - NORM_TILES[i][0])
                elif name == "weights":
                    weights_high(i)
                elif name == "turn":
                    high_halves(i, b0)
                elif name == "weigh":
                    act.wait_ge(LG_ready, i + 1)
                    for j in range(HT):
                        post(nc.scalar.activation(ex[:, j, :], LG[:, j, 0:E], ACT.Exp, bias=nmx[:, j:j + 1]))
                    nc.scalar.activation(ez[:, :], LG[:, :, E], ACT.Exp, scale=-1.0).then_inc(ex_ready, 1)
                elif name == "turn_weights":
                    act.wait_ge(W_turned, i + 1)
                    if i >= 1:
                        act.wait_ge(WT_stored, 16 * i)
                    nc.scalar.activation(WT[0:E + 1, :], bank(b0)[0:E + 1, :], ACT.Copy,
                                         scale=ROUTING_SCALE).then_inc(WT_ready, 1)

            for n in range(NG):
                probabilities(2 * n)
                probabilities(2 * n + 1)
                for name, i in BESIDE.get(n, ()):
                    beside(name, i, 6)

            def experts_high(d):
                if d >= 2:
                    act.wait_ge(edown_done, d - 1)
                act.wait_ge(inter_ready, d + 1)
                nc.scalar.copy(inH[:, d % 2, :], inter[:, d % 2, :]).then_inc(inH_ready, 1)

            nc.scalar.preload_act_table(ACT.Silu)
            for c in range(NCH + 1):
                if c < NCH:
                    act.wait_ge(egu_done, c + 1)
                    if c >= 2:
                        act.wait_ge(inter_ready, c - 1)
                    nc.scalar.activation(sgm[:, c % 2, :], bank(GATE_BANK[c % 2]), ACT.Silu, scale=UNSCALE).then_inc(esilu_done, 1)
                if c >= 1:
                    experts_high(c - 1)
                for name, i in BESIDE_EXPERTS.get(c, ()):
                    if name in ("norm", "weigh"):
                        nc.scalar.preload_act_table_set(EXP_LN)
                    beside(name, i, 2)
                    if name in ("norm", "weigh"):
                        nc.scalar.preload_act_table(ACT.Silu)
                if c in FETCHED:
                    weights_high(FETCHED[c])
                if c == FIRST_DONE + 2:
                    act.wait_ge(edown_done, FIRST_DONE + 1)
                    for k in range(DK):
                        nc.scalar.copy(accS[:, k, 0:HALF], bank(k)).then_inc(acc_read, 1)
            act.wait_ge(edown_done, NCH)
            nc.scalar.copy(accS[:, 0, HALF:NT], bank(2)).then_inc(acc_read, 1)

        @block.vector
        def _(dve):
            done = [0]

            def post(ins):
                done[0] += 1
                ins.then_inc(v_ord, 1)

            def settle():
                dve.wait_ge(v_ord, done[0])

            def link(ins):
                post(ins)
                settle()

            V = nc.vector
            begun, ended = [0], [0]

            def root_begin(src, n, mul, eps):
                e = begun[0]
                begun[0] += 1
                V.tensor_scalar(ve[:, e % 2, 0:n], src, mul, eps, ALU.mult, ALU.add).then_inc(var_ready, 1)

            def root_end(n, gain):
                e = ended[0]
                ended[0] += 1
                v, r = ve[:, e % 2, 0:n], root[:, e % 2, 0:n]
                dve.wait_ge(var_ready, e + 1)
                dve.wait_ge(root_ready, e + 1)
                link(V.tensor_tensor(newt[:, 0:n], v, r, ALU.mult))
                link(V.tensor_tensor(newt[:, 0:n], newt[:, 0:n], r, ALU.mult))
                link(V.tensor_scalar(newt[:, 0:n], newt[:, 0:n], -0.5 * gain, 1.5 * gain, ALU.mult, ALU.add))
                link(V.tensor_tensor(rstd[:, 0:n], newt[:, 0:n], r, ALU.mult))

            def stats(q):
                a, b = NORM_TILES[q]
                for t in range(a, b):
                    post(V.bn_stats(bn[:, t, :], x[:, t, :]))
                settle()
                for t in range(a, b):
                    post(V.bn_aggr(mv[:, t, :], bn[:, t, :]))
                settle()
                root_begin(mv[:, a:b, 1], b - a, 1.0, LN_EPS)

            def norm(q, gain):
                a, b = NORM_TILES[q]
                root_end(b - a, gain)
                if q in FORMER:
                    dve.wait_ge(xn_turned, FORMER[q] + 1)
                for t in range(a, b):
                    ins = V.tensor_scalar(xn[:, t, :], x[:, t, :], mv[:, t, 0:1], rstd[:, t - a:t - a + 1],
                                          ALU.subtract, ALU.mult)
                    if q in FFN_NORMS:
                        post(ins)
                    else:
                        ins.then_inc(xn_ready, 1)

            def chunk(c):
                h, s = c // 2, c % 2
                two = lambda a: a.rearrange("p (b n) -> p b n", b=2)
                return (h, s, two(kT[:, s, h * CH:(h + 1) * CH]), two(ctxT[:, s, h * CH:(h + 1) * CH]),
                        {n: two(wk[n][:, s, :]) for n in names}, {n: st[n][:, s] for n in st})

            def running_max(c):
                h, s, k, v, W, Z = chunk(c)
                dve.wait_ge(kT_ready, 2 * h + s + 1)
                if c >= 2:
                    dve.wait_ge(exp_done, 4 * (c - 1))
                wb = wkv[:, 0, s:s + 1].broadcast_to([P, S])
                for b in range(2):
                    post(V.tensor_tensor_scan(Z["O"][:, b, 1:S + 1], wb, k[:, b, :], NEG, ALU.add, ALU.max))
                settle()
                V.scalar_tensor_tensor(W["NO"], k, wkv[:, 1, s:s + 1], Z["O"][:, :, 0:S], ALU.add,
                                       ALU.max).then_inc(scan_done, 1)

            def sums(c):
                h, s, k, v, W, Z = chunk(c)
                dve.wait_ge(exp_done, 4 * c + 2)
                post(V.tensor_tensor(W["EV"], W["E2"], v, ALU.mult))
                for b in range(2):
                    post(V.tensor_tensor_scan(Z["Qn"][:, b, 1:S + 1], W["A2"][:, b, :], W["E2"][:, b, :], 0.0, ALU.mult, ALU.add))
                settle()
                for b in range(2):
                    post(V.tensor_tensor_scan(Z["Pn"][:, b, 1:S + 1], W["A2"][:, b, :], W["EV"][:, b, :], 0.0, ALU.mult, ALU.add))
                settle()
                dve.wait_ge(exp_done, 4 * c + 4)
                post(V.tensor_tensor(W["EV"], W["A"], Z["Qn"][:, :, 0:S], ALU.mult))
                post(V.tensor_tensor(W["NO"], W["A"], Z["Pn"][:, :, 0:S], ALU.mult))
                post(V.tensor_tensor(W["A2"], W["E"], v, ALU.mult))
                settle()
                V.tensor_tensor(W["EV"], W["EV"], W["E"], ALU.add).then_inc(den_ready, 1)
                link(V.tensor_tensor(W["NO"], W["NO"], W["A2"], ALU.add))

            def quotient(c):
                h, s, k, v, W, Z = chunk(c)
                dve.wait_ge(recip_ready, c + 1)
                dve.wait_ge(den_ready, c + 1)
                post(V.tensor_tensor(W["EV"], W["EV"], W["A"], ALU.mult))
                post(V.tensor_tensor(W["NO"], W["NO"], W["A"], ALU.mult))
                settle()
                V.scalar_tensor_tensor(YN[:, s, h * CH:(h + 1) * CH], wk["EV"][:, s, :], -2.0, wk["NO"][:, s, :],
                                       ALU.add, ALU.mult).then_inc(y_ready, 1)

            def weight_scales():
                dve.wait_ge(abs_summed, 1)
                link(V.tensor_scalar(ws[:, 0:3], bank(7)[:, 0:3], 1.0 / (INNER * D), Q_EPS, ALU.mult, ALU.add))
                post(V.tensor_scalar(wdt[:, :], ws[:, 2:3], tg[:, 1:2], None, ALU.mult))
                V.reciprocal(rws[:, 0:3], ws[:, 0:3]).then_inc(ws_ready, 1)

            def project(n):
                j = n % HT
                dve.wait_ge(sq_ready, n + 1)
                V.tensor_reduce(ss[:, j * HEADS:(j + 1) * HEADS], sq[:, n % 2, :].rearrange("p (h d) -> p h d", h=HEADS),
                                AX.X, ALU.add).then_inc(sq_read, 1)

            def rows_begin(r):
                a, b = ROW_RUNS[r]
                dve.wait_ge(sq_read, b)
                root_begin(ss[:, (a % HT) * HEADS:(a % HT + b - a) * HEADS], (b - a) * HEADS, 1.0 / HD, RMS_EPS)

            def rows_end(r):
                a, b = ROW_RUNS[r]
                root_end((b - a) * HEADS, 1.0)
                dve.wait_ge(proj_read, b)
                for n in range(a, b):
                    rows = kc[:, n % HT, :].rearrange("p (h d) -> p h d", h=HEADS)
                    root = rstd[:, (n - a) * HEADS:(n - a + 1) * HEADS]
                    V.tensor_tensor(rows, rows, root.unsqueeze(2).broadcast_to([P, HEADS, HD]),
                                    ALU.mult).then_inc(kn_ready, 1)
                dve.wait_ge(kn_ready, b)

            def split(n):
                dve.wait_ge(repH, n + 1)
                rows = kc[:, n % HT, :].rearrange("p (h d) -> p h d", h=HEADS).unsqueeze(2).broadcast_to([P, HEADS, 2, HD])
                V.tensor_tensor(rep[:, n % 2, :, 2:4, :], rows, rep[:, n % 2, :, 0:2, :], ALU.subtract).then_inc(repL, 1)

            def turn_rows(n, src):
                dve.wait_ge(rep_turned, n + 1)
                dst = KT if n < TT else QT
                t = n % TT
                V.tensor_copy(dst[:, :, t * P:(t + 1) * P],
                              src.bitcast(F16).rearrange("p (g t) -> p g t", g=GROUPS)).then_inc(qk_ready, 1)

            def low_halves(q, b0):
                a, b = NORM_TILES[q]
                for k in range(DK):
                    dve.wait_ge(hH_ready, halves_before(q) + k + 1)
                    V.tensor_tensor(hL[:, k, a * P:b * P], bank(b0 + k)[:, 0:(b - a) * P], hH[:, k, a * P:b * P],
                                    ALU.subtract).then_inc(hL_ready, 1)

            def add_y(h):
                for j in range(HT):
                    t = h * HT + j
                    dve.wait_ge(y_turned, (t | 1) + 1)
                    V.scalar_tensor_tensor(x[:, t, :], bank(j // 2)[:, (j % 2) * D:(j % 2 + 1) * D], ntg[:, 0:1],
                                           x[:, t, :], ALU.mult, ALU.add).then_inc(x1_done, 1)
                dve.wait_ge(x1_done, HT * (h + 1))

            def token_scales(h):
                settle()
                hs = slice(h * HT, (h + 1) * HT)
                link(V.tensor_reduce(amax[:, hs], xn[:, hs, :], AX.X, ALU.max, apply_absolute_value=True))
                link(V.tensor_scalar(qs[:, hs], amax[:, hs], 1.0 / 127.0, Q_EPS, ALU.mult, ALU.add))
                post(V.tensor_scalar(sus[:, hs], qs[:, hs], ws[:, 1:2], None, ALU.mult))
                post(V.tensor_scalar(sgs[:, hs], qs[:, hs], ws[:, 0:1], None, ALU.mult))
                V.reciprocal(rqs[:, hs], qs[:, hs]).then_inc(qs_ready, 1)
                settle()

            def ffn_inner(t):
                dve.wait_ge(silu_done, t + 1)
                dve.wait_ge(up_done, t + 1)
                if t >= 2:
                    dve.wait_ge(hz_ready, t - 1)
                V.scalar_tensor_tensor(fhp[:, t % 2, :], bank(4, 2), sus[:, t:t + 1], fsg, ALU.mult, ALU.mult).then_inc(hp_done, 1)
                dve.wait_ge(hp_done, t + 1)
                link(V.tensor_reduce(tiny[:, 0:1], fhp[:, t % 2, :], AX.X, ALU.max, apply_absolute_value=True))
                link(V.tensor_scalar(tiny[:, 1:2], tiny[:, 0:1], 1.0 / 127.0, Q_EPS, ALU.mult, ALU.add))
                V.reciprocal(rhs[:, t:t + 1], tiny[:, 1:2]).then_inc(hscale_ready, 1)
                post(V.tensor_tensor(so[:, t:t + 1], tiny[:, 1:2], wdt[:, :], ALU.mult))
                settle()

            def ffn_residual(t):
                dve.wait_ge(down_done, t + 1)
                V.scalar_tensor_tensor(x[:, t, :], bank(6)[:, 0:D], so[:, t:t + 1], x[:, t, :],
                                       ALU.mult, ALU.add).then_inc(x2_done, 1)

            post(V.memset(magic[:, 0:1], MAGIC))
            post(V.memset(magic[:, 1:2], -MAGIC))
            post(V.memset(ones[:, :], 1.0))
            post(V.memset(vaug[:, :, :, HD:HD + 1], 1.0))
            post(V.memset(st["O"][:, :, :, 0:1], NEG))
            post(V.memset(st["Pn"][:, :, :, 0:1], 0.0))
            post(V.memset(st["Qn"][:, :, :, 0:1], 0.0))
            settle()
            V.memset(tiny[:, :], 0.0).then_inc(const_set, 1)
            dve.wait_ge(ld_x[0], 16)
            stats(0)
            dve.wait_ge(ld_x[1], 16)
            stats(1)
            norm(0, 1.0)
            norm(1, 1.0)
            dve.wait_ge(tanh_done, 1)
            post(V.tensor_scalar(ntg[:, :], tg[:, :], -1.0, None, ALU.mult))
            post(V.tensor_scalar(tgd[:, :], tg[:, 3:4], DOWN_UNSCALE, None, ALU.mult))
            dve.wait_ge(ld_const, 64)
            running_max(0)
            running_max(1)
            def low_part(i, lo, hi, src, scale):
                dve.wait_ge(splitH, i + 1)
                V.scalar_tensor_tensor(lo[:, :, :], src[:, :, :], scale, hi[:, :, :], ALU.mult,
                                       ALU.subtract).then_inc(splitL, 1)

            dve.wait_ge(ld_ctx, 16)
            low_part(0, ctxL, ctxH, ctxT, ACT_SCALE)
            sums(0)
            weight_scales()
            sums(1)
            quotient(0)
            running_max(2)
            quotient(1)
            running_max(3)
            low_part(1, projL, projH, proj, W_SCALE)
            low_part(2, gateL, gateH, gate, W_SCALE)
            add_y(0)
            stats(2)
            for n in range(HT):
                project(n)
            rows_begin(0)
            norm(2, 1.0)
            token_scales(0)
            rows_end(0)
            sums(2)
            turn_rows(0, bank(6))
            turn_rows(1, bank(7))
            sums(3)
            turn_rows(2, bank(6))
            turn_rows(3, bank(7))
            quotient(2)
            project(4)
            project(5)
            quotient(3)
            project(6)
            project(7)
            rows_begin(1)
            ffn_inner(0)
            add_y(1)
            stats(3)
            for t in range(1, TT):
                ffn_inner(t)
                ffn_residual(t - 1)
                if t == 1:
                    rows_end(1)
                    norm(3, 1.0)
                    token_scales(1)
                elif t == 3:
                    turn_rows(4, bank(0))
                    turn_rows(5, bank(1))
                elif t == 4:
                    turn_rows(6, bank(0))
                    dve.wait_ge(x2_done, HT)
                    stats(4)
                elif t == 5:
                    turn_rows(7, bank(1))
                    norm(4, ACT_SCALE)
                elif t == 6:
                    low_halves(4, 0)
            project(8)
            project(9)
            rows_begin(2)
            rows_end(2)
            split(8)
            split(9)
            turn_rows(8, bank(0))
            ffn_residual(TT - 1)
            turn_rows(9, bank(1))
            dve.wait_ge(x2_done, TT)

            def heads_out(t, b0):
                dve.wait_ge(o_turned, t + 1)
                o = bank(b0, 2).rearrange("p (h e) -> p h e", e=32)
                link(V.reciprocal(rden[:, :].unsqueeze(2), o[:, :, HD:HD + 1]))
                link(V.tensor_tensor(oat.rearrange("p (h d) -> p h d", h=HEADS), o[:, :, 0:HD],
                                     rden[:, :].unsqueeze(2).broadcast_to([P, HEADS, HD]), ALU.mult))
                V.scalar_tensor_tensor(x[:, t, :], oat, tg[:, 2:3], x[:, t, :], ALU.mult, ALU.add).then_inc(x3_done, 1)
                dve.wait_ge(x3_done, t + 1)

            def logits(h, src):
                dve.wait_ge(logit_done, h + 1)
                link(V.tensor_scalar(LG[:, :, 0:E + 1], src.rearrange("p (t e) -> p t e", t=HT)[:, :, 0:E + 1], UNSCALE,
                                     None, ALU.mult))
                for j in range(HT):
                    post(V.max(mx[:, j, :], LG[:, j, 0:E]))
                settle()
                V.tensor_scalar(nmx[:, :], mx[:, :, 0], -1.0, None, ALU.mult).then_inc(LG_ready, 1)
                for j in range(HT):
                    post(V.match_replace(zap[:, j, :], mx[:, j, :], LG[:, j, 0:E], 2.0 * NEG))
                settle()

            def weigh(h):
                dve.wait_ge(ex_ready, h + 1)
                if h >= 1:
                    dve.wait_ge(W_turned, h)
                for j in range(HT):
                    post(V.scalar_tensor_tensor(Wf[:, j, 0:E], zap[:, j, :], NEG, ex[:, j, :], ALU.is_lt, ALU.mult,
                                                accum_out=esum[:, j:j + 1]))
                link(V.tensor_scalar(ez[:, :], ez[:, :], 1.0, None, ALU.add))
                link(V.reciprocal(esum[:, :], esum[:, :]))
                post(V.reciprocal(Wf[:, :, E], ez[:, :]))
                V.tensor_tensor(Wf[:, :, 0:E], Wf[:, :, 0:E], esum[:, :].unsqueeze(2).broadcast_to([P, HT, E]),
                                ALU.mult).then_inc(W_ready, 1)
                settle()

            def weights_low(p):
                dve.wait_ge(mwH_ready, p + 1)
                V.scalar_tensor_tensor(mwL[:, p % NW, :], mst[:, p % NS, :], W_SCALE, mwH[:, p % NW, :],
                                       ALU.mult, ALU.subtract).then_inc(mwL_ready, 1)

            def beside(name, i, b0):
                if name == "project":
                    project(i)
                elif name == "rows":
                    rows_begin(i)
                    rows_end(i)
                elif name == "turn_rows":
                    turn_rows(i, bank(7))
                elif name == "stats":
                    stats(i)
                elif name == "norm":
                    norm(i, ACT_SCALE)
                elif name == "turn":
                    low_halves(i, b0)
                elif name == "heads_out":
                    heads_out(i, b0)
                elif name == "logits":
                    logits(i, bank(b0))
                elif name == "weigh":
                    weigh(i)
                elif name == "weights":
                    weights_low(i)

            def heads_sum(n):
                b, g = n // GROUPS, n % GROUPS
                dve.wait_ge(pv_done, n + 1)
                if b >= NO:
                    dve.wait_ge(o_turned, 2 * (b - NO + 1))
                V.tensor_copy(oT[:, b % NO, g, :], bank(4 + n % 2)[:, 0:S]).then_inc(oT_ready, 1)

            for n in range(NG + 1):
                if n >= 1:
                    heads_sum(n - 1)
                for name, i in BESIDE.get(n, ()):
                    beside(name, i, 6)

            def experts_residual(h):
                for t in range(HT * h, HT * (h + 1)):
                    dve.wait_ge(acc_turned, (t | 1) + 1)
                    V.scalar_tensor_tensor(x[:, t, :], bank(OUT_BANK[t // 2])[:, (t % 2) * D:(t % 2 + 1) * D], tgd[:, 0:1],
                                           x[:, t, :], ALU.mult, ALU.add).then_inc(out_ready, 1)

            for c in range(NCH + 1):
                d = c - 1
                if c < NCH:
                    dve.wait_ge(esilu_done, c + 1)
                    V.tensor_tensor(sgm[:, c % 2, :], bank(GATE_BANK[c % 2] + 1), sgm[:, c % 2, :], ALU.mult).then_inc(et_done, 1)
                if c >= 1:
                    dve.wait_ge(inH_ready, d + 1)
                    if d >= 2:
                        dve.wait_ge(edown_done, d - 1)
                    V.tensor_tensor(inL[:, d % 2, :], inter[:, d % 2, :], inH[:, d % 2, :], ALU.subtract).then_inc(inL_ready, 1)
                if c < NCH:
                    dve.wait_ge(et_done, c + 1)
                    dve.wait_ge(ld_route[c % NR], 32 * (c // NR + 1))
                    V.tensor_tensor(inter[:, c % 2, :], route[:, c % NR, :], sgm[:, c % 2, :], ALU.mult).then_inc(inter_ready, 1)
                for name, i in BESIDE_EXPERTS.get(c, ()):
                    beside(name, i, 2)
                if c in FETCHED:
                    weights_low(FETCHED[c])
                if c == FIRST_DONE + 3:
                    experts_residual(0)
            dve.wait_ge(edown_done, NCH)
            V.tensor_copy(accS[:, 1, HALF:NT], bank(3)).then_inc(acc_read_v, 1)
            experts_residual(1)

        @block.tensor
        def _(pe):
            T = nc.tensor

            def turn_norm(q, b0):
                a, b = NORM_TILES[q]
                for t in range(a, b):
                    if q in FFN_NORMS:
                        pe.wait_ge(xz_ready, t + 1)
                    else:
                        pe.wait_ge(xn_ready, normed_rows(q) + t - a + 1)
                    for k in range(DK):
                        mm = T.transpose(bank(b0 + k)[:, (t - a) * P:(t - a + 1) * P], xn[:, t, k * P:(k + 1) * P], identf[:, :])
                mm.then_inc(xn_turned, 1)

            def three_pass(out_ap, wH, wL, aH, aL):
                n = 0
                for k in range(DK):
                    for w, a in ((wH, aH), (wH, aL), (wL, aH)):
                        mm = T.matmul(out_ap, w(k), a(k), start=(n == 0), stop=(n == 3 * DK - 1))
                        n += 1
                return mm

            def project(n, dst):
                keys = n < TT
                t = n % TT
                H, L = (ctxH, ctxL) if keys else (hH, hL)
                if keys:
                    pe.wait_ge(splitL, 3)
                else:
                    q = 4 if t < HT else 5 + (t - HT) // 2
                    pe.wait_ge(hL_ready, halves_before(q) + DK)
                cols = slice(D, 3 * D) if keys else slice(0, D)
                width = 2 * D if keys else D
                three_pass(dst[:, 0:width],
                           lambda k: H[:, k, t * P:(t + 1) * P], lambda k: L[:, k, t * P:(t + 1) * P],
                           lambda k: projH[:, k, cols], lambda k: projL[:, k, cols]).then_inc(proj_done, 1)

            def turn_rows(n, dst):
                pe.wait_ge(repL, n + 1)
                for g in range(GROUPS):
                    mm = T.transpose(dst.bitcast(F16)[:, g * P:(g + 1) * P],
                                     rep[:, n % 2, 4 * g:4 * g + 4, :, :], identh[:, :])
                mm.then_inc(rep_turned, 1)

            def turn_y(h):
                pe.wait_ge(y_ready, 2 * (h + 1))
                for j in range(HT):
                    for k in range(DK):
                        t = h * HT + j
                        mm = T.transpose(bank(j // 2)[:, (j % 2) * D + k * P:(j % 2) * D + (k + 1) * P],
                                         YN[:, k, t * P:(t + 1) * P], identf[:, :])
                    mm.then_inc(y_turned, 1)

            def widen(t, w, b0):
                for n in range(2):
                    for k in range(DK):
                        mm = T.matmul(bank(b0 + n), xq[:, k, t * P:(t + 1) * P],
                                      w[:, k, n * 512:(n + 1) * 512], start=(k == 0), stop=(k == DK - 1))
                return mm

            def gate_product(t):
                if t >= 1:
                    pe.wait_ge(silu_done, t)
                widen(t, fwg, 2).then_inc(gate_done, 1)

            def up_product(t):
                if t >= 1:
                    pe.wait_ge(hp_done, t)
                widen(t, fwu, 4).then_inc(up_done, 1)

            def turn_hidden(t):
                pe.wait_ge(hz_ready, t + 1)
                for k in range(KI):
                    mm = T.transpose(bank(6 + k // 4)[:, (k % 4) * P:(k % 4 + 1) * P], fz[:, k * P:(k + 1) * P], identf[:, :])
                mm.then_inc(hz_turned, 1)

            def narrow(t):
                pe.wait_ge(hq_ready, t + 1)
                for k in range(KI):
                    mm = T.matmul(bank(6)[:, 0:D], hq[:, t % 2, k, :], fwd[:, k, :], start=(k == 0), stop=(k == KI - 1))
                mm.then_inc(down_done, 1)

            pe.wait_ge(ld_const, 64)
            turn_norm(0, 0)
            turn_norm(1, 2)
            pe.wait_ge(const_set, 1)
            pe.wait_ge(abs_done, 3)
            T.matmul(bank(7)[:, 0:3], ones[:, :], asum[:, 0:3], start=True, stop=True).then_inc(abs_summed, 1)
            pe.wait_ge(kT_ready, 4)
            turn_y(0)
            for n in range(HT):
                if n >= 2:
                    pe.wait_ge(proj_read, n - 1)
                project(n, bank(4 + n % 2))
            pe.wait_ge(ws_ready, 1)
            turn_norm(2, 2)
            for n in range(HT):
                if n >= 2:
                    pe.wait_ge(qk_ready, n - 1)
                turn_rows(n, bank(6 + n % 2))
            pe.wait_ge(x1_done, HT)
            project(4, bank(0))
            project(5, bank(1))
            pe.wait_ge(fw_ready, 2)
            pe.wait_ge(xq_ready, 2)
            gate_product(0)
            pe.wait_ge(proj_read, HT)
            up_product(0)
            for n in (6, 7):
                pe.wait_ge(proj_read, n - 1)
                project(n, bank(n % 2))
            pe.wait_ge(proj_read, TT)
            turn_y(1)
            gate_product(1)
            pe.wait_ge(qk_ready, HT)
            pe.wait_ge(fw_ready, 3)
            for t in range(TT):
                if t + 1 < TT:
                    up_product(t + 1)
                if t >= 1:
                    narrow(t - 1)
                if t + 2 < TT:
                    if t + 2 == HT:
                        pe.wait_ge(xq_ready, 4)
                    gate_product(t + 2)
                if t == 1:
                    pe.wait_ge(x1_done, 2 * HT)
                    turn_norm(3, 0)
                elif t == 2:
                    turn_rows(4, bank(0))
                    turn_rows(5, bank(1))
                elif t in (3, 4):
                    pe.wait_ge(qk_ready, t + 2)
                    turn_rows(t + 3, bank((t + 1) % 2))
                if t >= 1:
                    pe.wait_ge(x2_done, t)
                turn_hidden(t)
                if t == 5:
                    pe.wait_ge(qk_ready, TT)
                    turn_norm(4, 0)
                elif t == 6:
                    project(8, bank(0))
                    project(9, bank(1))
            narrow(TT - 1)
            pe.wait_ge(proj_read, 10)
            turn_rows(8, bank(0))
            turn_rows(9, bank(1))

            reader = {6: (x2_done, TT), 7: (hq_ready, TT), 2: (prob_ready, 2 * NG), 3: (prob_ready, 2 * NG)}

            def take(b, sem_value):
                pe.wait_ge(*reader[b])
                reader[b] = sem_value

            def beside(name, i, b0):
                if name == "project":
                    take(6, (proj_read, i + 1))
                    project(i, bank(6))
                elif name == "turn_rows":
                    take(7, (qk_ready, i + 1))
                    turn_rows(i, bank(7))
                elif name == "turn":
                    for b in (b0, b0 + 1):
                        take(b, (hL_ready, halves_before(i) + DK))
                    turn_norm(i, b0)
                elif name == "heads_out":
                    for b in (b0, b0 + 1):
                        take(b, (x3_done, i + 1))
                    pe.wait_ge(oT_ready, GROUPS * (i // 2 + 1))
                    for g in range(GROUPS):
                        mm = T.transpose(bank(b0 + g // 4)[:, (g % 4) * P:(g % 4 + 1) * P],
                                         oT[:, (i // 2) % NO, g, (i % 2) * P:(i % 2 + 1) * P], identf[:, :])
                    mm.then_inc(o_turned, 1)
                elif name == "logits":
                    take(b0, (LG_ready, i + 1))
                    pe.wait_ge(hL_ready, halves_before(7 + i) + DK)
                    for j in range(HT):
                        t = i * HT + j
                        n = 0
                        for k in range(DK):
                            for a in (hH, hL):
                                for w in (gateH, gateL):
                                    mm = T.matmul(bank(b0)[:, j * P:j * P + E + 1], a[:, k, t * P:(t + 1) * P], w[:, k, :],
                                                  start=(n == 0), stop=(n == 4 * DK - 1))
                                    n += 1
                    mm.then_inc(logit_done, 1)
                elif name == "turn_weights":
                    take(b0, (WT_ready, i + 1))
                    pe.wait_ge(W_ready, i + 1)
                    for j in range(HT):
                        mm = T.transpose(bank(b0)[0:E + 1, j * P:(j + 1) * P], Wf[:, j, :], identf[:, :])
                    mm.then_inc(W_turned, 1)

            def scores(u):
                b, g, jp = u // 16, (u // 2) % GROUPS, u % 2
                if u >= 2:
                    pe.wait_ge(prob_ready, u - 1)
                for mt in range(2):
                    for jj in range(2):
                        r = 32 * (2 * jp + jj)
                        mm = T.matmul(bank(2 * (u % 2) + jj)[:, mt * S:(mt + 1) * S],
                                      KT[r:r + 32, g, b * S + mt * P:b * S + (mt + 1) * P],
                                      QT[r:r + 32, g, b * S:(b + 1) * S], start=True, stop=True)
                mm.then_inc(score_done, 1)

            def weighted_values(n):
                b, g = n // GROUPS, n % GROUPS
                pe.wait_ge(prob_ready, 2 * n + 2)
                if n >= 2:
                    pe.wait_ge(oT_ready, n - 1)
                for mt in range(2):
                    for j in range(4):
                        u = 2 * n + j // 2
                        mm = T.matmul(bank(4 + n % 2)[32 * j:32 * j + HD + 1, 0:S], vaug[:, 2 * b + mt, 4 * g + j, :],
                                      Ex[:, u % NE, j % 2, mt * S:(mt + 1) * S], start=(mt == 0), stop=(mt == 1),
                                      skip_group_check=True)
                mm.then_inc(pv_done, 1)

            for n in range(NG + 1):
                if n % GROUPS == 0 and n < NG:
                    pe.wait_ge(qk_ready, TT + 2 * (n // GROUPS + 1))
                if n < NG:
                    scores(2 * n)
                    scores(2 * n + 1)
                if n >= 1:
                    weighted_values(n - 1)
                for name, i in BESIDE.get(n, ()):
                    beside(name, i, 6)

            def experts_in(c):
                p, h = CHUNKS[c]
                s = p % NW
                pe.wait_ge(mwH_ready, p + 1)
                pe.wait_ge(mwL_ready, p + 1)
                if h == 1:
                    pe.wait_ge(hL_ready, halves_before(8) + DK)
                if c >= 2:
                    pe.wait_ge(et_done, c - 1)
                elif c == 1:
                    pe.wait_ge(oT_ready, NG)
                else:
                    pe.wait_ge(x3_done, 6)
                for i in range(2):
                    at = lambda k: slice((i * DK + k) * P, (i * DK + k + 1) * P)
                    mm = three_pass(bank(GATE_BANK[c % 2] + i), lambda k: mwH[:, s, at(k)], lambda k: mwL[:, s, at(k)],
                                    lambda k: hH[:, k, h * HALF:(h + 1) * HALF],
                                    lambda k: hL[:, k, h * HALF:(h + 1) * HALF])
                mm.then_inc(egu_done, 1)

            def experts_out(c):
                p, h = CHUNKS[c]
                s = p % NW
                pe.wait_ge(inL_ready, c + 1)
                for k in range(DK):
                    at = slice(2 * DK * P + k * P, 2 * DK * P + (k + 1) * P)
                    for n, (w, a) in enumerate(((mwH, inH), (mwH, inL), (mwL, inH))):
                        mm = T.matmul(bank(2 * h + k), w[:, s, at], a[:, c % 2, :], start=(p == 0 and n == 0),
                                      stop=(p == PAIRS - 1 and n == 2), skip_group_check=True)
                mm.then_inc(edown_done, 1)

            def turn_sums(h):
                pe.wait_ge(acc_read, DK + h)
                for t in range(HT * h, HT * (h + 1)):
                    for k in range(DK):
                        mm = T.transpose(bank(OUT_BANK[t // 2])[:, (t % 2) * D + k * P:(t % 2) * D + (k + 1) * P],
                                         accS[:, k, t * P:(t + 1) * P], identf[:, :])
                    mm.then_inc(acc_turned, 1)

            for c in range(NCH + 2):
                if c < NCH:
                    experts_in(c)
                if c >= 2:
                    experts_out(c - 2)
                for name, i in BESIDE_EXPERTS.get(c, ()):
                    beside(name, i, 2)
                if c == FIRST_DONE + 3:
                    turn_sums(0)
            pe.wait_ge(acc_read_v, 1)
            turn_sums(1)


def kernel(x, ctx_2048, g_xattn, g_ffn, L0_xattn_w, L0_xattn_u, L0_ffn_w_gate, L0_ffn_w_up, L0_ffn_w_down,
           L1_xattn_Wq, L1_xattn_Wk, L1_xattn_Wv, L1_ffn_gate_w, L1_ffn_gu_w, L1_ffn_dp_w,
           L1_ffn_sh_gate_w, L1_ffn_sh_up_w, L1_ffn_sh_down_w, L1_ffn_sh_gate1_w):
    import concourse.bacc as _bacc
    from concourse.bass_utils import run_bass_kernel_spmd as _run

    A = np.asarray

    def rows(a):
        a = A(a)
        return a.reshape(-1, P, a.shape[-1]).transpose(1, 0, 2)

    x = A(x)
    g_x, g_f = A(g_xattn), A(g_ffn)
    gains = np.broadcast_to(np.stack([g_x[0], g_f[0], g_x[1], g_f[1]]), (P, 4))
    ffn = np.stack([rows(A(w).T).reshape(P, -1) for w in (L0_ffn_w_gate, L0_ffn_w_up, L0_ffn_w_down)], 1)
    kv = np.concatenate([A(L1_xattn_Wk), A(L1_xattn_Wv)], 0)
    proj = np.concatenate([rows(A(L1_xattn_Wq).T), rows(kv[0::2].T), rows(kv[1::2].T)], 2)
    gate = rows(np.concatenate([A(L1_ffn_gate_w), A(L1_ffn_sh_gate1_w)], 0).T)
    shared_gu = np.concatenate([A(L1_ffn_sh_gate_w), A(L1_ffn_sh_up_w)], 0)[None]
    gu = np.concatenate([A(L1_ffn_gu_w), shared_gu, np.zeros_like(shared_gu)], 0)
    gu = gu.reshape(PAIRS, 2, 2, EI, DK, P)
    gu = gu.transpose(5, 0, 2, 4, 1, 3).reshape(P, PAIRS, 2 * DK * P)
    shared_dp = A(L1_ffn_sh_down_w)[None]
    dp = np.concatenate([A(L1_ffn_dp_w), shared_dp, np.zeros_like(shared_dp)], 0)
    dp = dp.reshape(PAIRS, 2, D, EI).transpose(1, 3, 0, 2).reshape(P, PAIRS, D)
    arrays = {
        "x": x.reshape(NT, D),
        "ctxT": rows(A(ctx_2048).reshape(NT, D).T),
        "wkv": np.stack([A(L0_xattn_w).reshape(DK, P).T, A(L0_xattn_u).reshape(DK, P).T], 1),
        "g": gains,
        "ffn": ffn,
        "proj": proj,
        "gate": gate,
        "gu": gu,
        "dp": dp,
        "identf": np.eye(P, dtype=np.float32),
        "identh": np.eye(P, dtype=np.float16),
    }
    arrays = {f"in_{n}_dram": np.ascontiguousarray(a) for n, a in arrays.items()}
    nc = _bacc.Bacc("TRN2", target_bir_lowering=False, num_devices=1)
    args = [nc.dram_tensor(n, a.shape, mybir.dt.from_np(a.dtype), kind="ExternalInput").ap() for n, a in arrays.items()]
    args.append(nc.dram_tensor("routing_dram", (E + 1, NT), F32, kind="Internal").ap())
    args.append(nc.dram_tensor("out_0_dram", (NT, D), F32, kind="ExternalOutput").ap())
    bass_flamingo(nc, *args)
    r = _run(nc, [arrays], core_ids=[0])
    return r.results[0]["out_0_dram"].reshape(B, S, D)
```
